# Optimizing a Trainium2 kernel written in Bass

```python
import numpy as np
import jax
import jax.numpy as jnp

def _softmax(x, axis=-1):
    return jax.nn.softmax(x, axis=axis)

def _gelu(x):
    return jax.nn.gelu(x, approximate=True)

def _silu(x):
    return jax.nn.silu(x)

def _sigmoid(x):
    return jax.nn.sigmoid(x)

def _layernorm(x, axis=-1, eps=1e-05):
    m = jnp.mean(x, axis=axis, keepdims=True)
    v = jnp.var(x, axis=axis, keepdims=True)
    return (x - m) / jnp.sqrt(v + eps)

def _scatter_add(tgt, idx, src, axis=0):
    return tgt.at[idx].add(src)

def _segment_sum(src, seg, n):
    return jax.ops.segment_sum(src, seg, n)
kernel_name = 'mk_sandwich_d2_jaxref_r4_eda5b8'

def setup_inputs(seed: int=0):
    np.random.seed(seed)
    _w = jnp.asarray

    def _L0_attn_setup():
        import jax, jax.numpy as jnp
        import numpy as np
        B, N, D, H, DH = (2, 512, 256, 16, 64)
        key = jax.random.key(seed)
        ks = jax.random.split(key, 5)
        x = jax.random.normal(ks[0], (B, N, D), dtype=jnp.float32)
        Wq = jax.random.normal(ks[1], (D, H * DH), dtype=jnp.float32) * 0.02
        Wk = jax.random.normal(ks[2], (D, H * DH), dtype=jnp.float32) * 0.02
        Wv = jax.random.normal(ks[3], (D, H * DH), dtype=jnp.float32) * 0.02
        Wo = jax.random.normal(ks[4], (H * DH, D), dtype=jnp.float32) * 0.02
        bo = jnp.zeros((D,), dtype=jnp.float32)
        return {'x': x, 'Wq': Wq, 'Wk': Wk, 'Wv': Wv, 'Wo': Wo, 'bo': bo}
    _L0_attn_in = _L0_attn_setup()

    def _L0_ffn_setup():
        import jax, jax.numpy as jnp
        import numpy as np
        R = 64
        key = jax.random.key(seed)
        k1, k2, k3 = jax.random.split(key, 3)
        B, S, D_IN, D_OUT = (8, 1024, 256, 256)
        x = jax.random.normal(k1, (B, S, D_IN), dtype=jnp.float32)
        weight = jax.random.normal(k2, (D_OUT, D_IN), dtype=jnp.float32) * (1.0 / np.sqrt(D_IN))
        disha = jax.random.normal(k3, (R, D_OUT), dtype=jnp.float32) * 0.01
        return {'x': x, 'weight': weight, 'disha': disha}
    _L0_ffn_in = _L0_ffn_setup()

    def _L1_attn_setup():
        import jax, jax.numpy as jnp
        import numpy as np
        C = 256
        H = 16
        K = 2
        B, N = (4, 1024)

        def _heads(t):
            shp = t.shape
            d = shp[-1] // H
            t = t.reshape(shp[:-1] + (H, d))
            return jnp.swapaxes(t, -2, -3)
        key = jax.random.key(seed)
        ks_ = jax.random.split(key, 12)
        s = 1.0 / np.sqrt(C)
        inp = {'x': jax.random.normal(ks_[0], (B, N, C), dtype=jnp.float32), 'Wq': jax.random.normal(ks_[1], (C, C), dtype=jnp.float32) * s, 'bq': jnp.zeros((C,), dtype=jnp.float32), 'Wk': jax.random.normal(ks_[2], (K, C, C), dtype=jnp.float32) * s, 'bk': jnp.zeros((K, C), dtype=jnp.float32), 'Wv': jax.random.normal(ks_[3], (K, C, C), dtype=jnp.float32) * s, 'bv': jnp.zeros((K, C), dtype=jnp.float32), 'Wo': jax.random.normal(ks_[4], (C, C), dtype=jnp.float32) * s, 'bo': jnp.zeros((C,), dtype=jnp.float32), 'ln_g': jnp.ones((C,), dtype=jnp.float32), 'ln_b': jnp.zeros((C,), dtype=jnp.float32)}
        return inp
    _L1_attn_in = _L1_attn_setup()

    def _L1_ffn_setup():
        import jax, jax.numpy as jnp
        import numpy as np
        TOPK = 8
        NUM_EXPERTS = 64
        FFN = 768
        CAPACITY = 160

        def _swiglu(x, w1, w2):
            h = x @ w1.T
            x1, x2 = jnp.split(h, 2, axis=-1)
            return x1 * jax.nn.silu(x2) @ w2.T
        key = jax.random.key(seed)
        ks = jax.random.split(key, 6)
        B, S, H = (1, 128, 256)
        scale = 0.02
        return {'hidden_states': jax.random.normal(ks[0], (B, S, H), jnp.float32), 'wg': jax.random.normal(ks[1], (NUM_EXPERTS, H), jnp.float32) * scale, 'shared_w1': jax.random.normal(ks[2], (2 * FFN, H), jnp.float32) * scale, 'shared_w2': jax.random.normal(ks[3], (H, FFN), jnp.float32) * scale, 'expert_w1': jax.random.normal(ks[4], (NUM_EXPERTS, 2 * FFN, H), jnp.float32) * scale, 'expert_w2': jax.random.normal(ks[5], (NUM_EXPERTS, H, FFN), jnp.float32) * scale}
    _L1_ffn_in = _L1_ffn_setup()
    _d = {'L0_attn_x': _L0_attn_in['x'], 'L0_attn_Wq': _L0_attn_in['Wq'], 'L0_attn_Wk': _L0_attn_in['Wk'], 'L0_attn_Wv': _L0_attn_in['Wv'], 'L0_attn_Wo': _L0_attn_in['Wo'], 'L0_attn_bo': _L0_attn_in['bo'], 'L0_ffn_weight': _L0_ffn_in['weight'], 'L0_ffn_disha': _L0_ffn_in['disha'], 'L1_attn_Wq': _L1_attn_in['Wq'], 'L1_attn_bq': _L1_attn_in['bq'], 'L1_attn_Wk': _L1_attn_in['Wk'], 'L1_attn_bk': _L1_attn_in['bk'], 'L1_attn_Wv': _L1_attn_in['Wv'], 'L1_attn_bv': _L1_attn_in['bv'], 'L1_attn_Wo': _L1_attn_in['Wo'], 'L1_attn_bo': _L1_attn_in['bo'], 'L1_attn_ln_g': _L1_attn_in['ln_g'], 'L1_attn_ln_b': _L1_attn_in['ln_b'], 'L1_ffn_wg': _L1_ffn_in['wg'], 'L1_ffn_shared_w1': _L1_ffn_in['shared_w1'], 'L1_ffn_shared_w2': _L1_ffn_in['shared_w2'], 'L1_ffn_expert_w1': _L1_ffn_in['expert_w1'], 'L1_ffn_expert_w2': _L1_ffn_in['expert_w2']}
    _x0 = _d['L0_attn_x']
    _d['L0_attn_x'] = jax.random.normal(jax.random.fold_in(jax.random.key(seed), 1), (8, 512, 256), dtype=_x0.dtype)
    del _x0
    return _d

def reference(L0_attn_x, L0_attn_Wq, L0_attn_Wk, L0_attn_Wv, L0_attn_Wo, L0_attn_bo, L0_ffn_weight, L0_ffn_disha, L1_attn_Wq, L1_attn_bq, L1_attn_Wk, L1_attn_bk, L1_attn_Wv, L1_attn_bv, L1_attn_Wo, L1_attn_bo, L1_attn_ln_g, L1_attn_ln_b, L1_ffn_wg, L1_ffn_shared_w1, L1_ffn_shared_w2, L1_ffn_expert_w1, L1_ffn_expert_w2):

    def _L0_attn_ref(x, Wq, Wk, Wv, Wo, bo):
        import jax, jax.numpy as jnp
        import numpy as np
        B, N, D, H, DH = (2, 512, 256, 16, 64)
        b, n, _ = x.shape
        scale = DH ** (-0.5)
        q = (x @ Wq).reshape(b, n, H, DH)
        k = (x @ Wk).reshape(b, n, H, DH)
        v = (x @ Wv).reshape(b, n, H, DH)
        base = (2.0 ** 8) ** (1.0 / H)
        slope = 1.0 / base ** jnp.arange(1, H + 1, dtype=jnp.float32)
        pos = jnp.arange(n, dtype=jnp.float32)
        bias = slope[:, None, None] * (pos[:, None] - pos[None, :])
        scores = jnp.einsum('bihd,bjhd->bhij', q, k) * scale + bias[None]
        causal = pos[:, None] >= pos[None, :]
        scores = jnp.where(causal[None, None], scores, jnp.float32(-1e+30))
        attn = jax.nn.softmax(scores, axis=-1)
        out = jnp.einsum('bhij,bjhd->bihd', attn, v).reshape(b, n, H * DH)
        return out @ Wo + bo

    def _L0_ffn_ref(x, weight, disha):
        import jax, jax.numpy as jnp
        import numpy as np
        R = 64
        result = jnp.einsum('bsd,od->bso', x, weight)
        r = disha.shape[0]
        pooled = x.reshape(*x.shape[:-1], x.shape[-1] // r, r).sum(axis=-2)
        return result + pooled @ disha

    def _L1_attn_ref(x, Wq, bq, Wk, bk, Wv, bv, Wo, bo, ln_g, ln_b):
        import jax, jax.numpy as jnp
        import numpy as np
        C = 256
        H = 16
        K = 2
        B, N = (4, 1024)

        def _heads(t):
            shp = t.shape
            d = shp[-1] // H
            t = t.reshape(shp[:-1] + (H, d))
            return jnp.swapaxes(t, -2, -3)
        dtype = x.dtype
        q = x + jnp.einsum('bnc,cd->bnd', x, Wq) + bq
        ks = x[None] + jnp.einsum('bnc,kcd->kbnd', x, Wk) + bk[:, None, None, :]
        vs = x[None] + jnp.einsum('bnc,kcd->kbnd', x, Wv) + bv[:, None, None, :]
        q = _heads(q)
        ks = _heads(ks)
        vs = _heads(vs)
        scale = 1.0 / jnp.sqrt(jnp.asarray(N, dtype=jnp.float32))
        ks = ks.astype(jnp.float32) * scale
        vs = vs.astype(jnp.float32) * scale
        states = jnp.einsum('kbhnd,kbhne->kbhde', ks, vs)
        state = jnp.prod(states, axis=0)
        out = jnp.einsum('bhnd,bhde->bhne', q.astype(jnp.float32), state)
        out = out.astype(dtype)
        out = jnp.swapaxes(out, 1, 2).reshape(x.shape[0], x.shape[1], C)
        mu = jnp.mean(out, axis=-1, keepdims=True)
        var = jnp.var(out, axis=-1, keepdims=True)
        out = (out - mu) / jnp.sqrt(var + 1e-05) * ln_g + ln_b
        out = jnp.einsum('bnc,cd->bnd', out, Wo) + bo
        return out

    def _L1_ffn_ref(hidden_states, wg, shared_w1, shared_w2, expert_w1, expert_w2):
        import jax, jax.numpy as jnp
        import numpy as np
        TOPK = 8
        NUM_EXPERTS = 64
        FFN = 768
        CAPACITY = 160

        def _swiglu(x, w1, w2):
            h = x @ w1.T
            x1, x2 = jnp.split(h, 2, axis=-1)
            return x1 * jax.nn.silu(x2) @ w2.T
        B, S, H = hidden_states.shape
        T = B * S
        x = hidden_states.reshape(T, H)
        shared_out = _swiglu(x, shared_w1, shared_w2)
        logits = x.astype(jnp.float32) @ wg.T
        gates = jax.nn.softmax(logits, axis=-1)
        w_topk, idx_topk = jax.lax.top_k(gates, TOPK)
        denom = jnp.maximum(w_topk.sum(-1, keepdims=True), jnp.finfo(jnp.float32).eps)
        w_topk = w_topk / denom
        A = T * TOPK
        flat_e = idx_topk.reshape(A)
        flat_w = w_topk.reshape(A)
        flat_t = jnp.repeat(jnp.arange(T), TOPK)
        order = jnp.argsort(flat_e)
        se, st, sw = (flat_e[order], flat_t[order], flat_w[order])
        counts = jnp.zeros(NUM_EXPERTS, jnp.int32).at[flat_e].add(1)
        starts = jnp.cumsum(counts) - counts
        rank = jnp.arange(A) - starts[se]
        valid = rank < CAPACITY
        buf = jnp.zeros((NUM_EXPERTS, CAPACITY, H), x.dtype).at[se, rank].set(x[st], mode='drop')
        h = jnp.einsum('ech,efh->ecf', buf, expert_w1)
        x1, x2 = jnp.split(h, 2, axis=-1)
        out = jnp.einsum('ecf,ehf->ech', x1 * jax.nn.silu(x2), expert_w2)
        y = out[se, jnp.clip(rank, 0, CAPACITY - 1)]
        y = jnp.where(valid[:, None], y * sw[:, None].astype(y.dtype), 0.0)
        combined = jnp.zeros((T, H), x.dtype).at[st].add(y)
        return (shared_out + combined).reshape(B, S, H)
    x = L0_attn_x
    x = x + _layernorm(_L0_attn_ref(_layernorm(x, axis=-1), L0_attn_Wq, L0_attn_Wk, L0_attn_Wv, L0_attn_Wo, L0_attn_bo), axis=-1)
    x = x + _layernorm(_L0_ffn_ref(_layernorm(x, axis=-1), L0_ffn_weight, L0_ffn_disha), axis=-1)
    x = x + _layernorm(_L1_attn_ref(_layernorm(x, axis=-1), L1_attn_Wq, L1_attn_bq, L1_attn_Wk, L1_attn_bk, L1_attn_Wv, L1_attn_bv, L1_attn_Wo, L1_attn_bo, L1_attn_ln_g, L1_attn_ln_b), axis=-1)
    x = x + _layernorm(_L1_ffn_ref(_layernorm(x, axis=-1), L1_ffn_wg, L1_ffn_shared_w1, L1_ffn_shared_w2, L1_ffn_expert_w1, L1_ffn_expert_w2), axis=-1)
    return x

_drawn_inputs = setup_inputs


def setup_inputs(seed=0):
    import zlib

    import numpy as np

    out = dict(_drawn_inputs(seed))
    spreads = {'L0_attn_bo': (0.0, 0.1),
     'L1_attn_bq': (0.0, 0.3),
     'L1_attn_bk': (0.0, 0.1),
     'L1_attn_bv': (0.0, 0.1),
     'L1_attn_bo': (0.0, 0.1),
     'L1_attn_ln_g': (1.0, 0.2),
     'L1_attn_ln_b': (0.0, 0.1)}
    factors = {}
    for name, (base, spread) in spreads.items():
        noise = np.random.default_rng([zlib.crc32(name.encode()), seed]).standard_normal(out[name].shape)
        drawn = base * np.exp(spread * noise) if base else spread * noise
        out[name] = jnp.asarray(drawn.astype(out[name].dtype))
    for name, factor in factors.items():
        out[name] = (out[name] * factor).astype(out[name].dtype)
    return out
```

```python
from contextlib import ExitStack

import concourse.bass as bass
from concourse import mybir
from concourse.alu_op_type import AluOpType as ALU

ACT = mybir.ActivationFunctionType
AX = mybir.AxisListType.X
F32, BF16, U32 = mybir.dt.float32, mybir.dt.bfloat16, mybir.dt.uint32

P = 128
B, N, D = 8, 512, 256
T = N // P
C = D // P
H, DH = 16, 64
HP = H // 2
INNER = H * DH
L1H = 16
L1N = 1024
KS = 2
NE, TOPK, FFN, CAP = 64, 8, 768, 160
FC = FFN // P
CAPR = CAP - P
SLOTS = NE * CAP
EPS_LN = 1e-5
EPS_F32 = 2.0 ** -23
MASKED = -1e33
LARGE = 3e38
W1C = 2 * FFN * C
EWC = W1C + FC * D


DVE_STEPS, F_STEPS = 127, 40


def slope(h):
    return 1.0 / (2.0 ** (8.0 / H)) ** (h + 1)


def bass_sandwich(nc, x, wq, wk, wv, wo, bo, ffn_w, ffn_d, l1_wq, l1_wqT, l1_bq, l1_wk, l1_bk, l1_wv, l1_bv,
                  l1_wo, l1_bo, ln_g, ln_b, wgT, sw, ew, out):
    disp = nc.dram_tensor("disp", [SLOTS, D], F32).ap()
    eout = nc.dram_tensor("eout", [SLOTS + 1, D], F32).ap()
    x3_d = nc.dram_tensor("x3_d", [B, P, T * D], F32).ap()
    hT_d = nc.dram_tensor("hT_d", [B, P, C * N], F32).ap()
    slot_d = nc.dram_tensor("slot_d", [B, P, T * TOPK], U32).ap()
    gate_d = nc.dram_tensor("gate_d", [B, P, T * TOPK], F32).ap()
    x_v = x.rearrange("b (t p) d -> b p t d", p=P)
    out_v = out.rearrange("b (t p) d -> b p t d", p=P)

    ctx = ExitStack()
    with ctx:
        def sb(name, shape, dt=F32):
            return ctx.enter_context(nc.sbuf_tensor(name, shape, dt))

        def sem(name):
            return ctx.enter_context(nc.semaphore(name))

        bank = [ctx.enter_context(nc.psum_tensor(f"bank{i}", [P, 512], F32)) for i in range(8)]

        ident = sb("ident", [P, P])
        dist = sb("dist", [P, N])
        tri = sb("tri", [P, P], BF16)
        ones_b = sb("ones_b", [P, P], BF16)
        ones_f = sb("ones_f", [P, P])
        blocks = sb("blocks", [P, P])
        ebase = sb("ebase", [P, NE])
        big_w = sb("big_w", [P, 2 * EWC])
        wq_s, wk_s, wv_s = (big_w[:, j * C * INNER:(j + 1) * C * INNER].rearrange("p (c f) -> p c f", c=C)
                            for j in range(3))
        wo_s = big_w[:, 3 * C * INNER:3 * C * INNER + HP * D].rearrange("p (h d) -> p h d", h=HP)
        bo_b = sb("bo_b", [P, D])
        weff = sb("weff", [P, C, D])
        disha2 = sb("disha2", [P, D])
        a_qT = sb("a_qT", [P, C, D])
        a_k = sb("a_k", [P, KS, C, D])
        a_v = sb("a_v", [P, KS, C, D])
        bq_c = sb("bq_c", [P, C])
        bq_b = sb("bq_b", [P, C, P])
        bk_c = sb("bk_c", [P, KS, C])
        bv_b = sb("bv_b", [P, KS, D])
        nbv_b = sb("nbv_b", [P, KS, D])
        lng_c = sb("lng_c", [P, C])
        lnb_c = sb("lnb_c", [P, C])
        lnb_b = sb("lnb_b", [P, C, P])
        l1wo_raw = sb("l1wo_raw", [P, C, D])
        l1wo_s = sb("l1wo_s", [P, C, D])
        l1bo_b = sb("l1bo_b", [P, D])
        wg_s = sb("wg_s", [P, C, NE])

        xs = sb("xs", [P, T, D])
        xn = sb("xn", [P, T, D + 4])
        xT = sb("xT", [P, C, N])
        v_s = sb("v_s", [P, T, INNER])
        qT = sb("qT", [P, 2, N])
        kpad = sb("kpad", [P, 2, 2, N])
        alibi = sb("alibi", [P, 2, N])
        negs = sb("negs", [P, 2, 10 * P])
        prob = sb("prob", [P, 2, 10 * P])
        negmax = sb("negmax", [P, H, T])
        psumm = sb("psumm", [P, H, T])
        rsum = sb("rsum", [P, H, T])
        pT = sb("pT", [P, 2, 10 * P])
        oT = sb("oT", [P, HP, N])
        y = sb("y", [P, T, D])
        z = sb("z", [P, T, D])
        x1 = sb("x1", [P, T, D])
        x2 = sb("x2", [P, T, D])
        stats = sb("stats", [P, T, 6])
        mv = sb("mv", [P, T, 2])
        rstd = sb("rstd", [P, T])
        vare = sb("vare", [P, T])
        minus_half = sb("minus_half", [P, T])
        gram = sb("gram", [P, C, D + 4])
        ssum_b = sb("ssum_b", [P, C, P])
        t1 = sb("t1", [P, KS, C, D])
        u_b = sb("u_b", [P, KS, D])
        st = sb("st", [P, KS, C, P])
        sbd = sb("sbd", [P, C, P])
        mix = sb("mix", [P, C, D])
        bqs_b = sb("bqs_b", [P, D])
        hT = sb("hT", [P, C, N])
        nlmax = sb("nlmax", [P, T])
        lsum = sb("lsum", [P, T])
        rlsum = sb("rlsum", [P, T])
        lexp = sb("lexp", [P, T, NE])
        gates = sb("gates", [P, T, NE])
        top8 = sb("top8", [P, T, TOPK])
        rest = sb("rest", [P, T, NE])
        sel = sb("sel", [P, T, NE])
        sel_b = sb("sel_b", [P, T, NE], BF16)
        cum = sb("cum", [P, NE], BF16)
        cum_add = sb("cum_add", [P, NE])
        den = sb("den", [P, T])
        wdense = sb("wdense", [P, T, NE])
        valid = sb("valid", [P, T, NE])
        key = sb("key", [P, T, NE])
        key8 = sb("key8", [P, T, TOPK])
        slot = sb("slot", [P, T, TOPK], U32)
        eqw = negs[:].rearrange("p a n -> p (a n)")[:, 0:T * TOPK * NE].rearrange("p (k e) -> p k e", e=NE)
        gate8 = sb("gate8", [P, T * TOPK])
        hn = sb("hn", [P, T, D])

        ew_s = big_w[:].rearrange("p (s f) -> p s f", s=2)
        pT_f = pT[:].rearrange("p a n -> p (a n)")
        sil = pT_f[:, 0:1024].rearrange("p (s n) -> p s n", s=2)
        act_e = pT_f[:, 1024:1024 + FC * CAP].rearrange("p (f n) -> p f n", f=FC)
        xbT = pT_f[:, 2048:2048 + C * CAP].rearrange("p (c n) -> p c n", c=C)
        eo = gram[:].rearrange("p c d -> p (c d)")[:, 0:C * CAP].rearrange("p (c n) -> p c n", c=C)
        xb = qT[:, 0].rearrange("p (s d) -> p s d", s=2)
        ebo = qT[:, 1].rearrange("p (s d) -> p s d", s=2)
        xb2 = alibi[0:CAPR, 0].rearrange("p (s d) -> p s d", s=2)
        ebo2 = alibi[0:CAPR, 1].rearrange("p (s d) -> p s d", s=2)

        sw_s = ew_s[:, 0]
        gat = v_s[:].rearrange("p t f -> p (t f)").rearrange("p (s k d) -> p s k d", s=2, k=TOPK)
        act_s = oT[:, 0:FC]

        setup_loaded, setup_made, setup_dve, zeros_made = (
            sem("setup_loaded"), sem("setup_made"), sem("setup_dve"), sem("zeros_made"))
        setup_pe, ready, zeroed = sem("setup_pe"), sem("ready"), sem("zeroed")
        xs_loaded, xs_used = sem("xs_loaded"), sem("xs_used")
        dve_order = sem("dve_order")
        normed, transposed, xT_ready = sem("normed"), sem("transposed"), sem("xT_ready")
        v_psum, v_ready, qk_psum, qk_ready = sem("v_psum"), sem("v_ready"), sem("qk_psum"), sem("qk_ready")
        scores, biased, exped = sem("scores"), sem("biased"), sem("exped")
        rsum_ready, probs = sem("rsum_ready"), sem("probs")
        pT_psum, pT_ready, oT_psum, oT_ready = sem("pT_psum"), sem("pT_ready"), sem("oT_psum"), sem("oT_ready")
        proj_psum = sem("proj_psum")
        gram_psum, gram_ready, ssum_ready = sem("gram_psum"), sem("gram_ready"), sem("ssum_ready")
        t1_psum, t1_ready, state_psum, sbd_ready = sem("t1_psum"), sem("t1_ready"), sem("state_psum"), sem("sbd_ready")
        mix_psum, mix_ready = sem("mix_psum"), sem("mix_ready")
        x3_ready, batch_stores, stored = sem("x3_ready"), sem("batch_stores"), sem("stored")
        logits_psum, lmax_ready, lexp_ready = sem("logits_psum"), sem("lmax_ready"), sem("lexp_ready")
        sel_ready, rank_psum, key8_ready, slot_ready = (
            sem("sel_ready"), sem("rank_psum"), sem("key8_ready"), sem("slot_ready"))
        eqw_ready, eq_ready, gate8_ready = sem("eqw_ready"), sem("eq_ready"), sem("gate8_ready")
        dispatched, rows_sent = sem("dispatched"), sem("rows_sent")
        w_loaded = [sem(f"w_loaded{i}") for i in range(2)]
        xb_loaded = [sem(f"xb_loaded{i}") for i in range(2)]
        xb_psum, xbT_ready, h_psum, sil_ready, act_ready = (
            sem("xb_psum"), sem("xbT_ready"), sem("h_psum"), sem("sil_ready"), sem("act_ready"))
        eo_psum, eo_ready, ebo_psum, ebo_ready, ebo_stored, ebo_free = (
            sem("eo_psum"), sem("eo_ready"), sem("ebo_psum"), sem("ebo_ready"), sem("ebo_stored"), sem("ebo_free"))
        sw_loaded, f_hT, f_x3, f_gates = sem("sw_loaded"), sem("f_hT"), sem("f_x3"), sem("f_gates")
        sh_psum, ssil_ready, sact_ready, sout_psum = (
            sem("sh_psum"), sem("ssil_ready"), sem("sact_ready"), sem("sout_psum"))
        gathered = [sem(f"gathered{i}") for i in range(2)]
        gat_used, f_order, f_made, out_stored, out_free = (
            sem("gat_used"), sem("f_order"), sem("f_made"), sem("out_stored"), sem("out_free"))

        var_ready, rstd_ready = sem("var_ready"), sem("rstd_ready")
        passed, pool_passed = sem("passed"), sem("pool_passed")

        LN_ROUNDS = 8
        ROUNDS = 5
        R_ATT, R_FFN, R_L1, R_L1O, R_MOE = range(ROUNDS)
        COLS = [(t + 1) * P for t in range(T)]
        S_UNITS = [[(3, 0)], [(2, 0), (0, 3 * P)], [(1, 0)]]
        P_AT = {3: 0, 2: 512, 0: 896, 1: 1024}
        T_UNITS = [[(0, 0)], [(1, 0), (3, 384)], [(2, 0)]]
        T_AT = {0: 0, 1: 512, 3: 896, 2: 1024}
        T_BASE = [0, 512, 1024]
        T_COLS = [512, 512, 256]

        block = ctx.enter_context(nc.Block())

        @block.sync
        def _(sp):
            col = "(c p) f -> p c f"
            loads = [(wq_s, wq.rearrange(col, p=P)), (wk_s, wk.rearrange(col, p=P)),
                     (wv_s, wv.rearrange(col, p=P)), (wo_s, wo.rearrange(col, p=P)),
                     (weff[:], ffn_w.rearrange(col, p=P)), (a_qT[:], l1_wqT.rearrange(col, p=P)),
                     (l1wo_raw[:], l1_wo.rearrange(col, p=P)), (wg_s[:], wgT.rearrange(col, p=P)),
                     (disha2[0:64, :], ffn_d), (disha2[64:128, :], ffn_d),
                     (bo_b[:], bo.partition_broadcast(P)), (l1bo_b[:], l1_bo.partition_broadcast(P))]
            for k in range(KS):
                loads += [(a_k[:, k], l1_wk[k].rearrange(col, p=P)), (a_v[:, k], l1_wv[k].rearrange(col, p=P)),
                          (bv_b[:, k], l1_bv[k].partition_broadcast(P))]
            for dst, src in loads:
                sp.dma_start(dst, src).then_inc(setup_loaded, 16)
            with nc.allow_non_contiguous_dma(reason="short bias columns"):
                for dst, src in ((bq_c, l1_bq), (lng_c, ln_g), (lnb_c, ln_b)):
                    sp.dma_start(dst[:], src.rearrange("(c p) -> p c", p=P)).then_inc(setup_loaded, 16)
                for k in range(KS):
                    sp.dma_start(bk_c[:, k], l1_bk[k].rearrange("(c p) -> p c", p=P)).then_inc(setup_loaded, 16)
            sp.dma_start(xs[:], x_v[0]).then_inc(xs_loaded, 16)
            sp.sem_inc(stored, 1)

            def batch_out(b):
                sp.wait_ge(x3_ready, b + 1)
                sp.dma_start(x3_d[b], x2[:].rearrange("p t d -> p (t d)")).then_inc(batch_stores, 16)
                sp.wait_ge(xT_ready, b * (C * ROUNDS) + C * ROUNDS)
                sp.dma_start(hT_d[b], hT[:].rearrange("p c n -> p (c n)")).then_inc(batch_stores, 16)
                sp.wait_ge(slot_ready, b + 1)
                sp.dma_start(slot_d[b], slot[:].rearrange("p t k -> p (t k)")).then_inc(batch_stores, 16)
                sp.wait_ge(gate8_ready, b + 1)
                sp.dma_start(gate_d[b], gate8[:]).then_inc(batch_stores, 16)
                sp.wait_ge(batch_stores, b * 64 + 64)
                sp.sem_inc(stored, 1)

            with sp.Fori(0, B - 1) as b:
                sp.wait_ge(xs_used, b + 1)
                sp.dma_start(xs[:], x_v[b + 1]).then_inc(xs_loaded, 16)
                batch_out(b)
            sp.wait_ge(proj_psum, 8 * (B - 1) + 2)
            for e in range(2):
                sp.dma_start(ew_s[:, e], ew[e]).then_inc(w_loaded[e], 16)
            batch_out(B - 1)

            def load_rows(e, s):
                sp.dma_start(xb[:, s], disp_e[e][0:P]).then_inc(xb_loaded[s], 16)
                sp.dma_start(xb2[:, s], disp_e[e][P:CAP]).then_inc(xb_loaded[s], 16)

            def store_rows(e, s):
                sp.wait_ge(ebo_ready, 2 * e + 2)
                sp.dma_start(eout_e[e][0:P], ebo[:, s]).then_inc(ebo_stored, 16)
                sp.dma_start(eout_e[e][P:CAP], ebo2[:, s]).then_inc(ebo_stored, 16)
                sp.wait_ge(ebo_stored, 32 * e + 32)
                sp.sem_inc(ebo_free, 1)

            disp_e = disp.rearrange("(e c) d -> e c d", c=CAP)
            eout_e = eout[0:SLOTS].rearrange("(e c) d -> e c d", c=CAP)
            sp.wait_ge(rows_sent, B + 1)
            sp.sem_inc(ebo_free, 2)
            for e in range(2):
                load_rows(e, e)
            with sp.Fori(0, NE // 2 - 1) as j:
                for s in range(2):
                    e = 2 * j + s
                    sp.wait_ge(xb_psum, 2 * j + (s + 1))
                    load_rows(2 * j + (s + 2), s)
                    sp.wait_ge(eo_psum, 2 * j + (s + 1))
                    sp.dma_start(ew_s[:, s], ew[2 * j + (s + 2)]).then_inc(w_loaded[s], 16)
                    store_rows(e, s)
            sp.wait_ge(eo_psum, NE - 1)
            sp.dma_start(sw_s, sw).then_inc(sw_loaded, 16)
            for s in range(2):
                store_rows(NE - 2 + s, s)

            def load_hT(b):
                sp.dma_start(hT[:].rearrange("p c n -> p (c n)"), hT_d[b]).then_inc(f_hT, 16)

            def load_rest(b):
                sp.dma_start(slot[:].rearrange("p t k -> p (t k)"), slot_d[b]).then_inc(f_gates, 16)
                sp.dma_start(gate8[:], gate_d[b]).then_inc(f_gates, 16)
                sp.dma_start(x1[:].rearrange("p t d -> p (t d)"), x3_d[b]).then_inc(f_x3, 16)

            def store_out(b):
                sp.wait_ge(f_made, b + 1)
                sp.dma_start(out_v[b], x2[:]).then_inc(out_stored, 16)

            load_hT(0)
            load_rest(0)
            sp.sem_inc(out_free, 1)
            with sp.Fori(0, B - 1) as b:
                sp.wait_ge(sh_psum, b * (2 * FC) + 2 * FC)
                load_hT(b + 1)
                store_out(b)
                load_rest(b + 1)
                sp.wait_ge(out_stored, b * 16 + 16)
                sp.sem_inc(out_free, 1)
            store_out(B - 1)
            sp.wait_ge(out_stored, 16 * B)
        N_SETUP = 12 + 3 * KS + 3 + KS

        @block.gpsimd
        def _(pool):
            g = nc.gpsimd
            g.memset(ident[:], 0.0).then_inc(setup_made, 1)
            g.memset(ones_b[:], 1.0).then_inc(setup_made, 1)
            g.memset(ones_f[:], 1.0).then_inc(setup_made, 1)
            g.memset(blocks[:], 2.0 ** -20 * (1024.0 / L1N) ** 2).then_inc(setup_made, 1)
            g.memset(tri[:], 1.0).then_inc(setup_made, 1)
            g.memset(cum[:], 0.0).then_inc(setup_made, 1)
            g.memset(kpad[:], 0.0).then_inc(setup_made, 1)
            g.memset(xn[:], 1.0).then_inc(setup_made, 1)
            g.memset(minus_half[:], -0.5).then_inc(setup_made, 1)
            g.iota(dist[:], pattern=[[-1, N]], base=N - P, channel_multiplier=1,
                   allow_small_or_imprecise_dtypes=True).then_inc(setup_made, 1)
            g.iota(ebase[:], pattern=[[-CAP, NE]], base=SLOTS, channel_multiplier=0,
                   allow_small_or_imprecise_dtypes=True).then_inc(setup_made, 1)
            pool.wait_ge(setup_made, 11)
            g.affine_select(out=ident[:], in_=ident[:], compare_op=ALU.not_equal, fill=1.0, base=0,
                            pattern=[[-1, P]], channel_multiplier=1).then_inc(setup_made, 1)
            g.affine_select(out=tri[:], in_=tri[:], compare_op=ALU.is_gt, fill=0.0, base=0,
                            pattern=[[1, P]], channel_multiplier=-1).then_inc(setup_made, 1)
            g.affine_select(out=dist[:], in_=dist[:], compare_op=ALU.is_ge, fill=MASKED, base=N - P,
                            pattern=[[-1, N]], channel_multiplier=1).then_inc(setup_made, 1)
            blk = blocks[:].rearrange("p (h e) -> p h e", e=D // L1H)
            g.affine_select(out=blk, in_=blk, compare_op=ALU.is_ge, fill=0.0, base=0,
                            pattern=[[-(D // L1H), P // (D // L1H)], [0, D // L1H]],
                            channel_multiplier=1).then_inc(setup_made, 1)
            pool.wait_ge(setup_made, 15)
            g.affine_select(out=blk, in_=blk, compare_op=ALU.is_ge, fill=0.0, base=D // L1H - 1,
                            pattern=[[D // L1H, P // (D // L1H)], [0, D // L1H]],
                            channel_multiplier=-1).then_inc(setup_made, 1)
            pool.sem_inc(rows_sent, 1)
            pool.wait_ge(zeroed, 1)
            def rsqrt(n):
                pool.wait_ge(var_ready, n)
                g.tensor_tensor(rstd[:], vare[:], minus_half[:], ALU.pow).then_inc(rstd_ready, 1)

            with pool.Fori(0, B) as b:
                rsqrt(b * LN_ROUNDS + 1)
                for n in range(H):
                    pool.wait_ge(exped, b * (H * T) + (n + 1) * T)
                    pool.wait_ge(rsum_ready, b * H + (n + 1))
                    for t in range(T):
                        pr = prob[:, n % 2, P_AT[t]:P_AT[t] + COLS[t]]
                        i = g.tensor_tensor(pr, pr, rsum[:, n, t:t + 1].to_broadcast([P, COLS[t]]), ALU.mult)
                    i.then_inc(probs, 1)
                for r in range(1, LN_ROUNDS):
                    rsqrt(b * LN_ROUNDS + r + 1)
                pool.wait_ge(eq_ready, b * T + T)
                e4 = eqw.rearrange("p (t k) e -> p t k e", k=TOPK)
                w4 = wdense[:].rearrange("p t (a e) -> p t a e", a=1).to_broadcast([P, T, TOPK, NE])
                for t in range(T):
                    i = g.tensor_tensor(e4[:, t], e4[:, t], w4[:, t], ALU.mult)
                i.then_inc(eqw_ready, 1)
                pool.wait_ge(slot_ready, b + 1)
                pool.sem_inc(pool_passed, 1)
                for t in range(T):
                    for k in range(TOPK):
                        g.indirect_dma_start(
                            out=disp, out_offset=bass.IndirectOffsetOnAxis(ap=slot[:, t, k:k + 1], axis=0),
                            in_=hn[:, t, :], in_offset=None, bounds_check=SLOTS - 1,
                            oob_is_err=False).then_inc(dispatched, 16)
                pool.wait_ge(dispatched, b * (16 * T * TOPK) + 16 * T * TOPK)
                pool.sem_inc(rows_sent, 1)

            pool.wait_ge(ebo_free, NE + 2)
            pool.sem_inc(gat_used, 2)
            with pool.Fori(0, B) as b:
                pool.wait_ge(f_gates, b * 32 + 32)
                for t in range(T):
                    pool.wait_ge(gat_used, b * T + t + 1)
                    pool.sem_inc(pool_passed, 1)
                    for k in range(TOPK):
                        g.indirect_dma_start(
                            out=gat[:, t % 2, k], out_offset=None, in_=eout,
                            in_offset=bass.IndirectOffsetOnAxis(ap=slot[:, t, k:k + 1], axis=0),
                            bounds_check=SLOTS, oob_is_err=False).then_inc(gathered[t % 2], 16)
                rsqrt(b + (LN_ROUNDS * B + 1))

        @block.scalar
        def _(act):
            a = nc.scalar
            act.wait_ge(setup_made, 16)
            zrow = kpad[:].rearrange("p a b n -> p (a b n)")
            rows = SLOTS // P
            per = 4 * N // D
            dz = disp.rearrange("(p r) d -> p (r d)", p=P)
            for r in range(rows // per):
                act.dma_start(dz[:, r * per * D:(r + 1) * per * D], zrow).then_inc(zeros_made, 16)
            act.dma_start(eout[SLOTS:SLOTS + 1, :], zrow[0:1, 0:D]).then_inc(zeros_made, 16)
            act.wait_ge(setup_loaded, 16 * N_SETUP)
            for c in range(C):
                a.activation(bq_b[:, c], ones_f[:], ACT.Copy, scale=bq_c[:, c:c + 1]).then_inc(setup_pe, 1)
                a.activation(lnb_b[:, c], ones_f[:], ACT.Copy, scale=lnb_c[:, c:c + 1]).then_inc(setup_pe, 1)
            act.wait_ge(zeros_made, 16 * (rows // per + 1))
            act.sem_inc(zeroed, 1)
            act.wait_ge(ready, 1)

            with act.Fori(0, B) as b:
                def xT_evac(r, dst):
                    for c in range(C):
                        act.wait_ge(transposed, b * (C * ROUNDS) + r * C + c + 1)
                        a.activation(dst[:, c], bank[4 + c][:], ACT.Copy).then_inc(xT_ready, 1)

                xT_evac(R_ATT, xT)
                for hp in range(HP):
                    for s in range(2):
                        n = 2 * hp + s
                        for q, t in enumerate((3, 2, 0, 1)):
                            act.wait_ge(biased, b * (H * T) + n * T + q + 1)
                            a.activation(prob[:, s, P_AT[t]:P_AT[t] + COLS[t]], negs[:, s, P_AT[t]:P_AT[t] + COLS[t]],
                                         ACT.Exp, bias=negmax[:, n, t:t + 1], scale=-1.0,
                                         accum_out=psumm[:, n, t:t + 1]).then_inc(exped, 1)
                    for s in range(2):
                        for u in range(3):
                            m = (2 * hp + s) * 3 + u
                            act.wait_ge(pT_psum, b * (3 * H) + m + 1)
                            a.activation(pT[:, s, T_BASE[u]:T_BASE[u] + T_COLS[u]], bank[4 + m % 2][:, 0:T_COLS[u]],
                                         ACT.Copy).then_inc(pT_ready, 1)
                xT_evac(R_FFN, xT)
                xT_evac(R_L1, xT)
                for c in range(C):
                    act.wait_ge(gram_psum, b * C + c + 1)
                    a.activation(gram[:, c, 0:D + 1], bank[6 + c][:, 0:D + 1], ACT.Copy).then_inc(gram_ready, 1)
                act.wait_ge(gram_ready, b * C + C)
                for c in range(C):
                    a.activation(ssum_b[:, c], ones_f[:], ACT.Copy, scale=gram[:, c, D:D + 1]).then_inc(ssum_ready, 1)
                act.wait_ge(mix_psum, b + 1)
                a.activation(mix[:].rearrange("p c d -> p (c d)"), bank[6][:], ACT.Copy).then_inc(mix_ready, 1)
                xT_evac(R_L1O, xT)
                act.wait_ge(stored, b + 1)
                xT_evac(R_MOE, hT)
                act.wait_ge(lmax_ready, b + 1)
                for t in range(T):
                    a.activation(lexp[:, t], bank[2][:, t * NE:(t + 1) * NE], ACT.Exp, bias=nlmax[:, t:t + 1],
                                 accum_out=lsum[:, t:t + 1]).then_inc(lexp_ready, 1)

            def expert(e, s):
                for half in range(2):
                    act.wait_ge(h_psum, 4 * e + 2 * half + 1)
                    a.activation(sil[:, half, 0:3 * CAP], bank[2 * half][:, 0:3 * CAP], ACT.Silu).then_inc(sil_ready, 1)
                act.wait_ge(ebo_psum, e + 1)
                act.wait_ge(ebo_free, e + 1)
                a.activation(ebo[:, s], bank[5][:, 0:D], ACT.Copy).then_inc(ebo_ready, 1)
                a.activation(ebo2[:, s], bank[5][0:CAPR, D:2 * D], ACT.Copy).then_inc(ebo_ready, 1)

            with act.Fori(0, NE // 2) as j:
                for s in range(2):
                    expert(2 * j + s, s)

            with act.Fori(0, B) as b:
                for f in range(FC):
                    act.wait_ge(sh_psum, b * (2 * FC) + 2 * f + 1)
                    if f >= 2:
                        act.wait_ge(sact_ready, b * FC + f - 1)
                    a.activation(sil[:, f % 2], bank[2 * (f % 2)][:], ACT.Silu).then_inc(ssil_ready, 1)

        @block.vector
        def _(dve):
            v = nc.vector
            dve.wait_ge(setup_loaded, 16 * N_SETUP)
            dve.wait_ge(setup_made, 16)
            made = [0]

            def setup(i):
                made[0] += 1
                i.then_inc(setup_dve, 1)

            for c in range(C):
                setup(v.tensor_tensor(weff[:, c], weff[:, c], disha2[:], ALU.add))
                diag = slice(c * P, (c + 1) * P)
                setup(v.tensor_tensor(a_qT[:, c, diag], a_qT[:, c, diag], ident[:], ALU.add))
                setup(v.tensor_scalar(l1wo_s[:, c], l1wo_raw[:, c], lng_c[:, c:c + 1], None, ALU.mult))
                for k in range(KS):
                    setup(v.tensor_tensor(a_k[:, k, c, diag], a_k[:, k, c, diag], ident[:], ALU.add))
                    setup(v.tensor_tensor(a_v[:, k, c, diag], a_v[:, k, c, diag], ident[:], ALU.add))
            setup(v.tensor_scalar(nbv_b[:], bv_b[:], float(N), None, ALU.mult))
            dve.wait_ge(setup_pe, 2 * C + 1)
            setup(v.tensor_tensor(l1bo_b[:], l1bo_b[:], bank[0][:, 0:D], ALU.add))
            dve.wait_ge(setup_dve, made[0])
            dve.wait_ge(zeroed, 1)
            dve.sem_inc(ready, 1)

            with dve.Fori(0, B) as b:
                count, rounds = [0], [0]

                def did(i):
                    count[0] += 1
                    return i.then_inc(dve_order, 1)

                def in_order():
                    dve.wait_ge(dve_order, b * DVE_STEPS + count[0])

                def fixed():
                    dve.sem_inc(passed, 1)

                def moments(src):
                    in_order()
                    for t in range(T):
                        did(v.bn_stats(stats[:, t, :], src(t)))
                    in_order()
                    fixed()
                    for t in range(T):
                        did(v.bn_aggr(mv[:, t, :], stats[:, t, :]))
                    in_order()
                    v.tensor_scalar(vare[:], mv[:, :, 1], EPS_LN, None, ALU.add).then_inc(var_ready, 1)
                    rounds[0] += 1
                    dve.wait_ge(rstd_ready, b * LN_ROUNDS + rounds[0])

                def norm(dst, src, signal=None):
                    moments(src)
                    for t in range(T):
                        i = v.tensor_scalar(dst(t), src(t), mv[:, t, 0:1], rstd[:, t:t + 1], ALU.subtract, ALU.mult)
                        if signal is None:
                            did(i)
                        else:
                            i.then_inc(signal, 1)

                def xn_t(t):
                    return xn[:, t, 0:D]

                def proj(t):
                    return bank[t // 2][:, (t % 2) * D:(t % 2 + 1) * D]

                def whole(x_):
                    return x_[:].rearrange("p t d -> p (t d)")

                dve.wait_ge(xs_loaded, b * 16 + 16)
                norm(xn_t, lambda t: xs[:, t, :], normed)
                for u in range(2 * T):
                    dve.wait_ge(v_psum, b * (2 * T) + u + 1)
                    v.tensor_copy(v_s[:, u // 2, (u % 2) * 512:(u % 2 + 1) * 512],
                                  bank[2 + u % 2][:]).then_inc(v_ready, 1)

                def qk_evac(hp):
                    dve.wait_ge(qk_psum, b * (2 * HP) + 2 * hp + 1)
                    v.tensor_scalar(qT[:, hp % 2], bank[2][:], -float(DH) ** -0.5, None, ALU.mult).then_inc(qk_ready, 1)
                    dve.wait_ge(qk_psum, b * (2 * HP) + 2 * hp + 2)
                    v.tensor_copy(kpad[0:DH, hp % 2, 0], bank[3][0:DH, :]).then_inc(qk_ready, 1)
                    v.tensor_copy(kpad[DH:P, hp % 2, 1], bank[3][DH:P, :]).then_inc(qk_ready, 1)

                def bias_and_max(n):
                    s = n % 2
                    if n >= 2:
                        dve.wait_ge(biased, b * (H * T) + (n - 1) * T)
                    did(v.tensor_scalar(alibi[:, s], dist[:], -slope(n), None, ALU.mult))
                    in_order()
                    for u, unit in enumerate(S_UNITS):
                        dve.wait_ge(scores, b * (3 * H) + 3 * n + u + 1)
                        fixed()
                        for t, at in unit:
                            i = v.tensor_tensor_reduce(
                                out=negs[:, s, P_AT[t]:P_AT[t] + COLS[t]],
                                in0=bank[(3 * n + u) % 2][:, at:at + COLS[t]], in1=alibi[:, s, N - COLS[t]:N],
                                scale=1.0, scalar=LARGE, op0=ALU.add, op1=ALU.min,
                                accum_out=negmax[:, n, t:t + 1]).then_inc(biased, 1)

                def reciprocals(n):
                    dve.wait_ge(exped, b * (H * T) + (n + 1) * T)
                    v.reciprocal(rsum[:, n, :], psumm[:, n, :]).then_inc(rsum_ready, 1)

                qk_evac(0)
                for hp in range(HP):
                    bias_and_max(2 * hp)
                    bias_and_max(2 * hp + 1)
                    reciprocals(2 * hp)
                    if hp + 1 < HP:
                        qk_evac(hp + 1)
                    reciprocals(2 * hp + 1)
                    dve.wait_ge(oT_psum, b * HP + hp + 1)
                    v.tensor_copy(oT[:, hp], bank[6 + hp % 2][:]).then_inc(oT_ready, 1)

                for j in range(2):
                    dve.wait_ge(proj_psum, b * 8 + j + 1)
                    did(v.tensor_tensor(y[:, 2 * j:2 * j + 2], bank[j][:].rearrange("p (t d) -> p t d", d=D),
                                        bo_b[:].rearrange("p (a d) -> p a d", a=1).to_broadcast([P, 2, D]), ALU.add))
                norm(lambda t: z[:, t, :], lambda t: y[:, t, :])
                in_order()
                v.tensor_tensor(whole(x1), whole(xs), whole(z), ALU.add).then_inc(xs_used, 1)
                dve.wait_ge(xs_used, b + 1)
                norm(xn_t, lambda t: x1[:, t, :], normed)

                dve.wait_ge(proj_psum, b * 8 + 4)
                norm(lambda t: z[:, t, :], proj)
                dve.wait_ge(stored, b + 1)
                in_order()
                did(v.tensor_tensor(whole(x2), whole(x1), whole(z), ALU.add))
                norm(xn_t, lambda t: x2[:, t, :], normed)

                dve.wait_ge(ssum_ready, b * C + C)
                for k in range(KS):
                    dve.wait_ge(t1_psum, b * KS + k + 1)
                    for m in range(C):
                        v.scalar_tensor_tensor(out=t1[:, k, m], in0=bv_b[:, k], scalar=gram[:, m, D:D + 1],
                                               in1=bank[2 * k][:, m * D:(m + 1) * D], op0=ALU.mult,
                                               op1=ALU.add).then_inc(t1_ready, 1)
                    v.tensor_tensor(u_b[:, k], nbv_b[:, k], bank[2 * k + 1][:, 0:D], ALU.add).then_inc(t1_ready, 1)
                dve.wait_ge(t1_ready, b * 6 + 6)
                for k in range(KS):
                    dve.wait_ge(state_psum, b * KS + k + 1)
                    for c in range(C):
                        did(v.scalar_tensor_tensor(out=st[:, k, c], in0=u_b[:, k, c * P:(c + 1) * P],
                                                   scalar=bk_c[:, k, c:c + 1], in1=bank[4 + k][:, c * P:(c + 1) * P],
                                                   op0=ALU.mult, op1=ALU.add))
                in_order()
                did(v.tensor_tensor(st[:, 0], st[:, 0],
                                    blocks[:].rearrange("p (a e) -> p a e", a=1).to_broadcast([P, C, P]), ALU.mult))
                in_order()
                v.tensor_tensor(sbd[:], st[:, 0], st[:, 1], ALU.mult).then_inc(sbd_ready, 1)
                dve.wait_ge(mix_psum, b + 1)
                did(v.tensor_copy(bqs_b[:], bank[7][:, 0:D]))
                in_order()

                def two_tiles(j, bias):
                    did(v.tensor_tensor(y[:, 2 * j:2 * j + 2], bank[j][:].rearrange("p (t d) -> p t d", d=D),
                                        bias[:].rearrange("p (a d) -> p a d", a=1).to_broadcast([P, 2, D]), ALU.add))

                for j in range(2):
                    dve.wait_ge(proj_psum, b * 8 + 5 + j)
                    two_tiles(j, bqs_b)
                norm(xn_t, lambda t: y[:, t, :], normed)
                in_order()
                for j in range(2):
                    dve.wait_ge(proj_psum, b * 8 + 7 + j)
                    two_tiles(j, l1bo_b)
                norm(lambda t: z[:, t, :], lambda t: y[:, t, :])
                in_order()
                v.tensor_tensor(whole(x2), whole(x2), whole(z), ALU.add).then_inc(x3_ready, 1)
                dve.wait_ge(x3_ready, b + 1)
                dve.wait_ge(rows_sent, b + 1)
                norm(lambda t: hn[:, t, :], lambda t: x2[:, t, :], normed)

                dve.wait_ge(logits_psum, b + 1)
                did(v.tensor_reduce(nlmax[:], bank[2][:, 0:T * NE].rearrange("p (t e) -> p t e", e=NE), AX, ALU.max))
                in_order()
                v.tensor_scalar(nlmax[:], nlmax[:], -1.0, None, ALU.mult).then_inc(lmax_ready, 1)
                dve.wait_ge(lexp_ready, b * T + T)
                did(v.reciprocal(rlsum[:], lsum[:]))
                in_order()

                def per_tile(x_, n):
                    return x_[:].rearrange("p (t a) -> p t a", a=1).to_broadcast([P, T, n])

                did(v.tensor_tensor(gates[:], lexp[:], per_tile(rlsum, NE), ALU.mult))
                in_order()
                fixed()
                for t in range(T):
                    did(v.max(top8[:, t], gates[:, t]))
                in_order()
                fixed()
                for t in range(T):
                    did(v.match_replace(rest[:, t], top8[:, t], gates[:, t], -1.0))
                in_order()
                v.tensor_scalar(sel_b[:], rest[:], -1.0, None, ALU.is_equal).then_inc(sel_ready, 1)
                did(v.tensor_scalar(sel[:], rest[:], -1.0, None, ALU.is_equal))
                did(v.tensor_reduce(den[:], top8[:], AX, ALU.add))
                in_order()
                did(v.tensor_scalar(den[:], den[:], EPS_F32, None, ALU.max))
                in_order()
                did(v.reciprocal(den[:], den[:]))
                did(v.tensor_tensor(wdense[:], gates[:], sel[:], ALU.mult))
                in_order()
                did(v.tensor_tensor(wdense[:], wdense[:], per_tile(den, NE), ALU.mult))
                dve.wait_ge(rank_psum, b + 1)
                rank = bank[3][:, 0:T * NE].rearrange("p (t e) -> p t e", e=NE)
                did(v.scalar_tensor_tensor(out=valid[:], in0=rank, scalar=float(CAP), in1=sel[:],
                                           op0=ALU.is_lt, op1=ALU.mult))
                did(v.tensor_tensor(key[:], ebase[:].rearrange("p (a e) -> p a e", a=1).to_broadcast([P, T, NE]), rank,
                                    ALU.subtract))
                did(v.tensor_reduce(cum_add[:], sel[:].rearrange("p t e -> p e t"), AX, ALU.add))
                in_order()
                did(v.tensor_tensor(key[:], key[:], valid[:], ALU.mult))
                did(v.tensor_tensor(cum[:], cum[:], cum_add[:], ALU.add))
                in_order()
                fixed()
                for t in range(T):
                    v.max(key8[:, t], key[:, t]).then_inc(key8_ready, 1)
                dve.wait_ge(key8_ready, b * T + T)
                v.tensor_scalar(slot[:], key8[:], -1.0, float(SLOTS), ALU.mult, ALU.add).then_inc(slot_ready, 1)
                k4 = key[:].rearrange("p t (a e) -> p t a e", a=1).to_broadcast([P, T, TOPK, NE])
                e4 = eqw.rearrange("p (t k) e -> p t k e", k=TOPK)
                s4 = key8[:].rearrange("p t (k a) -> p t k a", a=1).to_broadcast([P, T, TOPK, NE])
                for t in range(T):
                    v.tensor_tensor(e4[:, t], k4[:, t], s4[:, t], ALU.is_equal).then_inc(eq_ready, 1)
                dve.wait_ge(eqw_ready, b + 1)
                v.tensor_reduce(gate8[:], eqw, AX, ALU.add).then_inc(gate8_ready, 1)
                assert count[0] == DVE_STEPS and rounds[0] == LN_ROUNDS, (count[0], rounds[0])

            with dve.Fori(0, NE // 2) as j:
                for s in range(2):
                    e = 2 * j + s
                    dve.wait_ge(xb_psum, e + 1)
                    v.tensor_copy(xbT.rearrange("p c n -> p (c n)"), bank[6][:, 0:C * CAP]).then_inc(xbT_ready, 1)
                    for half in range(2):
                        dve.wait_ge(sil_ready, 2 * e + half + 1)
                        dve.wait_ge(h_psum, 4 * e + 2 * half + 2)
                        v.tensor_tensor(act_e[:, 3 * half:3 * half + 3].rearrange("p f n -> p (f n)"),
                                        sil[:, half, 0:3 * CAP], bank[2 * half + 1][:, 0:3 * CAP],
                                        ALU.mult).then_inc(act_ready, 1)
                    dve.wait_ge(eo_psum, e + 1)
                    for c in range(C):
                        v.tensor_copy(eo[:, c], bank[(4, 7)[c]][:, 0:CAP]).then_inc(eo_ready, 1)

            with dve.Fori(0, B) as b:
                count = [0]

                def did(i):
                    count[0] += 1
                    return i.then_inc(f_order, 1)

                def in_order():
                    dve.wait_ge(f_order, b * F_STEPS + count[0])

                for f in range(FC):
                    dve.wait_ge(ssil_ready, b * FC + f + 1)
                    dve.wait_ge(sh_psum, b * (2 * FC) + 2 * f + 2)
                    v.tensor_tensor(act_s[:, f], sil[:, f % 2], bank[2 * (f % 2) + 1][:], ALU.mult).then_inc(sact_ready, 1)
                dve.wait_ge(f_gates, b * 32 + 32)
                for t in range(T):
                    dve.wait_ge(gathered[t % 2], b * (16 * TOPK * T // 2) + 16 * TOPK * (t // 2 + 1))
                    if t % 2 == 0:
                        dve.wait_ge(sout_psum, b * (T // 2) + t // 2 + 1)
                    for k in range(TOPK):
                        before = y[:, t] if k else bank[4 + t // 2][:, (t % 2) * D:(t % 2 + 1) * D]
                        i = v.scalar_tensor_tensor(out=y[:, t], in0=gat[:, t % 2, k],
                                                   scalar=gate8[:, t * TOPK + k:t * TOPK + k + 1], in1=before,
                                                   op0=ALU.mult, op1=ALU.add)
                        if k < TOPK - 1:
                            did(i)
                            in_order()
                    i.then_inc(gat_used, 1)
                dve.wait_ge(gat_used, b * T + T + 2)
                for t in range(T):
                    did(v.bn_stats(stats[:, t, :], y[:, t]))
                in_order()
                dve.sem_inc(passed, 1)
                for t in range(T):
                    did(v.bn_aggr(mv[:, t, :], stats[:, t, :]))
                in_order()
                v.tensor_scalar(vare[:], mv[:, :, 1], EPS_LN, None, ALU.add).then_inc(var_ready, 1)
                dve.wait_ge(rstd_ready, b + (LN_ROUNDS * B + 1))
                for t in range(T):
                    did(v.tensor_scalar(z[:, t], y[:, t], mv[:, t, 0:1], rstd[:, t:t + 1], ALU.subtract, ALU.mult))
                in_order()
                dve.wait_ge(f_x3, b * 16 + 16)
                dve.wait_ge(out_free, b + 1)
                v.tensor_tensor(x2[:].rearrange("p t d -> p (t d)"), x1[:].rearrange("p t d -> p (t d)"),
                                z[:].rearrange("p t d -> p (t d)"), ALU.add).then_inc(f_made, 1)
                assert count[0] == F_STEPS, count[0]

        @block.tensor
        def _(pe):
            mm = nc.tensor.matmul
            pe.wait_ge(setup_loaded, 16 * N_SETUP)
            pe.wait_ge(setup_pe, 2 * C)
            for c in range(C):
                i = mm(bank[0][:, 0:D], lnb_b[:, c], l1wo_raw[:, c], start=(c == 0), stop=(c == C - 1))
            i.then_inc(setup_pe, 1)
            pe.wait_ge(ready, 1)

            with pe.Fori(0, B) as b:
                def transposes(r, src=xn):
                    pe.wait_ge(normed, b * (ROUNDS * T) + (r + 1) * T)
                    for c in range(C):
                        for t in range(T):
                            i = nc.tensor.transpose(bank[4 + c][:, t * P:(t + 1) * P], src[:, t, c * P:(c + 1) * P],
                                                    ident[:])
                        i.then_inc(transposed, 1)

                def xT_wait(r):
                    pe.wait_ge(xT_ready, b * (C * ROUNDS) + (r + 1) * C)

                def rows_out(lhs, rhs, chunks):
                    for t in range(T):
                        for c in range(chunks):
                            i = mm(bank[t // 2][:, (t % 2) * D:(t % 2 + 1) * D], lhs[:, c, t * P:(t + 1) * P], rhs(c),
                                   start=(c == 0), stop=(c == chunks - 1), skip_group_check=True)
                        if t % 2:
                            i.then_inc(proj_psum, 1)

                def qk(hp):
                    for j, w in enumerate((wq_s, wk_s)):
                        for c in range(C):
                            i = mm(bank[2 + j][:], w[:, c, hp * P:(hp + 1) * P], xT[:, c], start=(c == 0),
                                   stop=(c == C - 1))
                        i.then_inc(qk_psum, 1)

                transposes(R_ATT)
                xT_wait(R_ATT)
                for u in range(2 * T):
                    if u >= 2:
                        pe.wait_ge(v_ready, b * (2 * T) + u - 1)
                    for c in range(C):
                        i = mm(bank[2 + u % 2][:], xT[:, c, (u // 2) * P:(u // 2 + 1) * P],
                               wv_s[:, c, (u % 2) * 512:(u % 2 + 1) * 512], start=(c == 0), stop=(c == C - 1))
                    i.then_inc(v_psum, 1)
                pe.wait_ge(v_ready, b * (2 * T) + 2 * T)
                qk(0)
                for hp in range(HP):
                    pe.wait_ge(qk_ready, b * (3 * HP) + 3 * hp + 3)
                    for s in range(2):
                        for u, unit in enumerate(S_UNITS):
                            m = (2 * hp + s) * 3 + u
                            if m >= 2:
                                pe.wait_ge(biased, b * (H * T) + ((m - 2) // 3) * T + (1, 3, 4)[(m - 2) % 3])
                            for t, at in unit:
                                i = mm(bank[m % 2][:, at:at + COLS[t]], qT[:, hp % 2, t * P:(t + 1) * P],
                                       kpad[:, hp % 2, s, 0:COLS[t]], start=True, stop=True, skip_group_check=True)
                            i.then_inc(scores, 1)
                    if hp + 1 < HP:
                        qk(hp + 1)
                    for s in range(2):
                        pe.wait_ge(probs, b * H + 2 * hp + s + 1)
                        for u, unit in enumerate(T_UNITS):
                            m = (2 * hp + s) * 3 + u
                            if m >= 2:
                                pe.wait_ge(pT_ready, b * (3 * H) + m - 1)
                            for j, at in unit:
                                for t in range(j, T):
                                    i = nc.tensor.transpose(bank[4 + m % 2][:, at + (t - j) * P:at + (t - j + 1) * P],
                                                            prob[:, s, P_AT[t] + j * P:P_AT[t] + (j + 1) * P], ident[:])
                            i.then_inc(pT_psum, 1)
                    pe.wait_ge(pT_ready, b * (3 * H) + 6 * hp + 6)
                    if hp >= 2:
                        pe.wait_ge(oT_ready, b * HP + hp - 1)
                    for j in range(T):
                        for s in range(2):
                            i = mm(bank[6 + hp % 2][s * DH:(s + 1) * DH, j * P:N],
                                   v_s[:, j, (2 * hp + s) * DH:(2 * hp + s + 1) * DH],
                                   pT[:, s, T_AT[j]:T_AT[j] + N - j * P], start=(j == 0), stop=(j == T - 1),
                                   skip_group_check=True)
                    i.then_inc(oT_psum, 1)
                pe.wait_ge(oT_ready, b * HP + HP)
                rows_out(oT, lambda c: wo_s[:, c], HP)

                transposes(R_FFN)
                xT_wait(R_FFN)
                rows_out(xT, lambda c: weff[:, c], C)

                transposes(R_L1)
                for c in range(C):
                    for t in range(T):
                        i = mm(bank[6 + c][:, 0:D + 2], xn[:, t, c * P:(c + 1) * P], xn[:, t, 0:D + 2], start=(t == 0),
                               stop=(t == T - 1))
                    i.then_inc(gram_psum, 1)
                pe.wait_ge(ssum_ready, b * C + C)
                for k in range(KS):
                    for m in range(C):
                        for c in range(C):
                            mm(bank[2 * k][:, m * D:(m + 1) * D], gram[:, c, m * P:(m + 1) * P], a_v[:, k, c],
                               start=(c == 0), stop=(c == C - 1), skip_group_check=True)
                    for c in range(C):
                        i = mm(bank[2 * k + 1][:, 0:D], ssum_b[:, c], a_v[:, k, c], start=(c == 0), stop=(c == C - 1))
                    i.then_inc(t1_psum, 1)
                xT_wait(R_L1)
                for k in range(KS):
                    pe.wait_ge(t1_ready, b * (3 * KS) + 3 * k + 3)
                    for h in range(C):
                        for m in range(C):
                            i = mm(bank[4 + k][:, h * P:(h + 1) * P], a_k[:, k, m, h * P:(h + 1) * P],
                                   t1[:, k, m, h * P:(h + 1) * P], start=(m == 0), stop=(m == C - 1),
                                   skip_group_check=True)
                    i.then_inc(state_psum, 1)
                pe.wait_ge(sbd_ready, b + 1)
                for h in range(C):
                    for c in range(C):
                        mm(bank[6][:, c * D + h * P:c * D + (h + 1) * P], a_qT[:, h, c * P:(c + 1) * P], sbd[:, h],
                           start=True, stop=True, skip_group_check=True)
                    i = mm(bank[7][:, h * P:(h + 1) * P], bq_b[:, h], sbd[:, h], start=True, stop=True,
                           skip_group_check=True)
                i.then_inc(mix_psum, 1)
                pe.wait_ge(mix_ready, b + 1)
                rows_out(xT, lambda c: mix[:, c], C)
                transposes(R_L1O)
                xT_wait(R_L1O)
                rows_out(xT, lambda c: l1wo_s[:, c], C)

                transposes(R_MOE, hn)
                xT_wait(R_MOE)
                for t in range(T):
                    for c in range(C):
                        i = mm(bank[2][:, t * NE:(t + 1) * NE], hT[:, c, t * P:(t + 1) * P], wg_s[:, c],
                               start=(c == 0), stop=(c == C - 1), skip_group_check=True)
                i.then_inc(logits_psum, 1)
                pe.wait_ge(sel_ready, b + 1)
                for t in range(T):
                    dst = bank[3][:, t * NE:(t + 1) * NE]
                    mm(dst, ones_b[:], cum[:], start=True, stop=False, skip_group_check=True)
                    for s in range(t):
                        mm(dst, ones_b[:], sel_b[:, s], start=False, stop=False, skip_group_check=True)
                    i = mm(dst, tri[:], sel_b[:, t], start=False, stop=True, skip_group_check=True)
                i.then_inc(rank_psum, 1)

            def rows_in(e, s, j):
                pe.wait_ge(xb_loaded[s], j * 32 + 32)
                for c in range(C):
                    nc.tensor.transpose(bank[6][:, c * CAP:c * CAP + P], xb[:, s, c * P:(c + 1) * P], ident[:])
                    i = nc.tensor.transpose(bank[6][:, c * CAP + P:(c + 1) * CAP], xb2[:, s, c * P:(c + 1) * P],
                                            ident[0:CAPR, 0:CAPR])
                i.then_inc(xb_psum, 1)

            def expert(e, s, j, following):
                w1 = ew_s[:, s, 0:W1C].rearrange("p (c f) -> p c f", c=C)
                w2 = ew_s[:, s, W1C:EWC].rearrange("p (f d) -> p f d", f=FC)
                pe.wait_ge(w_loaded[s], j * 16 + 16)
                pe.wait_ge(xbT_ready, e + 1)
                for half in range(2):
                    for part in (1, 0):
                        for q in range(3):
                            f = part * FC + 3 * half + q
                            for c in range(C):
                                i = mm(bank[2 * half + 1 - part][:, q * CAP:(q + 1) * CAP], w1[:, c, f * P:(f + 1) * P],
                                       xbT[:, c], start=(c == 0), stop=(c == C - 1), skip_group_check=True)
                        i.then_inc(h_psum, 1)
                for half in range(2):
                    pe.wait_ge(act_ready, 2 * e + half + 1)
                    for c in range(C):
                        for f in range(3 * half, 3 * half + 3):
                            i = mm(bank[(4, 7)[c]][:, 0:CAP],
                                   w2[:, f, c * P:(c + 1) * P], act_e[:, f], start=(f == 0), stop=(f == FC - 1),
                                   skip_group_check=True)
                i.then_inc(eo_psum, 1)
                if following is not None:
                    rows_in(*following)
                pe.wait_ge(eo_ready, 2 * e + 2)
                for c in range(C):
                    nc.tensor.transpose(bank[5][:, c * P:(c + 1) * P], eo[:, c, 0:P], ident[:])
                    i = nc.tensor.transpose(bank[5][0:CAPR, D + c * P:D + (c + 1) * P], eo[:, c, P:CAP], ident[:])
                i.then_inc(ebo_psum, 1)

            rows_in(0, 0, 0)
            with pe.Fori(0, NE // 2 - 1) as j:
                expert(2 * j, 0, j, (2 * j + 1, 1, j))
                expert(2 * j + 1, 1, j, (2 * j + 2, 0, j + 1))
            expert(NE - 2, 0, NE // 2 - 1, (NE - 1, 1, NE // 2 - 1))
            expert(NE - 1, 1, NE // 2 - 1, None)

            pe.wait_ge(sw_loaded, 16)
            pe.wait_ge(ebo_ready, 2 * NE)
            w1 = sw_s[:, 0:W1C].rearrange("p (c f) -> p c f", c=C)
            w2 = sw_s[:, W1C:EWC].rearrange("p (f d) -> p f d", f=FC)
            with pe.Fori(0, B) as b:
                pe.wait_ge(f_hT, b * 16 + 16)
                for f in range(FC):
                    if f >= 2:
                        pe.wait_ge(sact_ready, b * FC + f - 1)
                    for part in (1, 0):
                        for c in range(C):
                            i = mm(bank[2 * (f % 2) + 1 - part][:], w1[:, c, (part * FC + f) * P:(part * FC + f + 1) * P],
                                   hT[:, c], start=(c == 0), stop=(c == C - 1))
                        i.then_inc(sh_psum, 1)
                pe.wait_ge(sact_ready, b * FC + FC)
                pe.wait_ge(gat_used, b * T + 2)
                for t in range(T):
                    for f in range(FC):
                        i = mm(bank[4 + t // 2][:, (t % 2) * D:(t % 2 + 1) * D], act_s[:, f, t * P:(t + 1) * P], w2[:, f],
                               start=(f == 0), stop=(f == FC - 1), skip_group_check=True)
                    if t % 2:
                        i.then_inc(sout_psum, 1)


_NAMES = ["x", "wq", "wk", "wv", "wo", "bo", "ffn_w", "ffn_d", "l1_wq", "l1_wqT", "l1_bq", "l1_wk", "l1_bk", "l1_wv",
          "l1_bv", "l1_wo", "l1_bo", "ln_g", "ln_b", "wgT", "sw", "ew"]


def _gated_weights(np, w1, w2):
    lead = w1.shape[:-2]
    a = np.swapaxes(w1, -1, -2).reshape(*lead, C, P, 2 * FFN)
    b = np.swapaxes(w2, -1, -2).reshape(*lead, FC, P, D)
    a = np.swapaxes(a, -3, -2).reshape(*lead, P, W1C)
    b = np.swapaxes(b, -3, -2).reshape(*lead, P, FC * D)
    return np.concatenate([a, b], axis=-1)


def kernel(**inputs):
    import numpy as np
    import concourse.bacc as bacc
    from concourse.bass_utils import run_bass_kernel_spmd

    i = {k: np.asarray(v) for k, v in inputs.items()}
    laid = [i["L0_attn_x"], i["L0_attn_Wq"], i["L0_attn_Wk"], i["L0_attn_Wv"], i["L0_attn_Wo"], i["L0_attn_bo"],
            i["L0_ffn_weight"].T, i["L0_ffn_disha"], i["L1_attn_Wq"], i["L1_attn_Wq"].T, i["L1_attn_bq"],
            i["L1_attn_Wk"], i["L1_attn_bk"], i["L1_attn_Wv"], i["L1_attn_bv"], i["L1_attn_Wo"], i["L1_attn_bo"],
            i["L1_attn_ln_g"], i["L1_attn_ln_b"], i["L1_ffn_wg"].T,
            _gated_weights(np, i["L1_ffn_shared_w1"], i["L1_ffn_shared_w2"]),
            _gated_weights(np, i["L1_ffn_expert_w1"], i["L1_ffn_expert_w2"])]
    nc = bacc.Bacc("TRN2", target_bir_lowering=False, num_devices=1)
    arrays, args = {}, []
    for name, a in zip(_NAMES, laid):
        arrays[name] = np.ascontiguousarray(a)
        args.append(nc.dram_tensor(name, a.shape, mybir.dt.from_np(a.dtype), kind="ExternalInput").ap())
    out = nc.dram_tensor("out", [B, N, D], F32, kind="ExternalOutput").ap()
    bass_sandwich(nc, *args, out)
    r = run_bass_kernel_spmd(nc, [arrays], core_ids=[0])
    return r.results[0]["out"]
```

```python
from contextlib import ExitStack

import concourse.bass as bass
from concourse import mybir
from concourse.alu_op_type import AluOpType as ALU

ACT = mybir.ActivationFunctionType
AX = mybir.AxisListType.X
F32, BF16, U32 = mybir.dt.float32, mybir.dt.bfloat16, mybir.dt.uint32

P = 128
B, N, D = 8, 512, 256
T = N // P
C = D // P
H, DH = 16, 64
HP = H // 2
INNER = H * DH
L1H = 16
L1N = 1024
KS = 2
NE, TOPK, FFN, CAP = 64, 8, 768, 160
FC = FFN // P
CAPR = CAP - P
SLOTS = NE * CAP
EPS_LN = 1e-5
EPS_F32 = 2.0 ** -23
MASKED = 1e33
LOWEST = -3e38
W1C = 2 * FFN * C
EWC = W1C + FC * D


ATT_STEPS, POST_STEPS, F_STEPS = 19, 177, 51
RSQRT_GUESS = float(0x5F3759DF)


def slope(h):
    return 1.0 / (2.0 ** (8.0 / H)) ** (h + 1)


def at(i, per, n):
    reg, k = i
    return k * per + n if reg is None else reg * per + (k * per + n)


def index(i):
    reg, k = i
    return k if reg is None else reg + k


def bass_sandwich(nc, x, wq, wk, wv, wo, bo, ffn_w, ffn_d, l1_wq, l1_wqT, l1_bq, l1_wk, l1_bk, l1_wv, l1_bv,
                  l1_wo, l1_bo, ln_g, ln_b, wgT, sw, ew, out):
    disp = nc.dram_tensor("disp", [SLOTS, D], F32).ap()
    eout = nc.dram_tensor("eout", [SLOTS + 1, D], F32).ap()
    x3_d = nc.dram_tensor("x3_d", [B, P, T * D], F32).ap()
    hT_d = nc.dram_tensor("hT_d", [B, P, C * N], F32).ap()
    slot_d = nc.dram_tensor("slot_d", [B, P, T * TOPK], U32).ap()
    gate_d = nc.dram_tensor("gate_d", [B, P, T * TOPK], F32).ap()
    x_v = x.rearrange("b (t p) d -> b p t d", p=P)
    out_v = out.rearrange("b (t p) d -> b p t d", p=P)

    ctx = ExitStack()
    with ctx:
        def sb(name, shape, dt=F32):
            return ctx.enter_context(nc.sbuf_tensor(name, shape, dt))

        def sem(name):
            return ctx.enter_context(nc.semaphore(name))

        bank = [ctx.enter_context(nc.psum_tensor(f"bank{i}", [P, 512], F32)) for i in range(8)]

        ident = sb("ident", [P, P])
        dist = sb("dist", [P, N])
        tri = sb("tri", [P, P], BF16)
        ones_b = sb("ones_b", [P, P], BF16)
        ones_f = sb("ones_f", [P, P])
        blocks = sb("blocks", [P, P])
        ebase = sb("ebase", [P, NE])
        big_w = sb("big_w", [P, 2 * EWC])
        wq_s, wk_s, wv_s = (big_w[:, j * C * INNER:(j + 1) * C * INNER].rearrange("p (c f) -> p c f", c=C)
                            for j in range(3))
        wo_s = big_w[:, 3 * C * INNER:3 * C * INNER + HP * D].rearrange("p (h d) -> p h d", h=HP)
        bo_b = sb("bo_b", [P, D])
        weff = sb("weff", [P, C, D])
        disha2 = sb("disha2", [P, D])
        a_qT = sb("a_qT", [P, C, D])
        a_k = sb("a_k", [P, KS, C, D])
        a_v = sb("a_v", [P, KS, C, D])
        bq_c = sb("bq_c", [P, C])
        bq_b = sb("bq_b", [P, C, P])
        bk_c = sb("bk_c", [P, KS, C])
        bv_b = sb("bv_b", [P, KS, D])
        lng_c = sb("lng_c", [P, C])
        lnb_c = sb("lnb_c", [P, C])
        lnb_b = sb("lnb_b", [P, C, P])
        l1wo_raw = sb("l1wo_raw", [P, C, D])
        l1wo_s = sb("l1wo_s", [P, C, D])
        l1bo_b = sb("l1bo_b", [P, D])
        wg_s = sb("wg_s", [P, C, NE])

        xs = sb("xs", [P, T, D])
        xa = sb("xa", [P, T, D])
        xT = sb("xT", [P, C, N])
        xn = sb("xn", [P, T, D + 4])
        xTp = sb("xTp", [P, C, N])
        v_s = sb("v_s", [P, T, INNER])
        qT = sb("qT", [P, 2, N])
        kpad = sb("kpad", [P, 2, 2, N])
        qscale = sb("qscale", [P, HP])
        biased_s = sb("biased_s", [P, 2, 10 * P])
        prob = sb("prob", [P, 2, 10 * P])
        rawmax = sb("rawmax", [P, H, T])
        negmax = sb("negmax", [P, H, T])
        psumm = sb("psumm", [P, H, T])
        rsum = sb("rsum", [P, H, T])
        pT = sb("pT", [P, 2, 10 * P])
        oT = sb("oT", [P, HP, N])
        y = sb("y", [P, T, D])
        x1 = sb("x1", [P, T, D])
        x2 = sb("x2", [P, T, D])
        stats_a, stats_p = (sb(f"stats{i}", [P, T, 6]) for i in range(2))
        mv_a, mv_p = (sb(f"mv{i}", [P, T, 2]) for i in range(2))
        vare_a, vare_p = (sb(f"vare{i}", [P, T]) for i in range(2))
        rstd_a, rstd_p = (sb(f"rstd{i}", [P, T]) for i in range(2))
        newton_a, newton_p = (sb(f"newton{i}", [P, T]) for i in range(2))
        gram = sb("gram", [P, C, D + 4])
        ssum_b = sb("ssum_b", [P, C, P])
        t1 = sb("t1", [P, KS, C, D])
        u_b = sb("u_b", [P, KS, D])
        st = sb("st", [P, KS, C, P])
        sbd = sb("sbd", [P, C, P])
        mix = sb("mix", [P, C, D])
        bqs_b = sb("bqs_b", [P, D])
        hT = sb("hT", [P, C, N])
        nlmax = sb("nlmax", [P, T])
        lsum = sb("lsum", [P, T])
        rlsum = sb("rlsum", [P, T])
        lexp = sb("lexp", [P, T, NE])
        gates = sb("gates", [P, T, NE])
        top8 = sb("top8", [P, T, TOPK])
        rest = sb("rest", [P, T, NE])
        sel = sb("sel", [P, T, NE])
        sel_b = sb("sel_b", [P, T, NE], BF16)
        cum = sb("cum", [P, NE], BF16)
        cum_add = sb("cum_add", [P, NE])
        den = sb("den", [P, T])
        wdense = sb("wdense", [P, T, NE])
        valid = sb("valid", [P, T, NE])
        key = sb("key", [P, T, NE])
        key8 = sb("key8", [P, T, TOPK])
        slot = sb("slot", [P, T, TOPK], U32)
        gate8 = sb("gate8", [P, T * TOPK])
        hn = sb("hn", [P, T, D])

        ew_s = big_w[:].rearrange("p (s f) -> p s f", s=2)
        pT_f = pT[:].rearrange("p a n -> p (a n)")
        sil = pT_f[:, 0:1024].rearrange("p (s n) -> p s n", s=2)
        act_e = pT_f[:, 1024:1024 + FC * CAP].rearrange("p (f n) -> p f n", f=FC)
        xbT = pT_f[:, 2048:2048 + C * CAP].rearrange("p (c n) -> p c n", c=C)
        eo = gram[:].rearrange("p c d -> p (c d)")[:, 0:C * CAP].rearrange("p (c n) -> p c n", c=C)
        xb = qT[:, 0].rearrange("p (s d) -> p s d", s=2)
        ebo = qT[:, 1].rearrange("p (s d) -> p s d", s=2)
        xb2 = xTp[0:CAPR, 0].rearrange("p (s d) -> p s d", s=2)
        ebo2 = xTp[0:CAPR, 1].rearrange("p (s d) -> p s d", s=2)

        sw_s = ew_s[:, 0]
        gat = v_s[:].rearrange("p t f -> p (t f)").rearrange("p (s k d) -> p s k d", s=2, k=TOPK)
        act_s = oT[:, 0:FC]

        att_loaded, post_loaded, setup_made, zeros_made = (
            sem("att_loaded"), sem("post_loaded"), sem("setup_made"), sem("zeros_made"))
        scales_made, setup_dve, setup_pe, ready = sem("scales_made"), sem("setup_dve"), sem("setup_pe"), sem("ready")
        xs_loaded, xs_used, x1_loaded, x1_used = sem("xs_loaded"), sem("xs_used"), sem("x1_loaded"), sem("x1_used")
        att_order, x_normed, x_transposed, xT_ready = (
            sem("att_order"), sem("x_normed"), sem("x_transposed"), sem("xT_ready"))
        v_psum, v_ready = sem("v_psum"), sem("v_ready")
        q_psum, q_ready, k_psum, k_ready = sem("q_psum"), sem("q_ready"), sem("k_psum"), sem("k_ready")
        scores, biased, max_ready, exped = sem("scores"), sem("biased"), sem("max_ready"), sem("exped")
        rsum_ready, probs = sem("rsum_ready"), sem("probs")
        pT_psum, pT_ready, oT_psum, oT_ready = sem("pT_psum"), sem("pT_ready"), sem("oT_psum"), sem("oT_ready")
        wo_psum = sem("wo_psum")
        post_order, normed, transposed, xTp_ready, rows_psum = (
            sem("post_order"), sem("normed"), sem("transposed"), sem("xTp_ready"), sem("rows_psum"))
        gram_psum, gram_ready, ssum_ready = sem("gram_psum"), sem("gram_ready"), sem("ssum_ready")
        t1_psum, t1_ready, state_psum, sbd_ready = sem("t1_psum"), sem("t1_ready"), sem("state_psum"), sem("sbd_ready")
        mix_psum, mix_ready, bqs_ready = sem("mix_psum"), sem("mix_ready"), sem("bqs_ready")
        x3_ready, batch_stores, stored = sem("x3_ready"), sem("batch_stores"), sem("stored")
        logits_psum, lmax_ready, lexp_ready = sem("logits_psum"), sem("lmax_ready"), sem("lexp_ready")
        sel_ready, rank_psum, ranks_read, key8_ready, slot_ready, gate8_ready = (
            sem("sel_ready"), sem("rank_psum"), sem("ranks_read"), sem("key8_ready"), sem("slot_ready"),
            sem("gate8_ready"))
        dispatched, rows_sent = sem("dispatched"), sem("rows_sent")
        w_loaded = [sem(f"w_loaded{i}") for i in range(2)]
        xb_loaded = [sem(f"xb_loaded{i}") for i in range(2)]
        xb_psum, xbT_ready, h_psum, sil_ready, act_ready = (
            sem("xb_psum"), sem("xbT_ready"), sem("h_psum"), sem("sil_ready"), sem("act_ready"))
        eo_psum, eo_ready, ebo_psum, ebo_ready, ebo_stored, ebo_free = (
            sem("eo_psum"), sem("eo_ready"), sem("ebo_psum"), sem("ebo_ready"), sem("ebo_stored"), sem("ebo_free"))
        sw_loaded, f_hT, f_x3, f_gates = sem("sw_loaded"), sem("f_hT"), sem("f_x3"), sem("f_gates")
        sh_psum, ssil_ready, sact_ready, sout_psum = (
            sem("sh_psum"), sem("ssil_ready"), sem("sact_ready"), sem("sout_psum"))
        gathered = [sem(f"gathered{i}") for i in range(2)]
        gat_used, f_order, f_made, out_stored, out_free = (
            sem("gat_used"), sem("f_order"), sem("f_made"), sem("out_stored"), sem("out_free"))

        passed, pool_passed = sem("passed"), sem("pool_passed")

        ROUNDS = 4
        R_FFN, R_L1, R_L1O, R_MOE = range(ROUNDS)
        ROWS = 6
        POINTS = 2 * HP + 1
        PA, PB = 6, 7
        COLS = [(t + 1) * P for t in range(T)]
        S_UNITS = [[(3, 0)], [(2, 0), (0, 3 * P)], [(1, 0)]]
        P_AT = {3: 0, 2: 512, 0: 896, 1: 1024}
        T_UNITS = [[(0, 0)], [(1, 0), (3, 384)], [(2, 0)]]
        T_AT = {0: 0, 1: 512, 3: 896, 2: 1024}
        T_BASE = [0, 512, 1024]
        T_COLS = [512, 512, 256]

        block = ctx.enter_context(nc.Block())

        N_POST = 12 + 4 * KS
        N_MADE = 18

        @block.sync
        def _(sp):
            col = "(c p) f -> p c f"
            sp.dma_start(xs[:], x_v[0]).then_inc(xs_loaded, 16)
            for dst, src in ((wv_s, wv), (wq_s, wq), (wk_s, wk)):
                sp.dma_start(dst, src.rearrange(col, p=P)).then_inc(att_loaded, 16)
            sp.dma_start(x1[:], x_v[0]).then_inc(x1_loaded, 16)
            loads = [(wo_s, wo.rearrange(col, p=P)),
                     (weff[:], ffn_w.rearrange(col, p=P)), (a_qT[:], l1_wqT.rearrange(col, p=P)),
                     (l1wo_raw[:], l1_wo.rearrange(col, p=P)), (wg_s[:], wgT.rearrange(col, p=P)),
                     (disha2[0:64, :], ffn_d), (disha2[64:128, :], ffn_d),
                     (bo_b[:], bo.partition_broadcast(P)), (l1bo_b[:], l1_bo.partition_broadcast(P))]
            for k in range(KS):
                loads += [(a_k[:, k], l1_wk[k].rearrange(col, p=P)), (a_v[:, k], l1_wv[k].rearrange(col, p=P)),
                          (bv_b[:, k], l1_bv[k].partition_broadcast(P))]
            for dst, src in loads:
                sp.dma_start(dst, src).then_inc(post_loaded, 16)
            with nc.allow_non_contiguous_dma(reason="short bias columns"):
                for dst, src in ((bq_c, l1_bq), (lng_c, ln_g), (lnb_c, ln_b)):
                    sp.dma_start(dst[:], src.rearrange("(c p) -> p c", p=P)).then_inc(post_loaded, 16)
                for k in range(KS):
                    sp.dma_start(bk_c[:, k], l1_bk[k].rearrange("(c p) -> p c", p=P)).then_inc(post_loaded, 16)
            sp.wait_ge(setup_made, N_MADE)
            zrow = y[:].rearrange("p t d -> p (t d)")
            dz = disp.rearrange("(p r) d -> p (r d)", p=P)
            for r in range(SLOTS // P // T):
                sp.dma_start(dz[:, r * T * D:(r + 1) * T * D], zrow).then_inc(zeros_made, 16)
            sp.dma_start(eout[SLOTS:SLOTS + 1, :], zrow[0:1, 0:D]).then_inc(zeros_made, 16)
            sp.sem_inc(stored, 1)

            def load_xs(a):
                sp.wait_ge(xs_used, at(a, 1, 0))
                sp.dma_start(xs[:], x_v[index(a)]).then_inc(xs_loaded, 16)

            def batch_out(p):
                sp.wait_ge(x3_ready, at(p, 1, 1))
                sp.dma_start(x3_d[index(p)], x2[:].rearrange("p t d -> p (t d)")).then_inc(batch_stores, 16)
                sp.wait_ge(xTp_ready, at(p, C * ROUNDS, C * ROUNDS))
                sp.dma_start(hT_d[index(p)], hT[:].rearrange("p c n -> p (c n)")).then_inc(batch_stores, 16)
                sp.wait_ge(slot_ready, at(p, 1, 2))
                sp.dma_start(slot_d[index(p)], slot[:].rearrange("p t k -> p (t k)")).then_inc(batch_stores, 16)
                sp.wait_ge(gate8_ready, at(p, T * TOPK, T * TOPK))
                sp.dma_start(gate_d[index(p)], gate8[:]).then_inc(batch_stores, 16)
                sp.wait_ge(batch_stores, at(p, 64, 64))
                sp.sem_inc(stored, 1)

            def iteration(a, p, following):
                sp.wait_ge(x1_used, at(p, 1, 1))
                sp.dma_start(x1[:], x_v[index(a)]).then_inc(x1_loaded, 16)
                if following is not None:
                    load_xs(following)
                batch_out(p)

            load_xs((None, 1))
            with sp.Fori(0, B - 2) as b:
                iteration((b, 1), (b, 0), (b, 2))
            iteration((None, B - 1), (None, B - 2), None)
            sp.wait_ge(wo_psum, 2 * B)
            for e in range(2):
                sp.dma_start(ew_s[:, e], ew[e]).then_inc(w_loaded[e], 16)
            batch_out((None, B - 1))

            def load_rows(e, s):
                sp.dma_start(xb[:, s], disp_e[e][0:P]).then_inc(xb_loaded[s], 16)
                sp.dma_start(xb2[:, s], disp_e[e][P:CAP]).then_inc(xb_loaded[s], 16)

            def store_rows(e, s):
                sp.wait_ge(ebo_ready, 2 * e + 2)
                sp.dma_start(eout_e[e][0:P], ebo[:, s]).then_inc(ebo_stored, 16)
                sp.dma_start(eout_e[e][P:CAP], ebo2[:, s]).then_inc(ebo_stored, 16)
                sp.wait_ge(ebo_stored, 32 * e + 32)
                sp.sem_inc(ebo_free, 1)

            disp_e = disp.rearrange("(e c) d -> e c d", c=CAP)
            eout_e = eout[0:SLOTS].rearrange("(e c) d -> e c d", c=CAP)
            sp.wait_ge(rows_sent, B + 1)
            sp.sem_inc(ebo_free, 2)
            for e in range(2):
                load_rows(e, e)
            with sp.Fori(0, NE // 2 - 1) as j:
                for s in range(2):
                    e = 2 * j + s
                    sp.wait_ge(xb_psum, 2 * j + (s + 1))
                    load_rows(2 * j + (s + 2), s)
                    sp.wait_ge(eo_psum, 2 * j + (s + 1))
                    sp.dma_start(ew_s[:, s], ew[2 * j + (s + 2)]).then_inc(w_loaded[s], 16)
                    store_rows(e, s)
            sp.wait_ge(eo_psum, NE - 1)
            sp.dma_start(sw_s, sw).then_inc(sw_loaded, 16)
            for s in range(2):
                store_rows(NE - 2 + s, s)

            def load_hT(b):
                sp.dma_start(hT[:].rearrange("p c n -> p (c n)"), hT_d[b]).then_inc(f_hT, 16)

            def load_rest(b):
                sp.dma_start(slot[:].rearrange("p t k -> p (t k)"), slot_d[b]).then_inc(f_gates, 16)
                sp.dma_start(gate8[:], gate_d[b]).then_inc(f_gates, 16)
                sp.dma_start(x1[:].rearrange("p t d -> p (t d)"), x3_d[b]).then_inc(f_x3, 16)

            def store_out(b):
                sp.wait_ge(f_made, b + 1)
                sp.dma_start(out_v[b], x2[:]).then_inc(out_stored, 16)

            load_hT(0)
            load_rest(0)
            sp.sem_inc(out_free, 1)
            with sp.Fori(0, B - 1) as b:
                sp.wait_ge(sh_psum, b * (2 * FC) + 2 * FC)
                load_hT(b + 1)
                store_out(b)
                load_rest(b + 1)
                sp.wait_ge(out_stored, b * 16 + 16)
                sp.sem_inc(out_free, 1)
            store_out(B - 1)
            sp.wait_ge(out_stored, 16 * B)

        @block.gpsimd
        def _(pool):
            g = nc.gpsimd
            g.memset(ident[:], 0.0).then_inc(setup_made, 1)
            g.memset(ones_b[:], 1.0).then_inc(setup_made, 1)
            g.memset(ones_f[:], 1.0).then_inc(setup_made, 1)
            g.memset(blocks[:], 2.0 ** -20 * (1024.0 / L1N) ** 2).then_inc(setup_made, 1)
            g.memset(tri[:], 1.0).then_inc(setup_made, 1)
            g.memset(cum[:], 0.0).then_inc(setup_made, 1)
            g.memset(kpad[:], 0.0).then_inc(setup_made, 1)
            g.memset(xn[:], 1.0).then_inc(setup_made, 1)
            g.memset(y[:], 0.0).then_inc(setup_made, 1)
            g.memset(hn[:], 0.0).then_inc(setup_made, 1)
            g.memset(slot[:], SLOTS).then_inc(setup_made, 1)
            g.iota(dist[:], pattern=[[1, N]], base=P - N, channel_multiplier=-1,
                   allow_small_or_imprecise_dtypes=True).then_inc(setup_made, 1)
            g.iota(ebase[:], pattern=[[-CAP, NE]], base=SLOTS, channel_multiplier=0,
                   allow_small_or_imprecise_dtypes=True).then_inc(setup_made, 1)
            pool.wait_ge(setup_made, N_MADE - 5)
            g.affine_select(out=ident[:], in_=ident[:], compare_op=ALU.not_equal, fill=1.0, base=0,
                            pattern=[[-1, P]], channel_multiplier=1).then_inc(setup_made, 1)
            g.affine_select(out=tri[:], in_=tri[:], compare_op=ALU.is_gt, fill=0.0, base=0,
                            pattern=[[1, P]], channel_multiplier=-1).then_inc(setup_made, 1)
            g.affine_select(out=dist[:], in_=dist[:], compare_op=ALU.is_ge, fill=MASKED, base=N - P,
                            pattern=[[-1, N]], channel_multiplier=1).then_inc(setup_made, 1)
            blk = blocks[:].rearrange("p (h e) -> p h e", e=D // L1H)
            g.affine_select(out=blk, in_=blk, compare_op=ALU.is_ge, fill=0.0, base=0,
                            pattern=[[-(D // L1H), P // (D // L1H)], [0, D // L1H]],
                            channel_multiplier=1).then_inc(setup_made, 1)
            pool.wait_ge(setup_made, N_MADE - 1)
            g.affine_select(out=blk, in_=blk, compare_op=ALU.is_ge, fill=0.0, base=D // L1H - 1,
                            pattern=[[D // L1H, P // (D // L1H)], [0, D // L1H]],
                            channel_multiplier=-1).then_inc(setup_made, 1)
            pool.sem_inc(slot_ready, 1)

            def normalise(a, n):
                pool.wait_ge(exped, at(a, H * T, (n + 1) * T))
                pool.wait_ge(rsum_ready, at(a, H, n + 1))
                for t in range(T):
                    pr = prob[:, n % 2, P_AT[t]:P_AT[t] + COLS[t]]
                    i = g.tensor_tensor(pr, pr, rsum[:, n, t:t + 1].to_broadcast([P, COLS[t]]), ALU.mult)
                i.then_inc(probs, 1)

            def send_rows(t, k):
                g.indirect_dma_start(out=disp, out_offset=bass.IndirectOffsetOnAxis(ap=slot[:, t, k:k + 1], axis=0),
                                     in_=hn[:, t, :], in_offset=None, bounds_check=SLOTS - 1,
                                     oob_is_err=False).then_inc(dispatched, 16)

            def sent(r):
                pool.wait_ge(dispatched, at(r, 16 * T * TOPK, 16 * T * TOPK))
                pool.sem_inc(rows_sent, 1)

            def slots_wait(r):
                pool.wait_ge(slot_ready, at(r, 1, 1))
                pool.sem_inc(pool_passed, 1)

            for n in range(H):
                normalise((None, 0), n)
            pool.wait_ge(zeros_made, 16 * (SLOTS // P // T + 1))
            SENDERS = H // 2
            with pool.Fori(0, B - 1) as b:
                slots_wait((b, 0))
                for n in range(H):
                    normalise((b, 1), n)
                    if n < SENDERS:
                        for j in range(n * T * TOPK // SENDERS, (n + 1) * T * TOPK // SENDERS):
                            send_rows(j // TOPK, j % TOPK)
                    if n == SENDERS:
                        sent((b, 0))
            for r in range(B - 1, B + 1):
                slots_wait((None, r))
                for j in range(T * TOPK):
                    send_rows(j // TOPK, j % TOPK)
                sent((None, r))

            pool.wait_ge(ebo_free, NE + 2)
            pool.sem_inc(gat_used, 2)
            with pool.Fori(0, B) as b:
                pool.wait_ge(f_gates, b * 32 + 32)
                for t in range(T):
                    pool.wait_ge(gat_used, b * T + t + 1)
                    pool.sem_inc(pool_passed, 1)
                    for k in range(TOPK):
                        g.indirect_dma_start(
                            out=gat[:, t % 2, k], out_offset=None, in_=eout,
                            in_offset=bass.IndirectOffsetOnAxis(ap=slot[:, t, k:k + 1], axis=0),
                            bounds_check=SLOTS, oob_is_err=False).then_inc(gathered[t % 2], 16)

        @block.scalar
        def _(act):
            a = nc.scalar
            def a_copy(dst, src):
                return a.activation(dst, src, ACT.Copy)

            def q_evac(i, hp):
                act.wait_ge(q_psum, at(i, HP, hp + 1))
                a.activation(qT[:, hp % 2], bank[2][:], ACT.Copy, scale=qscale[:, hp:hp + 1]).then_inc(q_ready, 1)

            def enter(i):
                for c in range(C):
                    act.wait_ge(x_transposed, at(i, C, c + 1))
                    a_copy(xT[:, c], bank[4 + c][:]).then_inc(xT_ready, 1)
                for u in range(2 * T):
                    act.wait_ge(v_psum, at(i, 2 * T, u + 1))
                    a_copy(v_s[:, u // 2, (u % 2) * 512:(u % 2 + 1) * 512], bank[2 + u % 2][:]).then_inc(v_ready, 1)
                q_evac(i, 0)

            def exps(i, hp):
                if hp + 1 < HP:
                    q_evac(i, hp + 1)
                for n in (2 * hp, 2 * hp + 1):
                    act.wait_ge(max_ready, at(i, H, n + 1))
                    for t in (3, 2, 0, 1):
                        at_t = slice(P_AT[t], P_AT[t] + COLS[t])
                        a.activation(prob[:, n % 2, at_t], biased_s[:, n % 2, at_t], ACT.Exp, bias=negmax[:, n, t:t + 1],
                                     scale=slope(n), accum_out=psumm[:, n, t:t + 1]).then_inc(exped, 1)

            def probs_out(i, hp):
                for s in range(2):
                    for u in range(3):
                        m = (2 * hp + s) * 3 + u
                        act.wait_ge(pT_psum, at(i, 3 * H, m + 1))
                        a_copy(pT[:, s, T_BASE[u]:T_BASE[u] + T_COLS[u]],
                               bank[4 + m % 2][:, 0:T_COLS[u]]).then_inc(pT_ready, 1)

            def xT_evac(p, r, dst):
                for c in range(C):
                    act.wait_ge(transposed, at(p, C * ROUNDS, r * C + c + 1))
                    a_copy(dst[:, c], bank[PA + c][:]).then_inc(xTp_ready, 1)

            def post(p, point):
                if point == 0:
                    xT_evac(p, R_FFN, xTp)
                elif point == 3:
                    xT_evac(p, R_L1, xTp)
                elif point == 4:
                    for c in range(C):
                        act.wait_ge(gram_psum, at(p, C, c + 1))
                        a_copy(gram[:, c, 0:D + 1], bank[PA + c][:, 0:D + 1]).then_inc(gram_ready, 1)
                    act.wait_ge(gram_ready, at(p, C, C))
                    for c in range(C):
                        a.activation(ssum_b[:, c], ones_f[:], ACT.Copy,
                                     scale=gram[:, c, D:D + 1]).then_inc(ssum_ready, 1)
                elif point == 8:
                    act.wait_ge(mix_psum, at(p, 1, 1))
                    a_copy(mix[:].rearrange("p c d -> p (c d)"), bank[PA][:]).then_inc(mix_ready, 1)
                elif point == 10:
                    xT_evac(p, R_L1O, xTp)
                elif point == 13:
                    act.wait_ge(stored, at(p, 1, 1))
                    xT_evac(p, R_MOE, hT)
                elif point == 14:
                    act.wait_ge(lmax_ready, at(p, 1, 1))
                    for t in range(T):
                        a.activation(lexp[:, t], bank[PA][:, t * NE:(t + 1) * NE], ACT.Exp, bias=nlmax[:, t:t + 1],
                                     accum_out=lsum[:, t:t + 1]).then_inc(lexp_ready, 1)

            act.wait_ge(scales_made, H)
            act.wait_ge(setup_made, N_MADE)
            enter((None, 0))
            for hp in range(HP):
                exps((None, 0), hp)
                probs_out((None, 0), hp)
            act.wait_ge(post_loaded, 16 * N_POST)
            for c in range(C):
                a.activation(bq_b[:, c], ones_f[:], ACT.Copy, scale=bq_c[:, c:c + 1]).then_inc(setup_pe, 1)
                a.activation(lnb_b[:, c], ones_f[:], ACT.Copy, scale=lnb_c[:, c:c + 1]).then_inc(setup_pe, 1)
            act.wait_ge(ready, 1)
            with act.Fori(0, B - 1) as b:
                enter((b, 1))
                post((b, 0), 0)
                for hp in range(HP):
                    exps((b, 1), hp)
                    post((b, 0), 2 * hp + 1)
                    probs_out((b, 1), hp)
                    post((b, 0), 2 * hp + 2)
            for point in range(POINTS):
                post((None, B - 1), point)

            def expert(e, s):
                for half in range(2):
                    act.wait_ge(h_psum, 4 * e + 2 * half + 1)
                    a.activation(sil[:, half, 0:3 * CAP], bank[2 * half][:, 0:3 * CAP], ACT.Silu).then_inc(sil_ready, 1)
                act.wait_ge(ebo_psum, e + 1)
                act.wait_ge(ebo_free, e + 1)
                a.activation(ebo[:, s], bank[5][:, 0:D], ACT.Copy).then_inc(ebo_ready, 1)
                a.activation(ebo2[:, s], bank[5][0:CAPR, D:2 * D], ACT.Copy).then_inc(ebo_ready, 1)

            with act.Fori(0, NE // 2) as j:
                for s in range(2):
                    expert(2 * j + s, s)

            with act.Fori(0, B) as b:
                for f in range(FC):
                    act.wait_ge(sh_psum, b * (2 * FC) + 2 * f + 1)
                    if f >= 2:
                        act.wait_ge(sact_ready, b * FC + f - 1)
                    a.activation(sil[:, f % 2], bank[2 * (f % 2)][:], ACT.Silu).then_inc(ssil_ready, 1)

        @block.vector
        def _(dve):
            v = nc.vector
            def fixed():
                dve.sem_inc(passed, 1)

            def moments(did, in_order, src, stats, mv, vare, rstd, newton):
                for t in range(T):
                    did(v.bn_stats(stats[:, t, :], src(t)))
                in_order()
                fixed()
                for t in range(T):
                    did(v.bn_aggr(mv[:, t, :], stats[:, t, :]))
                in_order()
                did(v.tensor_scalar(vare[:], mv[:, :, 1], EPS_LN, None, ALU.add))
                in_order()
                did(v.tensor_scalar(rstd[:].bitcast(U32), vare[:].bitcast(U32), -0.5, RSQRT_GUESS, ALU.mult, ALU.add))
                for _ in range(3):
                    in_order()
                    did(v.tensor_tensor(newton[:], rstd[:], rstd[:], ALU.mult))
                    in_order()
                    did(v.scalar_tensor_tensor(out=newton[:], in0=newton[:], scalar=-0.5, in1=vare[:], op0=ALU.mult,
                                               op1=ALU.mult))
                    in_order()
                    did(v.scalar_tensor_tensor(out=rstd[:], in0=newton[:], scalar=1.5, in1=rstd[:], op0=ALU.add,
                                               op1=ALU.mult))
                in_order()

            def x_norm(i):
                count = [0]

                def did(ins):
                    count[0] += 1
                    return ins.then_inc(att_order, 1)

                def in_order():
                    dve.wait_ge(att_order, at(i, ATT_STEPS, count[0]))

                dve.wait_ge(xs_loaded, at(i, 16, 16))
                moments(did, in_order, lambda t: xs[:, t, :], stats_a, mv_a, vare_a, rstd_a, newton_a)
                for t in range(T):
                    v.tensor_scalar(xa[:, t], xs[:, t, :], mv_a[:, t, 0:1], rstd_a[:, t:t + 1], ALU.subtract,
                                    ALU.mult).then_inc(x_normed, 1)
                dve.wait_ge(x_normed, at(i, T, T))
                dve.sem_inc(xs_used, 1)
                assert count[0] == ATT_STEPS, count[0]

            def k_evac(i, hp):
                dve.wait_ge(k_psum, at(i, HP, hp + 1))
                v.tensor_copy(kpad[0:DH, hp % 2, 0], bank[2][0:DH, :]).then_inc(k_ready, 1)
                v.tensor_copy(kpad[DH:P, hp % 2, 1], bank[2][DH:P, :]).then_inc(k_ready, 1)

            def bias_and_max(i, n):
                for u, unit in enumerate(S_UNITS):
                    dve.wait_ge(scores, at(i, 3 * H, 3 * n + u + 1))
                    fixed()
                    for t, col in unit:
                        v.tensor_tensor_reduce(
                            out=biased_s[:, n % 2, P_AT[t]:P_AT[t] + COLS[t]],
                            in0=bank[(3 * n + u) % 2][:, col:col + COLS[t]], in1=dist[:, N - COLS[t]:N],
                            scale=1.0, scalar=LOWEST, op0=ALU.subtract, op1=ALU.max,
                            accum_out=rawmax[:, n, t:t + 1]).then_inc(biased, 1)
                dve.wait_ge(biased, at(i, H * T, (n + 1) * T))
                v.tensor_scalar(negmax[:, n], rawmax[:, n], -slope(n), None, ALU.mult).then_inc(max_ready, 1)

            def reciprocals(i, n):
                dve.wait_ge(exped, at(i, H * T, (n + 1) * T))
                v.reciprocal(rsum[:, n, :], psumm[:, n, :]).then_inc(rsum_ready, 1)

            def heads(i, hp):
                bias_and_max(i, 2 * hp)
                bias_and_max(i, 2 * hp + 1)
                reciprocals(i, 2 * hp)
                if hp + 1 < HP:
                    k_evac(i, hp + 1)
                reciprocals(i, 2 * hp + 1)

            def o_evac(i, hp):
                dve.wait_ge(oT_psum, at(i, HP, hp + 1))
                v.tensor_copy(oT[:, hp], bank[3][:]).then_inc(oT_ready, 1)

            count = [0]

            def post(p, point):
                def did(ins):
                    count[0] += 1
                    return ins.then_inc(post_order, 1)

                def in_order():
                    dve.wait_ge(post_order, at(p, POST_STEPS, count[0]))

                def norm(dst, src, signal=None):
                    moments(did, in_order, src, stats_p, mv_p, vare_p, rstd_p, newton_p)
                    for t in range(T):
                        ins = v.tensor_scalar(dst(t), src(t), mv_p[:, t, 0:1], rstd_p[:, t:t + 1], ALU.subtract,
                                              ALU.mult)
                        if signal is None:
                            did(ins)
                        else:
                            ins.then_inc(signal, 1)
                    if signal is None:
                        in_order()

                def xn_t(t):
                    return xn[:, t, 0:D]

                def y_t(t):
                    return y[:, t, :]

                def rows(t):
                    return bank[PA + t // 2][:, (t % 2) * D:(t % 2 + 1) * D]

                def whole(x_):
                    return x_[:].rearrange("p t d -> p (t d)")

                def add_bias(j, bias):
                    return did(v.tensor_tensor(y[:, 2 * j:2 * j + 2],
                                               bank[PA + j][:].rearrange("p (t d) -> p t d", d=D),
                                               bias[:].rearrange("p (a d) -> p a d", a=1).to_broadcast([P, 2, D]),
                                               ALU.add))

                def per_tile(x_, n):
                    return x_[:].rearrange("p (t a) -> p t a", a=1).to_broadcast([P, T, n])

                if point == 0:
                    count[0] = 0
                    for j in range(2):
                        dve.wait_ge(wo_psum, at(p, 2, j + 1))
                        add_bias(j, bo_b)
                    in_order()
                    norm(y_t, y_t)
                    dve.wait_ge(x1_loaded, at(p, 16, 16))
                    did(v.tensor_tensor(whole(x1), whole(x1), whole(y), ALU.add))
                    in_order()
                    norm(xn_t, lambda t: x1[:, t, :], normed)
                elif point == 1:
                    dve.wait_ge(rows_psum, at(p, ROWS, 2))
                    norm(y_t, rows)
                elif point == 2:
                    dve.wait_ge(stored, at(p, 1, 1))
                    v.tensor_tensor(whole(x2), whole(x1), whole(y), ALU.add).then_inc(x1_used, 1)
                    dve.wait_ge(x1_used, at(p, 1, 1))
                    norm(xn_t, lambda t: x2[:, t, :], normed)
                elif point in (5, 6):
                    k = point - 5
                    dve.wait_ge(ssum_ready, at(p, C, C))
                    dve.wait_ge(t1_psum, at(p, KS, k + 1))
                    for m in range(C):
                        v.scalar_tensor_tensor(out=t1[:, k, m], in0=bv_b[:, k], scalar=gram[:, m, D:D + 1],
                                               in1=bank[PA][:, m * D:(m + 1) * D], op0=ALU.mult,
                                               op1=ALU.add).then_inc(t1_ready, 1)
                    v.scalar_tensor_tensor(out=u_b[:, k], in0=bv_b[:, k], scalar=float(N), in1=bank[PB][:, 0:D],
                                           op0=ALU.mult, op1=ALU.add).then_inc(t1_ready, 1)
                elif point == 7:
                    dve.wait_ge(t1_ready, at(p, 3 * KS, 3 * KS))
                    dve.wait_ge(state_psum, at(p, KS, KS))
                    for k in range(KS):
                        for c in range(C):
                            did(v.scalar_tensor_tensor(
                                out=st[:, k, c], in0=u_b[:, k, c * P:(c + 1) * P], scalar=bk_c[:, k, c:c + 1],
                                in1=bank[PA][:, (k * C + c) * P:(k * C + c + 1) * P], op0=ALU.mult, op1=ALU.add))
                    in_order()
                    did(v.tensor_tensor(st[:, 0], st[:, 0],
                                        blocks[:].rearrange("p (a e) -> p a e", a=1).to_broadcast([P, C, P]),
                                        ALU.mult))
                    in_order()
                    v.tensor_tensor(sbd[:], st[:, 0], st[:, 1], ALU.mult).then_inc(sbd_ready, 1)
                elif point == 8:
                    dve.wait_ge(mix_psum, at(p, 1, 1))
                    v.tensor_copy(bqs_b[:], bank[PB][:, 0:D]).then_inc(bqs_ready, 1)
                elif point == 9:
                    dve.wait_ge(bqs_ready, at(p, 1, 1))
                    for j in range(2):
                        dve.wait_ge(rows_psum, at(p, ROWS, 3 + j))
                        add_bias(j, bqs_b)
                    in_order()
                    norm(xn_t, y_t, normed)
                elif point == 11:
                    dve.wait_ge(normed, at(p, ROUNDS * T, (R_L1O + 1) * T))
                    for j in range(2):
                        dve.wait_ge(rows_psum, at(p, ROWS, 5 + j))
                        add_bias(j, l1bo_b)
                    in_order()
                    norm(y_t, y_t)
                elif point == 12:
                    v.tensor_tensor(whole(x2), whole(x2), whole(y), ALU.add).then_inc(x3_ready, 1)
                    dve.wait_ge(x3_ready, at(p, 1, 1))
                    dve.wait_ge(rows_sent, at(p, 1, 1))
                    norm(lambda t: hn[:, t, :], lambda t: x2[:, t, :], normed)
                elif point == 14:
                    dve.wait_ge(logits_psum, at(p, 1, 1))
                    did(v.tensor_reduce(nlmax[:], bank[PA][:, 0:T * NE].rearrange("p (t e) -> p t e", e=NE), AX,
                                        ALU.max))
                    in_order()
                    v.tensor_scalar(nlmax[:], nlmax[:], -1.0, None, ALU.mult).then_inc(lmax_ready, 1)
                elif point == 15:
                    dve.wait_ge(lexp_ready, at(p, T, T))
                    did(v.reciprocal(rlsum[:], lsum[:]))
                    in_order()
                    did(v.tensor_tensor(gates[:], lexp[:], per_tile(rlsum, NE), ALU.mult))
                    in_order()
                    fixed()
                    for t in range(T):
                        did(v.max(top8[:, t], gates[:, t]))
                    in_order()
                    fixed()
                    for t in range(T):
                        did(v.match_replace(rest[:, t], top8[:, t], gates[:, t], -1.0))
                    in_order()
                    v.tensor_scalar(sel_b[:], rest[:], -1.0, None, ALU.is_equal).then_inc(sel_ready, 1)
                    did(v.tensor_scalar(sel[:], rest[:], -1.0, None, ALU.is_equal))
                    did(v.tensor_reduce(den[:], top8[:], AX, ALU.add))
                    in_order()
                    did(v.tensor_scalar(den[:], den[:], EPS_F32, None, ALU.max))
                    in_order()
                    did(v.reciprocal(den[:], den[:]))
                    did(v.tensor_tensor(wdense[:], gates[:], sel[:], ALU.mult))
                    in_order()
                    did(v.tensor_tensor(wdense[:], wdense[:], per_tile(den, NE), ALU.mult))
                elif point == 16:
                    dve.wait_ge(rank_psum, at(p, 1, 1))
                    rank = bank[PB][:, 0:T * NE].rearrange("p (t e) -> p t e", e=NE)
                    v.scalar_tensor_tensor(out=valid[:], in0=rank, scalar=float(CAP), in1=sel[:],
                                           op0=ALU.is_lt, op1=ALU.mult).then_inc(ranks_read, 1)
                    v.tensor_tensor(key[:], ebase[:].rearrange("p (a e) -> p a e", a=1).to_broadcast([P, T, NE]), rank,
                                    ALU.subtract).then_inc(ranks_read, 1)
                    did(v.tensor_reduce(cum_add[:], sel[:].rearrange("p t e -> p e t"), AX, ALU.add))
                    dve.wait_ge(ranks_read, at(p, 2, 2))
                    did(v.tensor_tensor(key[:], key[:], valid[:], ALU.mult))
                    in_order()
                    did(v.tensor_tensor(cum[:], cum[:], cum_add[:], ALU.add))
                    in_order()
                    fixed()
                    for t in range(T):
                        v.max(key8[:, t], key[:, t]).then_inc(key8_ready, 1)
                    dve.wait_ge(key8_ready, at(p, T, T))
                    v.tensor_scalar(slot[:], key8[:], -1.0, float(SLOTS), ALU.mult, ALU.add).then_inc(slot_ready, 1)
                    products = y[:].rearrange("p t (k e) -> p (t k) e", e=NE)
                    half = T * TOPK // 2
                    for j in range(T * TOPK):
                        t, k = j // TOPK, j % TOPK
                        if j == half:
                            dve.wait_ge(gate8_ready, at(p, T * TOPK, half))
                            fixed()
                        v.scalar_tensor_tensor(out=products[:, j % half], in0=key[:, t], scalar=key8[:, t, k:k + 1],
                                               in1=wdense[:, t], op0=ALU.is_equal, op1=ALU.mult,
                                               accum_out=gate8[:, j:j + 1]).then_inc(gate8_ready, 1)
                    dve.wait_ge(gate8_ready, at(p, T * TOPK, T * TOPK))
                    fixed()
                    assert count[0] == POST_STEPS, count[0]

            for n in range(H):
                v.memset(qscale[(n % 2) * DH:(n % 2 + 1) * DH, n // 2:n // 2 + 1],
                         float(DH) ** -0.5 / slope(n)).then_inc(scales_made, 1)
            dve.wait_ge(setup_made, N_MADE)
            x_norm((None, 0))
            k_evac((None, 0), 0)
            for hp in range(HP):
                heads((None, 0), hp)
                o_evac((None, 0), hp)

            dve.wait_ge(post_loaded, 16 * N_POST)
            made = [0]

            def setup(ins):
                made[0] += 1
                ins.then_inc(setup_dve, 1)

            for c in range(C):
                setup(v.tensor_tensor(weff[:, c], weff[:, c], disha2[:], ALU.add))
                diag = slice(c * P, (c + 1) * P)
                setup(v.tensor_tensor(a_qT[:, c, diag], a_qT[:, c, diag], ident[:], ALU.add))
                setup(v.tensor_scalar(l1wo_s[:, c], l1wo_raw[:, c], lng_c[:, c:c + 1], None, ALU.mult))
                for k in range(KS):
                    setup(v.tensor_tensor(a_k[:, k, c, diag], a_k[:, k, c, diag], ident[:], ALU.add))
                    setup(v.tensor_tensor(a_v[:, k, c, diag], a_v[:, k, c, diag], ident[:], ALU.add))
            dve.wait_ge(setup_pe, 2 * C + 1)
            setup(v.tensor_tensor(l1bo_b[:], l1bo_b[:], bank[3][:, 0:D], ALU.add))
            dve.wait_ge(setup_dve, made[0])
            dve.wait_ge(zeros_made, 16 * (SLOTS // P // T + 1))
            dve.sem_inc(ready, 1)

            with dve.Fori(0, B - 1) as b:
                x_norm((b, 1))
                post((b, 0), 0)
                k_evac((b, 1), 0)
                for hp in range(HP):
                    heads((b, 1), hp)
                    post((b, 0), 2 * hp + 1)
                    o_evac((b, 1), hp)
                    post((b, 0), 2 * hp + 2)
            for point in range(POINTS):
                post((None, B - 1), point)

            with dve.Fori(0, NE // 2) as j:
                for s in range(2):
                    e = 2 * j + s
                    dve.wait_ge(xb_psum, e + 1)
                    v.tensor_copy(xbT.rearrange("p c n -> p (c n)"), bank[6][:, 0:C * CAP]).then_inc(xbT_ready, 1)
                    for half in range(2):
                        dve.wait_ge(sil_ready, 2 * e + half + 1)
                        dve.wait_ge(h_psum, 4 * e + 2 * half + 2)
                        v.tensor_tensor(act_e[:, 3 * half:3 * half + 3].rearrange("p f n -> p (f n)"),
                                        sil[:, half, 0:3 * CAP], bank[2 * half + 1][:, 0:3 * CAP],
                                        ALU.mult).then_inc(act_ready, 1)
                    dve.wait_ge(eo_psum, e + 1)
                    for c in range(C):
                        v.tensor_copy(eo[:, c], bank[(4, 7)[c]][:, 0:CAP]).then_inc(eo_ready, 1)

            with dve.Fori(0, B) as b:
                count = [0]

                def did(i):
                    count[0] += 1
                    return i.then_inc(f_order, 1)

                def in_order():
                    dve.wait_ge(f_order, b * F_STEPS + count[0])

                for f in range(FC):
                    dve.wait_ge(ssil_ready, b * FC + f + 1)
                    dve.wait_ge(sh_psum, b * (2 * FC) + 2 * f + 2)
                    v.tensor_tensor(act_s[:, f], sil[:, f % 2], bank[2 * (f % 2) + 1][:], ALU.mult).then_inc(sact_ready, 1)
                dve.wait_ge(f_gates, b * 32 + 32)
                for t in range(T):
                    dve.wait_ge(gathered[t % 2], b * (16 * TOPK * T // 2) + 16 * TOPK * (t // 2 + 1))
                    if t % 2 == 0:
                        dve.wait_ge(sout_psum, b * (T // 2) + t // 2 + 1)
                    for k in range(TOPK):
                        before = y[:, t] if k else bank[4 + t // 2][:, (t % 2) * D:(t % 2 + 1) * D]
                        i = v.scalar_tensor_tensor(out=y[:, t], in0=gat[:, t % 2, k],
                                                   scalar=gate8[:, t * TOPK + k:t * TOPK + k + 1], in1=before,
                                                   op0=ALU.mult, op1=ALU.add)
                        if k < TOPK - 1:
                            did(i)
                            in_order()
                    i.then_inc(gat_used, 1)
                dve.wait_ge(gat_used, b * T + (T + 2))
                moments(did, in_order, lambda t: y[:, t], stats_p, mv_p, vare_p, rstd_p, newton_p)
                for t in range(T):
                    did(v.tensor_scalar(y[:, t], y[:, t], mv_p[:, t, 0:1], rstd_p[:, t:t + 1], ALU.subtract, ALU.mult))
                in_order()
                dve.wait_ge(f_x3, b * 16 + 16)
                dve.wait_ge(out_free, b + 1)
                v.tensor_tensor(x2[:].rearrange("p t d -> p (t d)"), x1[:].rearrange("p t d -> p (t d)"),
                                y[:].rearrange("p t d -> p (t d)"), ALU.add).then_inc(f_made, 1)
                assert count[0] == F_STEPS, count[0]

        @block.tensor
        def _(pe):
            mm = nc.tensor.matmul

            def enter(i):
                pe.wait_ge(x_normed, at(i, T, T))
                for c in range(C):
                    for t in range(T):
                        ins = nc.tensor.transpose(bank[4 + c][:, t * P:(t + 1) * P], xa[:, t, c * P:(c + 1) * P],
                                                  ident[:])
                    ins.then_inc(x_transposed, 1)
                pe.wait_ge(xT_ready, at(i, C, C))
                for u in range(2 * T):
                    if u >= 2:
                        pe.wait_ge(v_ready, at(i, 2 * T, u - 1))
                    for c in range(C):
                        ins = mm(bank[2 + u % 2][:], xT[:, c, (u // 2) * P:(u // 2 + 1) * P],
                                 wv_s[:, c, (u % 2) * 512:(u % 2 + 1) * 512], start=(c == 0), stop=(c == C - 1))
                    ins.then_inc(v_psum, 1)
                pe.wait_ge(v_ready, at(i, 2 * T, 2 * T))
                queries(i, 0)
                keys(i, 0)

            def queries(i, hp):
                if hp:
                    pe.wait_ge(k_ready, at(i, 2 * HP, 2 * hp))
                for c in range(C):
                    ins = mm(bank[2][:], wq_s[:, c, hp * P:(hp + 1) * P], xT[:, c], start=(c == 0), stop=(c == C - 1))
                ins.then_inc(q_psum, 1)

            def keys(i, hp):
                pe.wait_ge(q_ready, at(i, HP, hp + 1))
                for c in range(C):
                    ins = mm(bank[2][:], wk_s[:, c, hp * P:(hp + 1) * P], xT[:, c], start=(c == 0), stop=(c == C - 1))
                ins.then_inc(k_psum, 1)

            def head_scores(i, n):
                hp, s = n // 2, n % 2
                for u, unit in enumerate(S_UNITS):
                    m = 3 * n + u
                    if m >= 2:
                        pe.wait_ge(biased, at(i, H * T, ((m - 2) // 3) * T + (1, 3, 4)[(m - 2) % 3]))
                    for t, col in unit:
                        ins = mm(bank[m % 2][:, col:col + COLS[t]], qT[:, hp % 2, t * P:(t + 1) * P],
                                 kpad[:, hp % 2, s, 0:COLS[t]], start=True, stop=True, skip_group_check=True)
                    ins.then_inc(scores, 1)

            def pair_scores(i, hp):
                pe.wait_ge(k_ready, at(i, 2 * HP, 2 * hp + 2))
                head_scores(i, 2 * hp)
                if hp + 1 < HP:
                    queries(i, hp + 1)
                head_scores(i, 2 * hp + 1)
                if hp + 1 < HP:
                    keys(i, hp + 1)

            def pair_values(i, hp):
                for s in range(2):
                    pe.wait_ge(probs, at(i, H, 2 * hp + s + 1))
                    for u, unit in enumerate(T_UNITS):
                        m = (2 * hp + s) * 3 + u
                        if m >= 2:
                            pe.wait_ge(pT_ready, at(i, 3 * H, m - 1))
                        for j, col in unit:
                            for t in range(j, T):
                                ins = nc.tensor.transpose(bank[4 + m % 2][:, col + (t - j) * P:col + (t - j + 1) * P],
                                                          prob[:, s, P_AT[t] + j * P:P_AT[t] + (j + 1) * P], ident[:])
                        ins.then_inc(pT_psum, 1)
                pe.wait_ge(pT_ready, at(i, 3 * H, 6 * hp + 6))
                if hp:
                    pe.wait_ge(oT_ready, at(i, HP, hp))
                for j in range(T):
                    for s in range(2):
                        ins = mm(bank[3][s * DH:(s + 1) * DH, j * P:N],
                                 v_s[:, j, (2 * hp + s) * DH:(2 * hp + s + 1) * DH],
                                 pT[:, s, T_AT[j]:T_AT[j] + N - j * P], start=(j == 0), stop=(j == T - 1),
                                 skip_group_check=True)
                ins.then_inc(oT_psum, 1)

            def rows_out(lhs, rhs, chunks, signal):
                for t in range(T):
                    for c in range(chunks):
                        ins = mm(bank[PA + t // 2][:, (t % 2) * D:(t % 2 + 1) * D], lhs[:, c, t * P:(t + 1) * P],
                                 rhs(c), start=(c == 0), stop=(c == chunks - 1), skip_group_check=True)
                    if t % 2:
                        ins.then_inc(signal, 1)

            def leave(i):
                pe.wait_ge(oT_ready, at(i, HP, HP))
                rows_out(oT, lambda c: wo_s[:, c], HP, wo_psum)

            def transposes(p, r, src):
                pe.wait_ge(normed, at(p, ROUNDS * T, (r + 1) * T))
                for c in range(C):
                    for t in range(T):
                        ins = nc.tensor.transpose(bank[PA + c][:, t * P:(t + 1) * P], src[:, t, c * P:(c + 1) * P],
                                                  ident[:])
                    ins.then_inc(transposed, 1)

            def xT_wait(p, r):
                pe.wait_ge(xTp_ready, at(p, C * ROUNDS, (r + 1) * C))

            def post(p, point):
                if point == 0:
                    transposes(p, R_FFN, xn)
                elif point == 1:
                    xT_wait(p, R_FFN)
                    rows_out(xTp, lambda c: weff[:, c], C, rows_psum)
                elif point == 3:
                    transposes(p, R_L1, xn)
                elif point == 4:
                    xT_wait(p, R_L1)
                    for c in range(C):
                        for t in range(T):
                            ins = mm(bank[PA + c][:, 0:D + 2], xn[:, t, c * P:(c + 1) * P], xn[:, t, 0:D + 2],
                                     start=(t == 0), stop=(t == T - 1))
                        ins.then_inc(gram_psum, 1)
                elif point in (5, 6):
                    k = point - 5
                    if k == 0:
                        pe.wait_ge(ssum_ready, at(p, C, C))
                    else:
                        pe.wait_ge(t1_ready, at(p, 3 * KS, 3))
                    for m in range(C):
                        for c in range(C):
                            mm(bank[PA][:, m * D:(m + 1) * D], gram[:, c, m * P:(m + 1) * P], a_v[:, k, c],
                               start=(c == 0), stop=(c == C - 1), skip_group_check=True)
                    for c in range(C):
                        ins = mm(bank[PB][:, 0:D], ssum_b[:, c], a_v[:, k, c], start=(c == 0), stop=(c == C - 1))
                    ins.then_inc(t1_psum, 1)
                elif point == 7:
                    pe.wait_ge(t1_ready, at(p, 3 * KS, 3 * KS))
                    for k in range(KS):
                        for h in range(C):
                            for m in range(C):
                                ins = mm(bank[PA][:, (k * C + h) * P:(k * C + h + 1) * P],
                                         a_k[:, k, m, h * P:(h + 1) * P], t1[:, k, m, h * P:(h + 1) * P],
                                         start=(m == 0), stop=(m == C - 1), skip_group_check=True)
                        ins.then_inc(state_psum, 1)
                elif point == 8:
                    pe.wait_ge(sbd_ready, at(p, 1, 1))
                    for h in range(C):
                        for c in range(C):
                            mm(bank[PA][:, c * D + h * P:c * D + (h + 1) * P], a_qT[:, h, c * P:(c + 1) * P], sbd[:, h],
                               start=True, stop=True, skip_group_check=True)
                        ins = mm(bank[PB][:, h * P:(h + 1) * P], bq_b[:, h], sbd[:, h], start=True, stop=True,
                                 skip_group_check=True)
                    ins.then_inc(mix_psum, 1)
                elif point == 9:
                    pe.wait_ge(mix_ready, at(p, 1, 1))
                    pe.wait_ge(bqs_ready, at(p, 1, 1))
                    rows_out(xTp, lambda c: mix[:, c], C, rows_psum)
                elif point == 10:
                    transposes(p, R_L1O, xn)
                elif point == 11:
                    xT_wait(p, R_L1O)
                    rows_out(xTp, lambda c: l1wo_s[:, c], C, rows_psum)
                elif point == 13:
                    transposes(p, R_MOE, hn)
                elif point == 14:
                    xT_wait(p, R_MOE)
                    for t in range(T):
                        for c in range(C):
                            ins = mm(bank[PA][:, t * NE:(t + 1) * NE], hT[:, c, t * P:(t + 1) * P], wg_s[:, c],
                                     start=(c == 0), stop=(c == C - 1), skip_group_check=True)
                    ins.then_inc(logits_psum, 1)
                elif point == 16:
                    pe.wait_ge(sel_ready, at(p, 1, 1))
                    for t in range(T):
                        dst = bank[PB][:, t * NE:(t + 1) * NE]
                        mm(dst, ones_b[:], cum[:], start=True, stop=False, skip_group_check=True)
                        for s in range(t):
                            mm(dst, ones_b[:], sel_b[:, s], start=False, stop=False, skip_group_check=True)
                        ins = mm(dst, tri[:], sel_b[:, t], start=False, stop=True, skip_group_check=True)
                    ins.then_inc(rank_psum, 1)

            pe.wait_ge(setup_made, N_MADE)
            pe.wait_ge(att_loaded, 16 * 3)
            enter((None, 0))
            for hp in range(HP):
                pair_scores((None, 0), hp)
                pair_values((None, 0), hp)
            pe.wait_ge(post_loaded, 16 * N_POST)
            leave((None, 0))
            pe.wait_ge(setup_pe, 2 * C)
            for c in range(C):
                ins = mm(bank[3][:, 0:D], lnb_b[:, c], l1wo_raw[:, c], start=(c == 0), stop=(c == C - 1))
            ins.then_inc(setup_pe, 1)
            pe.wait_ge(ready, 1)
            with pe.Fori(0, B - 1) as b:
                enter((b, 1))
                post((b, 0), 0)
                for hp in range(HP):
                    pair_scores((b, 1), hp)
                    post((b, 0), 2 * hp + 1)
                    pair_values((b, 1), hp)
                    post((b, 0), 2 * hp + 2)
                pe.wait_ge(ranks_read, b * 2 + 2)
                leave((b, 1))
            for point in range(POINTS):
                post((None, B - 1), point)

            def rows_in(e, s, j):
                pe.wait_ge(xb_loaded[s], j * 32 + 32)
                for c in range(C):
                    nc.tensor.transpose(bank[6][:, c * CAP:c * CAP + P], xb[:, s, c * P:(c + 1) * P], ident[:])
                    i = nc.tensor.transpose(bank[6][:, c * CAP + P:(c + 1) * CAP], xb2[:, s, c * P:(c + 1) * P],
                                            ident[0:CAPR, 0:CAPR])
                i.then_inc(xb_psum, 1)

            def expert(e, s, j, following):
                w1 = ew_s[:, s, 0:W1C].rearrange("p (c f) -> p c f", c=C)
                w2 = ew_s[:, s, W1C:EWC].rearrange("p (f d) -> p f d", f=FC)
                pe.wait_ge(w_loaded[s], j * 16 + 16)
                pe.wait_ge(xbT_ready, e + 1)
                for half in range(2):
                    for part in (1, 0):
                        for q in range(3):
                            f = part * FC + 3 * half + q
                            for c in range(C):
                                i = mm(bank[2 * half + 1 - part][:, q * CAP:(q + 1) * CAP], w1[:, c, f * P:(f + 1) * P],
                                       xbT[:, c], start=(c == 0), stop=(c == C - 1), skip_group_check=True)
                        i.then_inc(h_psum, 1)
                for half in range(2):
                    pe.wait_ge(act_ready, 2 * e + half + 1)
                    for c in range(C):
                        for f in range(3 * half, 3 * half + 3):
                            i = mm(bank[(4, 7)[c]][:, 0:CAP],
                                   w2[:, f, c * P:(c + 1) * P], act_e[:, f], start=(f == 0), stop=(f == FC - 1),
                                   skip_group_check=True)
                i.then_inc(eo_psum, 1)
                if following is not None:
                    rows_in(*following)
                pe.wait_ge(eo_ready, 2 * e + 2)
                for c in range(C):
                    nc.tensor.transpose(bank[5][:, c * P:(c + 1) * P], eo[:, c, 0:P], ident[:])
                    i = nc.tensor.transpose(bank[5][0:CAPR, D + c * P:D + (c + 1) * P], eo[:, c, P:CAP], ident[:])
                i.then_inc(ebo_psum, 1)

            rows_in(0, 0, 0)
            with pe.Fori(0, NE // 2 - 1) as j:
                expert(2 * j, 0, j, (2 * j + 1, 1, j))
                expert(2 * j + 1, 1, j, (2 * j + 2, 0, j + 1))
            expert(NE - 2, 0, NE // 2 - 1, (NE - 1, 1, NE // 2 - 1))
            expert(NE - 1, 1, NE // 2 - 1, None)

            pe.wait_ge(sw_loaded, 16)
            pe.wait_ge(ebo_ready, 2 * NE)
            w1 = sw_s[:, 0:W1C].rearrange("p (c f) -> p c f", c=C)
            w2 = sw_s[:, W1C:EWC].rearrange("p (f d) -> p f d", f=FC)
            with pe.Fori(0, B) as b:
                pe.wait_ge(f_hT, b * 16 + 16)
                for f in range(FC):
                    if f >= 2:
                        pe.wait_ge(sact_ready, b * FC + f - 1)
                    for part in (1, 0):
                        for c in range(C):
                            i = mm(bank[2 * (f % 2) + 1 - part][:], w1[:, c, (part * FC + f) * P:(part * FC + f + 1) * P],
                                   hT[:, c], start=(c == 0), stop=(c == C - 1))
                        i.then_inc(sh_psum, 1)
                pe.wait_ge(sact_ready, b * FC + FC)
                pe.wait_ge(gat_used, b * T + 2)
                for t in range(T):
                    for f in range(FC):
                        i = mm(bank[4 + t // 2][:, (t % 2) * D:(t % 2 + 1) * D], act_s[:, f, t * P:(t + 1) * P], w2[:, f],
                               start=(f == 0), stop=(f == FC - 1), skip_group_check=True)
                    if t % 2:
                        i.then_inc(sout_psum, 1)


_NAMES = ["x", "wq", "wk", "wv", "wo", "bo", "ffn_w", "ffn_d", "l1_wq", "l1_wqT", "l1_bq", "l1_wk", "l1_bk", "l1_wv",
          "l1_bv", "l1_wo", "l1_bo", "ln_g", "ln_b", "wgT", "sw", "ew"]


def _gated_weights(np, w1, w2):
    lead = w1.shape[:-2]
    a = np.swapaxes(w1, -1, -2).reshape(*lead, C, P, 2 * FFN)
    b = np.swapaxes(w2, -1, -2).reshape(*lead, FC, P, D)
    a = np.swapaxes(a, -3, -2).reshape(*lead, P, W1C)
    b = np.swapaxes(b, -3, -2).reshape(*lead, P, FC * D)
    return np.concatenate([a, b], axis=-1)


def kernel(**inputs):
    import numpy as np
    import concourse.bacc as bacc
    from concourse.bass_utils import run_bass_kernel_spmd

    i = {k: np.asarray(v) for k, v in inputs.items()}
    laid = [i["L0_attn_x"], i["L0_attn_Wq"], i["L0_attn_Wk"], i["L0_attn_Wv"], i["L0_attn_Wo"], i["L0_attn_bo"],
            i["L0_ffn_weight"].T, i["L0_ffn_disha"], i["L1_attn_Wq"], i["L1_attn_Wq"].T, i["L1_attn_bq"],
            i["L1_attn_Wk"], i["L1_attn_bk"], i["L1_attn_Wv"], i["L1_attn_bv"], i["L1_attn_Wo"], i["L1_attn_bo"],
            i["L1_attn_ln_g"], i["L1_attn_ln_b"], i["L1_ffn_wg"].T,
            _gated_weights(np, i["L1_ffn_shared_w1"], i["L1_ffn_shared_w2"]),
            _gated_weights(np, i["L1_ffn_expert_w1"], i["L1_ffn_expert_w2"])]
    nc = bacc.Bacc("TRN2", target_bir_lowering=False, num_devices=1)
    arrays, args = {}, []
    for name, a in zip(_NAMES, laid):
        arrays[name] = np.ascontiguousarray(a)
        args.append(nc.dram_tensor(name, a.shape, mybir.dt.from_np(a.dtype), kind="ExternalInput").ap())
    out = nc.dram_tensor("out", [B, N, D], F32, kind="ExternalOutput").ap()
    bass_sandwich(nc, *args, out)
    r = run_bass_kernel_spmd(nc, [arrays], core_ids=[0])
    return r.results[0]["out"]
```

```python
from contextlib import ExitStack

import concourse.bass as bass
from concourse import mybir
from concourse.alu_op_type import AluOpType as ALU

ACT = mybir.ActivationFunctionType
AX = mybir.AxisListType.X
F32, BF16, U32 = mybir.dt.float32, mybir.dt.bfloat16, mybir.dt.uint32

P = 128
B, N, D = 8, 512, 256
T = N // P
C = D // P
H, DH = 16, 64
HP = H // 2
INNER = H * DH
L1H = 16
L1N = 1024
KS = 2
NE, TOPK, FFN, CAP = 64, 8, 768, 160
FC = FFN // P
CAPR = CAP - P
SLOTS = NE * CAP
ROW = D + NE + 1
EARLY = 4
LATE = B - EARLY
EPS_LN = 1e-5
EPS_F32 = 2.0 ** -23
MASKED = 1e33
LOWEST = -3e38
W1C = 2 * FFN * C
EWC = W1C + FC * D


ATT_STEPS, POST_STEPS, F_STEPS = 19, 179, (23, 25)
RSQRT_GUESS = float(0x5F3759DF)


def slope(h):
    return 1.0 / (2.0 ** (8.0 / H)) ** (h + 1)


def at(i, per, n):
    reg, k = i
    return k * per + n if reg is None else reg * per + (k * per + n)


def index(i):
    reg, k = i
    return k if reg is None else reg + k


def bass_sandwich(nc, x, wq, wk, wv, wo, bo, ffn_w, ffn_d, l1_wq, l1_wqT, l1_bq, l1_wk, l1_bk, l1_wv, l1_bv,
                  l1_wo, l1_bo, ln_g, ln_b, wgT, sw, ew, out):
    disp = nc.dram_tensor("disp", [SLOTS, ROW], F32).ap()
    acc = nc.dram_tensor("acc", [B * N + CAP, D], F32).ap()
    x3_d = nc.dram_tensor("x3_d", [B, P, T * D], F32).ap()
    hT_d = nc.dram_tensor("hT_d", [B, P, C * N], F32).ap()
    x_v = x.rearrange("b (t p) d -> b p t d", p=P)
    acc_v = acc[0:B * N].rearrange("(b t p) d -> b p t d", b=B, p=P)
    out_v = out.rearrange("b (t p) d -> b p t d", p=P)

    ctx = ExitStack()
    with ctx:
        def sb(name, shape, dt=F32):
            return ctx.enter_context(nc.sbuf_tensor(name, shape, dt))

        def sem(name):
            return ctx.enter_context(nc.semaphore(name))

        bank = [ctx.enter_context(nc.psum_tensor(f"bank{i}", [P, 512], F32)) for i in range(8)]

        ident = sb("ident", [P, P])
        dist = sb("dist", [P, N])
        tri = sb("tri", [P, P], BF16)
        ones_b = sb("ones_b", [P, P], BF16)
        ones_f = sb("ones_f", [P, P])
        blocks = sb("blocks", [P, P])
        ebase = sb("ebase", [P, NE])
        big_w = sb("big_w", [P, 2 * EWC])
        wq_s, wk_s, wv_s = (big_w[:, j * C * INNER:(j + 1) * C * INNER].rearrange("p (c f) -> p c f", c=C)
                            for j in range(3))
        wo_s = big_w[:, 3 * C * INNER:3 * C * INNER + HP * D].rearrange("p (h d) -> p h d", h=HP)
        bo_b = sb("bo_b", [P, D])
        weff = sb("weff", [P, C, D])
        disha2 = sb("disha2", [P, D])
        a_qT = sb("a_qT", [P, C, D])
        a_k = sb("a_k", [P, KS, C, D])
        a_v = sb("a_v", [P, KS, C, D])
        bq_c = sb("bq_c", [P, C])
        bq_b = sb("bq_b", [P, C, P])
        bk_c = sb("bk_c", [P, KS, C])
        bv_b = sb("bv_b", [P, KS, D])
        lng_c = sb("lng_c", [P, C])
        lnb_c = sb("lnb_c", [P, C])
        lnb_b = sb("lnb_b", [P, C, P])
        l1wo_raw = sb("l1wo_raw", [P, C, D])
        l1wo_s = sb("l1wo_s", [P, C, D])
        l1bo_b = sb("l1bo_b", [P, D])
        wg_s = sb("wg_s", [P, C, NE])

        xs = sb("xs", [P, T, D])
        xa = sb("xa", [P, T, D])
        xT = sb("xT", [P, C, N])
        xn = sb("xn", [P, T, D + 4])
        xTp = sb("xTp", [P, C, N])
        v_s = sb("v_s", [P, T, INNER])
        qT = sb("qT", [P, 2, N])
        kpad = sb("kpad", [P, 2, 2, N])
        qscale = sb("qscale", [P, HP])
        prob = sb("prob", [P, 2 * 2, 10 * P])
        rawmax = sb("rawmax", [P, H, T])
        negmax = sb("negmax", [P, H, T])
        psumm = sb("psumm", [P, H, T])
        rsum = sb("rsum", [P, H, T])
        pT = sb("pT", [P, 2, 10 * P])
        oT = sb("oT", [P, HP, N])
        y = sb("y", [P, T, D])
        x1 = sb("x1", [P, T, D])
        x2 = sb("x2", [P, T, D])
        stats_a, stats_p = (sb(f"stats{i}", [P, T, 6]) for i in range(2))
        mv_a, mv_p = (sb(f"mv{i}", [P, T, 2]) for i in range(2))
        vare_a, vare_p = (sb(f"vare{i}", [P, T]) for i in range(2))
        rstd_a, rstd_p = (sb(f"rstd{i}", [P, T]) for i in range(2))
        newton_a, newton_p = (sb(f"newton{i}", [P, T]) for i in range(2))
        gram = sb("gram", [P, C, D + 4])
        ssum_b = sb("ssum_b", [P, C, P])
        t1 = sb("t1", [P, KS, C, D])
        u_b = sb("u_b", [P, KS, D])
        st = sb("st", [P, KS, C, P])
        sbd = sb("sbd", [P, C, P])
        mix = sb("mix", [P, C, D])
        bqs_b = sb("bqs_b", [P, D])
        hT = sb("hT", [P, C, N])
        nlmax = sb("nlmax", [P, T])
        lsum = sb("lsum", [P, T])
        rlsum = sb("rlsum", [P, T])
        lexp = sb("lexp", [P, T, NE])
        gates = sb("gates", [P, T, NE])
        top8 = sb("top8", [P, T, TOPK])
        rest = sb("rest", [P, T, NE])
        sel = sb("sel", [P, T, NE])
        sel_b = sb("sel_b", [P, T, NE], BF16)
        cum = sb("cum", [P, NE], BF16)
        cum_add = sb("cum_add", [P, NE])
        den = sb("den", [P, T])
        valid = sb("valid", [P, T, NE])
        key = sb("key", [P, T, NE])
        key8 = sb("key8", [P, T, TOPK])
        slot = sb("slot", [P, T, TOPK], U32)
        token = sb("token", [P, T])
        send = sb("send", [P, T, ROW])
        hn, wdense = send[:, :, 0:D], send[:, :, D:D + NE]
        gate_e, gate_e2 = sb("gate_e", [P, 2]), sb("gate_e2", [CAPR, 2])
        token_e, token_e2 = sb("token_e", [P, 2], U32), sb("token_e2", [CAPR, 2], U32)

        ew_s = big_w[:].rearrange("p (s f) -> p s f", s=2)
        pT_f = pT[:].rearrange("p a n -> p (a n)")
        sil = pT_f[:, 0:1024].rearrange("p (s n) -> p s n", s=2)
        act_e = pT_f[:, 1024:1024 + FC * CAP].rearrange("p (f n) -> p f n", f=FC)
        xbT = pT_f[:, 2048:2048 + C * CAP].rearrange("p (c n) -> p c n", c=C)
        eo = gram[:].rearrange("p c d -> p (c d)")[:, 0:C * CAP].rearrange("p (c n) -> p c n", c=C)
        xT_f, xTp_f = (x_[:].rearrange("p c n -> p (c n)") for x_ in (xT, xTp))
        xb = xT_f[:, 0:2 * ROW].rearrange("p (s d) -> p s d", s=2)
        xb2 = xTp_f[0:CAPR, 0:2 * ROW].rearrange("p (s d) -> p s d", s=2)
        ebo = qT[:, 1].rearrange("p (s d) -> p s d", s=2)
        ebo2 = qT[0:CAPR, 0].rearrange("p (s d) -> p s d", s=2)

        def chunks(x_):
            return x_[:].rearrange("p t d -> p (t d)").rearrange("p (c n) -> p c n", c=C)

        sw_s = prob[:].rearrange("p a n -> p (a n)")[:, 0:EWC]
        hT_early = [xT[:], chunks(xa), chunks(xs), oT[:, FC:HP]]
        hT_late = [hT[:], chunks(xa)]
        shared_rows = v_s[:].rearrange("p t f -> p (t f)").rearrange("p (b t d) -> p b t d", b=EARLY, d=D)
        acc_f, x3_f = (shared_rows[:, 0], shared_rows[:, 1]), (x1[:], xs[:])
        out_f = (x2[:], shared_rows[:, 2])
        act_s = oT[:, 0:FC]

        att_loaded, post_loaded, setup_made, zeros_made = (
            sem("att_loaded"), sem("post_loaded"), sem("setup_made"), sem("zeros_made"))
        ident_made, scales_made, setup_dve, setup_pe, ready = (
            sem("ident_made"), sem("scales_made"), sem("setup_dve"), sem("setup_pe"), sem("ready"))
        xs_loaded, xs_used, x1_loaded, x1_used = sem("xs_loaded"), sem("xs_used"), sem("x1_loaded"), sem("x1_used")
        att_order, x_normed, x_transposed, xT_ready = (
            sem("att_order"), sem("x_normed"), sem("x_transposed"), sem("xT_ready"))
        v_psum, v_ready = sem("v_psum"), sem("v_ready")
        q_psum, q_ready, k_psum, k_ready = sem("q_psum"), sem("q_ready"), sem("k_psum"), sem("k_ready")
        scores, biased, max_ready, exped = sem("scores"), sem("biased"), sem("max_ready"), sem("exped")
        rsum_ready, probs = sem("rsum_ready"), sem("probs")
        pT_psum, pT_ready, oT_psum, oT_ready = sem("pT_psum"), sem("pT_ready"), sem("oT_psum"), sem("oT_ready")
        wo_psum = sem("wo_psum")
        post_order, normed, transposed, xTp_ready, rows_psum = (
            sem("post_order"), sem("normed"), sem("transposed"), sem("xTp_ready"), sem("rows_psum"))
        gram_psum, gram_ready, ssum_ready = sem("gram_psum"), sem("gram_ready"), sem("ssum_ready")
        t1_psum, t1_ready, state_psum, sbd_ready = sem("t1_psum"), sem("t1_ready"), sem("state_psum"), sem("sbd_ready")
        mix_psum, mix_ready, bqs_ready = sem("mix_psum"), sem("mix_ready"), sem("bqs_ready")
        x3_ready, batch_stores, stored = sem("x3_ready"), sem("batch_stores"), sem("stored")
        logits_psum, lmax_ready, lexp_ready = sem("logits_psum"), sem("lmax_ready"), sem("lexp_ready")
        sel_ready, rank_psum, ranks_read, key8_ready, slot_ready = (
            sem("sel_ready"), sem("rank_psum"), sem("ranks_read"), sem("key8_ready"), sem("slot_ready"))
        dispatched, rows_sent = sem("dispatched"), sem("rows_sent")
        w1_loaded, w2_loaded = ([sem(f"{x_}{i}") for i in range(2)] for x_ in ("w1_loaded", "w2_loaded"))
        xb_loaded = [sem(f"xb_loaded{i}") for i in range(2)]
        xb_psum, xbT_ready, h_psum, sil_ready, act_ready = (
            sem("xb_psum"), sem("xbT_ready"), sem("h_psum"), sem("sil_ready"), sem("act_ready"))
        eo_psum, eo_ready, ebo_psum, tags_ready, ebo_ready, added, ebo_free = (
            sem("eo_psum"), sem("eo_ready"), sem("ebo_psum"), sem("tags_ready"), sem("ebo_ready"), sem("added"),
            sem("ebo_free"))
        sw_loaded = sem("sw_loaded")
        early_loaded, early_ready, early_stored = (
            [sem(f"early_loaded{i}") for i in range(EARLY)], sem("early_ready"), sem("early_stored"))
        late_loaded = [sem(f"late_loaded{i}") for i in range(2)]
        sh_psum, ssil_ready, sact_ready, sout_psum, sout_free = (
            sem("sh_psum"), sem("ssil_ready"), sem("sact_ready"), sem("sout_psum"), sem("sout_free"))
        sums_loaded, f_order, f_made, out_stored, out_free = (
            [sem(f"{x_}{i}") for i in ("_early", "_late")]
            for x_ in ("sums_loaded", "f_order", "f_made", "out_stored", "out_free"))

        passed, pool_passed = sem("passed"), sem("pool_passed")

        ROUNDS = 4
        R_FFN, R_L1, R_L1O, R_MOE = range(ROUNDS)
        ROWS = 6
        POINTS = 2 * HP + 2
        PA, PB = 6, 7
        V_BANKS = 3, 4
        S_BANKS = 0, 1, 3
        T_BANKS = 4, 5, 2
        V_FIRST = 6
        BEHIND = 3, 15
        steps = [(i, f) for i in range(EARLY) for f in range(FC + 1)]
        taken = [2, 2, 3, 1, 1, 1, 1, 1, 1, 2, 1, 2, 0, 1, 1, 0, 0]
        taken.append(len(steps) - sum(taken))
        UNITS = [steps[sum(taken[:n]):sum(taken[:n + 1])] for n in range(POINTS)]
        COLS = [(t + 1) * P for t in range(T)]
        S_UNITS = [[(3, 0)], [(2, 0), (0, 3 * P)], [(1, 0)]]
        P_AT = {3: 0, 2: 512, 0: 896, 1: 1024}
        T_UNITS = [[(0, 0)], [(1, 0), (3, 384)], [(2, 0)]]
        T_AT = {0: 0, 1: 512, 3: 896, 2: 1024}
        T_BASE = [0, 512, 1024]
        T_COLS = [512, 512, 256]

        block = ctx.enter_context(nc.Block())

        N_POST = 12 + 4 * KS
        N_ZEROS = 2 + LATE + 2
        N_MADE = 18

        @block.sync
        def _(sp):
            col = "(c p) f -> p c f"
            sp.dma_start(xs[:], x_v[0]).then_inc(xs_loaded, 16)
            for dst, src in ((wv_s, wv), (wq_s, wq), (wk_s, wk)):
                sp.dma_start(dst, src.rearrange(col, p=P)).then_inc(att_loaded, 16)
            sp.dma_start(x1[:], x_v[0]).then_inc(x1_loaded, 16)
            loads = [(wo_s, wo.rearrange(col, p=P)),
                     (weff[:], ffn_w.rearrange(col, p=P)), (a_qT[:], l1_wqT.rearrange(col, p=P)),
                     (l1wo_raw[:], l1_wo.rearrange(col, p=P)), (wg_s[:], wgT.rearrange(col, p=P)),
                     (disha2[0:64, :], ffn_d), (disha2[64:128, :], ffn_d),
                     (bo_b[:], bo.partition_broadcast(P)), (l1bo_b[:], l1_bo.partition_broadcast(P))]
            for k in range(KS):
                loads += [(a_k[:, k], l1_wk[k].rearrange(col, p=P)), (a_v[:, k], l1_wv[k].rearrange(col, p=P)),
                          (bv_b[:, k], l1_bv[k].partition_broadcast(P))]
            for dst, src in loads:
                sp.dma_start(dst, src).then_inc(post_loaded, 16)
            with nc.allow_non_contiguous_dma(reason="short bias columns"):
                for dst, src in ((bq_c, l1_bq), (lng_c, ln_g), (lnb_c, ln_b)):
                    sp.dma_start(dst[:], src.rearrange("(c p) -> p c", p=P)).then_inc(post_loaded, 16)
                for k in range(KS):
                    sp.dma_start(bk_c[:, k], l1_bk[k].rearrange("(c p) -> p c", p=P)).then_inc(post_loaded, 16)
            sp.wait_ge(setup_made, N_MADE)
            slots_v = disp.rearrange("(e c) w -> c e w", c=CAP)
            for rows, t in ((slots_v[0:P], 0), (slots_v[P:CAP], 1)):
                n = rows.shape[0]
                src = send[0:n, t:t + 1, :].to_broadcast([n, NE, ROW])
                sp.dma_start(rows, src).then_inc(zeros_made, 16)
            for b in range(EARLY, B):
                sp.dma_start(acc_v[b], y[:]).then_inc(zeros_made, 16)
            for rows in (acc[B * N:B * N + P], acc[B * N + P:]):
                sp.dma_start(rows, y[0:rows.shape[0], 0, :]).then_inc(zeros_made, 16)
            sp.sem_inc(stored, 1)

            def load_xs(a):
                sp.wait_ge(xs_used, at(a, 1, 0))
                sp.dma_start(xs[:], x_v[index(a)]).then_inc(xs_loaded, 16)

            def batch_out(p):
                sp.wait_ge(x3_ready, at(p, 1, 1))
                sp.dma_start(x3_d[index(p)], x2[:].rearrange("p t d -> p (t d)")).then_inc(batch_stores, 16)
                sp.wait_ge(xTp_ready, at(p, C * ROUNDS, C * ROUNDS))
                sp.dma_start(hT_d[index(p)], hT[:].rearrange("p c n -> p (c n)")).then_inc(batch_stores, 16)
                sp.wait_ge(batch_stores, at(p, 32, 32))
                sp.sem_inc(stored, 1)

            def iteration(a, p, following):
                sp.wait_ge(x1_used, at(p, 1, 1))
                sp.dma_start(x1[:], x_v[index(a)]).then_inc(x1_loaded, 16)
                if following is not None:
                    load_xs(following)
                batch_out(p)

            load_xs((None, 1))
            with sp.Fori(0, B - 2) as b:
                iteration((b, 1), (b, 0), (b, 2))
            iteration((None, B - 1), (None, B - 2), None)
            def load_early(n):
                sp.dma_start(hT_early[n], hT_d[n].rearrange("p (c n) -> p c n", c=C)).then_inc(early_loaded[n], 16)

            def load_w1(e, s):
                sp.dma_start(ew_s[:, s, 0:W1C], ew[e][:, 0:W1C]).then_inc(w1_loaded[s], 16)

            def load_w2(e, s):
                sp.dma_start(ew_s[:, s, W1C:EWC], ew[e][:, W1C:EWC]).then_inc(w2_loaded[s], 16)

            sp.wait_ge(k_psum, HP * B)
            load_early(0)
            sp.wait_ge(x_transposed, C * B)
            load_early(1)
            sp.wait_ge(xs_used, B)
            load_early(2)
            sp.wait_ge(pT_psum, 3 * H * B)
            sp.dma_start(sw_s, sw).then_inc(sw_loaded, 16)
            sp.wait_ge(wo_psum, 2 * B)
            load_early(3)
            for e in range(2):
                load_w1(e, e)
                load_w2(e, e)
            for i in range(EARLY):
                sp.wait_ge(early_ready, 2 * i + 2)
                sp.dma_start(acc_v[i], shared_rows[:, i]).then_inc(early_stored, 16)
            batch_out((None, B - 1))

            def load_rows(e, s):
                sp.dma_start(xb[:, s], disp_e[e][0:P]).then_inc(xb_loaded[s], 16)
                sp.dma_start(xb2[:, s], disp_e[e][P:CAP]).then_inc(xb_loaded[s], 16)

            disp_e = disp.rearrange("(e c) d -> e c d", c=CAP)
            sp.wait_ge(rows_sent, B + 1)
            for e in range(2):
                load_rows(e, e)

            def load_late(n, s):
                r_, k = n
                sp.dma_start(hT_late[s], hT_d[index((r_, k + EARLY))].rearrange("p (c n) -> p c n", c=C)
                             ).then_inc(late_loaded[s], 16)

            for s in range(2):
                load_late((None, s), s)
            with sp.Fori(0, NE // 2 - 1) as j:
                for s in range(2):
                    sp.wait_ge(tags_ready, at((2 * j, s), 4, 4))
                    load_rows(2 * j + (s + 2), s)
                    sp.wait_ge(h_psum, at((2 * j, s), 4, 4))
                    load_w1(2 * j + (s + 2), s)
                    sp.wait_ge(eo_psum, at((2 * j, s), 1, 1))
                    load_w2(2 * j + (s + 2), s)

            def load_sums(i, late):
                r_, k = i
                b = index((r_, k + late * EARLY))
                sp.dma_start(acc_f[late], acc_v[b]).then_inc(sums_loaded[late], 16)
                sp.dma_start(x3_f[late], x3_d[b].rearrange("p (t d) -> p t d", d=D)).then_inc(sums_loaded[late], 16)

            def store_out(i, late):
                r_, k = i
                sp.wait_ge(f_made[late], at(i, 1, 1))
                sp.dma_start(out_v[index((r_, k + late * EARLY))], out_f[late]).then_inc(out_stored[late], 16)

            def next_sums(i, late):
                store_out(i, late)
                load_sums((i[0], i[1] + 1), late)
                sp.wait_ge(out_stored[late], at(i, 16, 16))
                sp.sem_inc(out_free[late], 1)

            sp.wait_ge(ebo_free, NE + 2)
            for late in range(2):
                load_sums((None, 0), late)
                sp.sem_inc(out_free[late], 1)
            with sp.Fori(0, LATE // 2 - 1) as j:
                for s in range(2):
                    n = (2 * j, s)
                    sp.wait_ge(sh_psum, at((2 * j, s + EARLY), 2 * FC, 2 * FC))
                    load_late((2 * j, s + 2), s)
                    for late in range(2):
                        next_sums(n, late)
            for late in range(2):
                next_sums((None, LATE - 2), late)
            for late in range(2):
                store_out((None, LATE - 1), late)
            for late in range(2):
                sp.wait_ge(out_stored[late], 16 * LATE)

        @block.gpsimd
        def _(pool):
            g = nc.gpsimd
            g.memset(ident[:], 0.0).then_inc(ident_made, 1)
            pool.wait_ge(ident_made, 1)
            g.affine_select(out=ident[:], in_=ident[:], compare_op=ALU.not_equal, fill=1.0, base=0,
                            pattern=[[-1, P]], channel_multiplier=1).then_inc(ident_made, 1)
            g.memset(ones_b[:], 1.0).then_inc(setup_made, 1)
            g.memset(ones_f[:], 1.0).then_inc(setup_made, 1)
            g.memset(blocks[:], 2.0 ** -20 * (1024.0 / L1N) ** 2).then_inc(setup_made, 1)
            g.memset(tri[:], 1.0).then_inc(setup_made, 1)
            g.memset(cum[:], 0.0).then_inc(setup_made, 1)
            g.memset(kpad[:], 0.0).then_inc(setup_made, 1)
            g.memset(xn[:], 1.0).then_inc(setup_made, 1)
            g.memset(y[:], 0.0).then_inc(setup_made, 1)
            g.memset(send[:], 0.0).then_inc(setup_made, 1)
            g.memset(slot[:], SLOTS).then_inc(setup_made, 1)
            g.iota(dist[:], pattern=[[1, N]], base=P - N, channel_multiplier=-1,
                   allow_small_or_imprecise_dtypes=True).then_inc(setup_made, 1)
            g.iota(ebase[:], pattern=[[-CAP, NE]], base=SLOTS, channel_multiplier=0,
                   allow_small_or_imprecise_dtypes=True).then_inc(setup_made, 1)
            g.iota(token[:], pattern=[[P, T]], base=0, channel_multiplier=1,
                   allow_small_or_imprecise_dtypes=True).then_inc(setup_made, 1)
            pool.wait_ge(setup_made, N_MADE - 5)
            g.iota(send[:, :, D + NE], pattern=[[P, T]], base=B * N, channel_multiplier=1,
                   allow_small_or_imprecise_dtypes=True).then_inc(setup_made, 1)
            g.affine_select(out=tri[:], in_=tri[:], compare_op=ALU.is_gt, fill=0.0, base=0,
                            pattern=[[1, P]], channel_multiplier=-1).then_inc(setup_made, 1)
            g.affine_select(out=dist[:], in_=dist[:], compare_op=ALU.is_ge, fill=MASKED, base=N - P,
                            pattern=[[-1, N]], channel_multiplier=1).then_inc(setup_made, 1)
            blk = blocks[:].rearrange("p (h e) -> p h e", e=D // L1H)
            g.affine_select(out=blk, in_=blk, compare_op=ALU.is_ge, fill=0.0, base=0,
                            pattern=[[-(D // L1H), P // (D // L1H)], [0, D // L1H]],
                            channel_multiplier=1).then_inc(setup_made, 1)
            pool.wait_ge(setup_made, N_MADE - 1)
            g.affine_select(out=blk, in_=blk, compare_op=ALU.is_ge, fill=0.0, base=D // L1H - 1,
                            pattern=[[D // L1H, P // (D // L1H)], [0, D // L1H]],
                            channel_multiplier=-1).then_inc(setup_made, 1)
            pool.sem_inc(slot_ready, 1)

            def normalise(a, n):
                pool.wait_ge(exped, at(a, H * T, (n + 1) * T))
                pool.wait_ge(rsum_ready, at(a, H, n + 1))
                for t in range(T):
                    pr = prob[:, n % 4, P_AT[t]:P_AT[t] + COLS[t]]
                    i = g.tensor_tensor(pr, pr, rsum[:, n, t:t + 1].to_broadcast([P, COLS[t]]), ALU.mult)
                i.then_inc(probs, 1)

            def send_rows(t, k):
                g.indirect_dma_start(out=disp, out_offset=bass.IndirectOffsetOnAxis(ap=slot[:, t, k:k + 1], axis=0),
                                     in_=send[:, t, :], in_offset=None, bounds_check=SLOTS - 1,
                                     oob_is_err=False).then_inc(dispatched, 16)

            def sent(r):
                pool.wait_ge(dispatched, at(r, 16 * T * TOPK, 16 * T * TOPK))
                pool.sem_inc(rows_sent, 1)

            def slots_wait(r):
                pool.wait_ge(slot_ready, at(r, 1, 1))
                pool.sem_inc(pool_passed, 1)

            for n in range(H):
                normalise((None, 0), n)
            pool.wait_ge(zeros_made, 16 * N_ZEROS)
            SENDERS = H // 2
            with pool.Fori(0, B - 1) as b:
                slots_wait((b, 0))
                for n in range(H):
                    normalise((b, 1), n)
                    if n < SENDERS:
                        for j in range(n * T * TOPK // SENDERS, (n + 1) * T * TOPK // SENDERS):
                            send_rows(j // TOPK, j % TOPK)
                    if n == SENDERS:
                        sent((b, 0))
            for r in range(B - 1, B + 1):
                slots_wait((None, r))
                for j in range(T * TOPK):
                    send_rows(j // TOPK, j % TOPK)
                sent((None, r))

            pool.wait_ge(early_stored, 16 * EARLY)
            pool.sem_inc(ebo_free, 2)
            with pool.Fori(0, NE // 2) as j:
                for s in range(2):
                    e = (2 * j, s)
                    pool.wait_ge(ebo_ready, at(e, 2, 2))
                    pool.sem_inc(pool_passed, 1)
                    for src, idx in ((ebo[:, s], token_e), (ebo2[:, s], token_e2)):
                        g.indirect_dma_start(out=acc, out_offset=bass.IndirectOffsetOnAxis(ap=idx[:, s:s + 1], axis=0),
                                             in_=src, in_offset=None, bounds_check=B * N + CAP - 1,
                                             compute_op=ALU.add).then_inc(added, 16)
                    pool.wait_ge(added, at(e, 32, 32))
                    pool.sem_inc(ebo_free, 1)

        @block.scalar
        def _(act):
            a = nc.scalar
            def a_copy(dst, src):
                return a.activation(dst, src, ACT.Copy)

            def q_evac(i, hp):
                act.wait_ge(q_psum, at(i, HP, hp + 1))
                a.activation(qT[:, hp % 2], bank[2][:], ACT.Copy, scale=qscale[:, hp:hp + 1]).then_inc(q_ready, 1)

            def enter(i):
                for c in range(C):
                    act.wait_ge(x_transposed, at(i, C, c + 1))
                    a_copy(xT[:, c], bank[4 + c][:]).then_inc(xT_ready, 1)
                q_evac(i, 0)
                v_evac(i, range(V_FIRST))

            def v_evac(i, units):
                for u in units:
                    act.wait_ge(v_psum, at(i, 2 * T, u + 1))
                    a_copy(v_s[:, u // 2, (u % 2) * 512:(u % 2 + 1) * 512],
                           bank[V_BANKS[u % 2]][:]).then_inc(v_ready, 1)

            def exps(i, n):
                if n % 2 == 0 and n + 2 < H:
                    q_evac(i, n // 2 + 1)
                act.wait_ge(max_ready, at(i, H, n + 1))
                for t in (3, 2, 0, 1):
                    at_t = slice(P_AT[t], P_AT[t] + COLS[t])
                    a.activation(prob[:, n % 4, at_t], prob[:, n % 4, at_t], ACT.Exp, bias=negmax[:, n, t:t + 1],
                                 scale=slope(n), accum_out=psumm[:, n, t:t + 1]).then_inc(exped, 1)

            def probs_out(i, n):
                for u in range(3):
                    m = 3 * n + u
                    act.wait_ge(pT_psum, at(i, 3 * H, m + 1))
                    a_copy(pT[:, n % 2, T_BASE[u]:T_BASE[u] + T_COLS[u]],
                           bank[T_BANKS[u]][:, 0:T_COLS[u]]).then_inc(pT_ready, 1)

            def pair(i, hp):
                for s in range(2):
                    if hp + 1 < HP:
                        exps(i, 2 * hp + 2 + s)
                for s in range(2):
                    probs_out(i, 2 * hp + s)

            def o_evac(i, hp):
                act.wait_ge(oT_psum, at(i, HP, hp + 1))
                a_copy(oT[:, hp], bank[3][:]).then_inc(oT_ready, 1)

            def xT_evac(p, r, dst):
                for c in range(C):
                    act.wait_ge(transposed, at(p, C * ROUNDS, r * C + c + 1))
                    a_copy(dst[:, c], bank[PA + c][:]).then_inc(xTp_ready, 1)

            def post(p, point):
                if point == 0:
                    xT_evac(p, R_FFN, xTp)
                elif point == 3:
                    xT_evac(p, R_L1, xTp)
                elif point == 4:
                    for c in range(C):
                        act.wait_ge(gram_psum, at(p, C, c + 1))
                        a_copy(gram[:, c, 0:D + 1], bank[PA + c][:, 0:D + 1]).then_inc(gram_ready, 1)
                    act.wait_ge(gram_ready, at(p, C, C))
                    for c in range(C):
                        a.activation(ssum_b[:, c], ones_f[:], ACT.Copy,
                                     scale=gram[:, c, D:D + 1]).then_inc(ssum_ready, 1)
                elif point == 8:
                    act.wait_ge(mix_psum, at(p, 1, 1))
                    a_copy(mix[:].rearrange("p c d -> p (c d)"), bank[PA][:]).then_inc(mix_ready, 1)
                elif point == 10:
                    xT_evac(p, R_L1O, xTp)
                elif point == 15:
                    act.wait_ge(stored, at(p, 1, 1))
                    xT_evac(p, R_MOE, hT)
                elif point == 16:
                    act.wait_ge(lmax_ready, at(p, 1, 1))
                    for t in range(T):
                        a.activation(lexp[:, t], bank[PB][:, t * NE:(t + 1) * NE], ACT.Exp, bias=nlmax[:, t:t + 1],
                                     accum_out=lsum[:, t:t + 1]).then_inc(lexp_ready, 1)

            act.wait_ge(scales_made, H)
            act.wait_ge(setup_made, N_MADE)
            enter((None, 0))
            for s in range(2):
                exps((None, 0), s)
            v_evac((None, 0), range(V_FIRST, 2 * T))
            for hp in range(HP):
                pair((None, 0), hp)
                o_evac((None, 0), hp)
            act.wait_ge(post_loaded, 16 * N_POST)
            for c in range(C):
                a.activation(bq_b[:, c], ones_f[:], ACT.Copy, scale=bq_c[:, c:c + 1]).then_inc(setup_pe, 1)
                a.activation(lnb_b[:, c], ones_f[:], ACT.Copy, scale=lnb_c[:, c:c + 1]).then_inc(setup_pe, 1)
            act.wait_ge(ready, 1)
            with act.Fori(0, B - 1) as b:
                enter((b, 1))
                for s in range(2):
                    exps((b, 1), s)
                v_evac((b, 1), range(V_FIRST, 2 * T))
                post((b, 0), 0)
                for hp in range(HP):
                    pair((b, 1), hp)
                    post((b, 0), 2 * hp + 1)
                    o_evac((b, 1), hp)
                    post((b, 0), 2 * hp + 2)
            def shared_silu(i, f):
                act.wait_ge(sh_psum, at(i, 2 * FC, 2 * f + 1))
                if f >= 2:
                    act.wait_ge(sact_ready, at(i, FC, f - 1))
                a.activation(sil[:, f % 2], bank[2 * (f % 2)][:], ACT.Silu).then_inc(ssil_ready, 1)

            for point in range(POINTS):
                if point:
                    post((None, B - 1), point)
                for i, f in UNITS[point]:
                    if f < FC:
                        shared_silu((None, i), f)
                    else:
                        for j in range(2):
                            act.wait_ge(sout_psum, 2 * i + j + 1)
                            a_copy(shared_rows[:, i, 2 * j:2 * j + 2].rearrange("p t d -> p (t d)"),
                                   bank[4 + j][:]).then_inc(early_ready, 1)
                if point == 0:
                    post((None, B - 1), point)

            def silu(e, half):
                act.wait_ge(h_psum, at(e, 4, 2 * half + 1))
                a.activation(sil[:, half, 0:3 * CAP], bank[2 * half][:, 0:3 * CAP], ACT.Silu).then_inc(sil_ready, 1)

            def rows_back(e, s):
                act.wait_ge(ebo_psum, at(e, 1, 1))
                act.wait_ge(ebo_free, at(e, 1, 1))
                act.wait_ge(tags_ready, at(e, 4, 4))
                a.activation(ebo[:, s], bank[5][:, 0:D], ACT.Copy, scale=gate_e[:, s:s + 1]).then_inc(ebo_ready, 1)
                a.activation(ebo2[:, s], bank[5][0:CAPR, D:2 * D], ACT.Copy,
                             scale=gate_e2[:, s:s + 1]).then_inc(ebo_ready, 1)

            for half in range(2):
                silu((None, 0), half)
            with act.Fori(0, NE // 2 - 1) as j:
                for s in range(2):
                    silu((2 * j, s + 1), 0)
                    rows_back((2 * j, s), s)
                    silu((2 * j, s + 1), 1)
            silu((None, NE - 1), 0)
            rows_back((None, NE - 2), 0)
            silu((None, NE - 1), 1)
            rows_back((None, NE - 1), 1)

            with act.Fori(0, LATE) as n:
                for f in range(FC):
                    shared_silu((n, EARLY), f)

        @block.vector
        def _(dve):
            v = nc.vector
            def fixed():
                dve.sem_inc(passed, 1)

            def means(did, in_order, src, stats, mv, vare):
                for t in range(T):
                    did(v.bn_stats(stats[:, t, :], src(t)))
                in_order()
                fixed()
                for t in range(T):
                    did(v.bn_aggr(mv[:, t, :], stats[:, t, :]))
                in_order()
                did(v.tensor_scalar(vare[:], mv[:, :, 1], EPS_LN, None, ALU.add))
                in_order()

            def rsqrt(did, in_order, vare, rstd, newton):
                did(v.tensor_scalar(rstd[:].bitcast(U32), vare[:].bitcast(U32), -0.5, RSQRT_GUESS, ALU.mult, ALU.add))
                for _ in range(3):
                    in_order()
                    did(v.tensor_tensor(newton[:], rstd[:], rstd[:], ALU.mult))
                    in_order()
                    did(v.scalar_tensor_tensor(out=newton[:], in0=newton[:], scalar=-0.5, in1=vare[:], op0=ALU.mult,
                                               op1=ALU.mult))
                    in_order()
                    did(v.scalar_tensor_tensor(out=rstd[:], in0=newton[:], scalar=1.5, in1=rstd[:], op0=ALU.add,
                                               op1=ALU.mult))
                in_order()

            def moments(did, in_order, src, stats, mv, vare, rstd, newton):
                means(did, in_order, src, stats, mv, vare)
                rsqrt(did, in_order, vare, rstd, newton)

            def x_norm(i):
                count = [0]

                def did(ins):
                    count[0] += 1
                    return ins.then_inc(att_order, 1)

                def in_order():
                    dve.wait_ge(att_order, at(i, ATT_STEPS, count[0]))

                dve.wait_ge(xs_loaded, at(i, 16, 16))
                moments(did, in_order, lambda t: xs[:, t, :], stats_a, mv_a, vare_a, rstd_a, newton_a)
                for t in range(T):
                    v.tensor_scalar(xa[:, t], xs[:, t, :], mv_a[:, t, 0:1], rstd_a[:, t:t + 1], ALU.subtract,
                                    ALU.mult).then_inc(x_normed, 1)
                dve.wait_ge(x_normed, at(i, T, T))
                dve.sem_inc(xs_used, 1)
                assert count[0] == ATT_STEPS, count[0]

            def k_evac(i, hp):
                dve.wait_ge(k_psum, at(i, HP, hp + 1))
                v.tensor_copy(kpad[0:DH, hp % 2, 0], bank[2][0:DH, :]).then_inc(k_ready, 1)
                v.tensor_copy(kpad[DH:P, hp % 2, 1], bank[2][DH:P, :]).then_inc(k_ready, 1)

            def bias_and_max(i, n):
                if n >= 4:
                    dve.wait_ge(pT_psum, at(i, 3 * H, 3 * (n - 3)))
                for u, unit in enumerate(S_UNITS):
                    dve.wait_ge(scores, at(i, 3 * H, 3 * n + u + 1))
                    fixed()
                    for t, col in unit:
                        v.tensor_tensor_reduce(
                            out=prob[:, n % 4, P_AT[t]:P_AT[t] + COLS[t]],
                            in0=bank[S_BANKS[u]][:, col:col + COLS[t]], in1=dist[:, N - COLS[t]:N],
                            scale=1.0, scalar=LOWEST, op0=ALU.subtract, op1=ALU.max,
                            accum_out=rawmax[:, n, t:t + 1]).then_inc(biased, 1)
                dve.wait_ge(biased, at(i, H * T, (n + 1) * T))
                v.tensor_scalar(negmax[:, n], rawmax[:, n], -slope(n), None, ALU.mult).then_inc(max_ready, 1)

            def reciprocals(i, n):
                dve.wait_ge(exped, at(i, H * T, (n + 1) * T))
                v.reciprocal(rsum[:, n, :], psumm[:, n, :]).then_inc(rsum_ready, 1)

            def heads(i, hp, p=None):
                bias_and_max(i, 2 * hp)
                if p is not None:
                    post(p, 2 * hp - 1.5)
                bias_and_max(i, 2 * hp + 1)
                if hp + 1 < HP:
                    k_evac(i, hp + 1)
                reciprocals(i, 2 * hp)

            count = [0]

            def post(p, point):
                def did(ins):
                    count[0] += 1
                    return ins.then_inc(post_order, 1)

                def in_order():
                    dve.wait_ge(post_order, at(p, POST_STEPS, count[0]))

                def norm(dst, src, signal=None):
                    moments(did, in_order, src, stats_p, mv_p, vare_p, rstd_p, newton_p)
                    scale(dst, src, signal)

                def scale(dst, src, signal=None):
                    for t in range(T):
                        ins = v.tensor_scalar(dst(t), src(t), mv_p[:, t, 0:1], rstd_p[:, t:t + 1], ALU.subtract,
                                              ALU.mult)
                        if signal is None:
                            did(ins)
                        else:
                            ins.then_inc(signal, 1)
                    if signal is None:
                        in_order()

                def xn_t(t):
                    return xn[:, t, 0:D]

                def y_t(t):
                    return y[:, t, :]

                def rows(t):
                    return bank[PA + t // 2][:, (t % 2) * D:(t % 2 + 1) * D]

                def whole(x_):
                    return x_[:].rearrange("p t d -> p (t d)")

                def add_bias(j, bias):
                    return did(v.tensor_tensor(y[:, 2 * j:2 * j + 2],
                                               bank[PA + j][:].rearrange("p (t d) -> p t d", d=D),
                                               bias[:].rearrange("p (a d) -> p a d", a=1).to_broadcast([P, 2, D]),
                                               ALU.add))

                def per_tile(x_, n):
                    return x_[:].rearrange("p (t a) -> p t a", a=1).to_broadcast([P, T, n])

                if point == 0:
                    count[0] = 0
                    for j in range(2):
                        dve.wait_ge(wo_psum, at(p, 2, j + 1))
                        add_bias(j, bo_b)
                    in_order()
                    norm(y_t, y_t)
                    dve.wait_ge(x1_loaded, at(p, 16, 16))
                    did(v.tensor_tensor(whole(x1), whole(x1), whole(y), ALU.add))
                    in_order()
                    norm(xn_t, lambda t: x1[:, t, :], normed)
                elif point == 1:
                    dve.wait_ge(rows_psum, at(p, ROWS, 2))
                    norm(y_t, rows)
                elif point == 2:
                    dve.wait_ge(stored, at(p, 1, 1))
                    v.tensor_tensor(whole(x2), whole(x1), whole(y), ALU.add).then_inc(x1_used, 1)
                elif point == 2.5:
                    dve.wait_ge(x1_used, at(p, 1, 1))
                    means(did, in_order, lambda t: x2[:, t, :], stats_p, mv_p, vare_p)
                elif point == 3:
                    rsqrt(did, in_order, vare_p, rstd_p, newton_p)
                    scale(xn_t, lambda t: x2[:, t, :], normed)
                elif point in (5, 6):
                    k = point - 5
                    dve.wait_ge(ssum_ready, at(p, C, C))
                    dve.wait_ge(t1_psum, at(p, KS, k + 1))
                    for m in range(C):
                        v.scalar_tensor_tensor(out=t1[:, k, m], in0=bv_b[:, k], scalar=gram[:, m, D:D + 1],
                                               in1=bank[PA][:, m * D:(m + 1) * D], op0=ALU.mult,
                                               op1=ALU.add).then_inc(t1_ready, 1)
                    v.scalar_tensor_tensor(out=u_b[:, k], in0=bv_b[:, k], scalar=float(N), in1=bank[PB][:, 0:D],
                                           op0=ALU.mult, op1=ALU.add).then_inc(t1_ready, 1)
                elif point == 7:
                    dve.wait_ge(t1_ready, at(p, 3 * KS, 3 * KS))
                    dve.wait_ge(state_psum, at(p, KS, KS))
                    for k in range(KS):
                        for c in range(C):
                            did(v.scalar_tensor_tensor(
                                out=st[:, k, c], in0=u_b[:, k, c * P:(c + 1) * P], scalar=bk_c[:, k, c:c + 1],
                                in1=bank[PA][:, (k * C + c) * P:(k * C + c + 1) * P], op0=ALU.mult, op1=ALU.add))
                    in_order()
                    did(v.tensor_tensor(st[:, 0], st[:, 0],
                                        blocks[:].rearrange("p (a e) -> p a e", a=1).to_broadcast([P, C, P]),
                                        ALU.mult))
                    in_order()
                    v.tensor_tensor(sbd[:], st[:, 0], st[:, 1], ALU.mult).then_inc(sbd_ready, 1)
                elif point == 8:
                    dve.wait_ge(mix_psum, at(p, 1, 1))
                    v.tensor_copy(bqs_b[:], bank[PB][:, 0:D]).then_inc(bqs_ready, 1)
                elif point == 9:
                    dve.wait_ge(bqs_ready, at(p, 1, 1))
                    for j in range(2):
                        dve.wait_ge(rows_psum, at(p, ROWS, 3 + j))
                        add_bias(j, bqs_b)
                    in_order()
                    norm(xn_t, y_t, normed)
                elif point == 11:
                    dve.wait_ge(normed, at(p, ROUNDS * T, (R_L1O + 1) * T))
                    for j in range(2):
                        dve.wait_ge(rows_psum, at(p, ROWS, 5 + j))
                        add_bias(j, l1bo_b)
                    in_order()
                    norm(y_t, y_t)
                elif point == 13:
                    v.tensor_tensor(whole(x2), whole(x2), whole(y), ALU.add).then_inc(x3_ready, 1)
                    dve.wait_ge(x3_ready, at(p, 1, 1))
                    means(did, in_order, lambda t: x2[:, t, :], stats_p, mv_p, vare_p)
                elif point == 14:
                    rsqrt(did, in_order, vare_p, rstd_p, newton_p)
                    dve.wait_ge(rows_sent, at(p, 1, 1))
                    scale(lambda t: hn[:, t], lambda t: x2[:, t, :], normed)
                elif point == 16:
                    dve.wait_ge(logits_psum, at(p, 1, 1))
                    did(v.tensor_reduce(nlmax[:], bank[PB][:, 0:T * NE].rearrange("p (t e) -> p t e", e=NE), AX,
                                        ALU.max))
                    in_order()
                    v.tensor_scalar(nlmax[:], nlmax[:], -1.0, None, ALU.mult).then_inc(lmax_ready, 1)
                    dve.wait_ge(lexp_ready, at(p, T, T))
                    did(v.reciprocal(rlsum[:], lsum[:]))
                    in_order()
                    did(v.tensor_tensor(gates[:], lexp[:], per_tile(rlsum, NE), ALU.mult))
                    in_order()
                    fixed()
                    for t in range(T):
                        did(v.max(top8[:, t], gates[:, t]))
                    in_order()
                    fixed()
                    for t in range(T):
                        did(v.match_replace(rest[:, t], top8[:, t], gates[:, t], -1.0))
                    in_order()
                    v.tensor_scalar(sel_b[:], rest[:], -1.0, None, ALU.is_equal).then_inc(sel_ready, 1)
                    did(v.tensor_scalar(sel[:], rest[:], -1.0, None, ALU.is_equal))
                    did(v.tensor_reduce(den[:], top8[:], AX, ALU.add))
                    in_order()
                    did(v.tensor_scalar(den[:], den[:], EPS_F32, None, ALU.max))
                    in_order()
                    did(v.reciprocal(den[:], den[:]))
                    did(v.tensor_tensor(wdense, gates[:], sel[:], ALU.mult))
                    did(v.tensor_copy(send[:, :, D + NE], token[:]))
                    in_order()
                    did(v.tensor_tensor(wdense, wdense, per_tile(den, NE), ALU.mult))
                    did(v.tensor_scalar(token[:], token[:], float(N), None, ALU.add))
                elif point == 17:
                    dve.wait_ge(rank_psum, at(p, 1, 1))
                    rank = bank[PB][:, T * NE:2 * T * NE].rearrange("p (t e) -> p t e", e=NE)
                    v.scalar_tensor_tensor(out=valid[:], in0=rank, scalar=float(CAP), in1=sel[:],
                                           op0=ALU.is_lt, op1=ALU.mult).then_inc(ranks_read, 1)
                    v.tensor_tensor(key[:], ebase[:].rearrange("p (a e) -> p a e", a=1).to_broadcast([P, T, NE]), rank,
                                    ALU.subtract).then_inc(ranks_read, 1)
                    did(v.tensor_reduce(cum_add[:], sel[:].rearrange("p t e -> p e t"), AX, ALU.add))
                    dve.wait_ge(ranks_read, at(p, 2, 2))
                    did(v.tensor_tensor(key[:], key[:], valid[:], ALU.mult))
                    in_order()
                    did(v.tensor_tensor(cum[:], cum[:], cum_add[:], ALU.add))
                    in_order()
                    fixed()
                    for t in range(T):
                        v.max(key8[:, t], key[:, t]).then_inc(key8_ready, 1)
                    dve.wait_ge(key8_ready, at(p, T, T))
                    v.tensor_scalar(slot[:], key8[:], -1.0, float(SLOTS), ALU.mult, ALU.add).then_inc(slot_ready, 1)
                    assert count[0] == POST_STEPS, count[0]

            for n in range(H):
                v.memset(qscale[(n % 2) * DH:(n % 2 + 1) * DH, n // 2:n // 2 + 1],
                         float(DH) ** -0.5 / slope(n)).then_inc(scales_made, 1)
            x_norm((None, 0))
            dve.wait_ge(setup_made, N_MADE)
            k_evac((None, 0), 0)
            heads((None, 0), 0)
            reciprocals((None, 0), 1)
            for hp in range(HP):
                if hp + 1 < HP:
                    heads((None, 0), hp + 1)
                    reciprocals((None, 0), 2 * hp + 3)

            dve.wait_ge(post_loaded, 16 * N_POST)
            made = [0]

            def setup(ins):
                made[0] += 1
                ins.then_inc(setup_dve, 1)

            for c in range(C):
                setup(v.tensor_tensor(weff[:, c], weff[:, c], disha2[:], ALU.add))
                diag = slice(c * P, (c + 1) * P)
                setup(v.tensor_tensor(a_qT[:, c, diag], a_qT[:, c, diag], ident[:], ALU.add))
                setup(v.tensor_scalar(l1wo_s[:, c], l1wo_raw[:, c], lng_c[:, c:c + 1], None, ALU.mult))
                for k in range(KS):
                    setup(v.tensor_tensor(a_k[:, k, c, diag], a_k[:, k, c, diag], ident[:], ALU.add))
                    setup(v.tensor_tensor(a_v[:, k, c, diag], a_v[:, k, c, diag], ident[:], ALU.add))
            dve.wait_ge(setup_pe, 2 * C + 1)
            setup(v.tensor_tensor(l1bo_b[:], l1bo_b[:], bank[3][:, 0:D], ALU.add))
            dve.wait_ge(setup_dve, made[0])
            dve.wait_ge(zeros_made, 16 * N_ZEROS)
            dve.sem_inc(ready, 1)

            with dve.Fori(0, B - 1) as b:
                x_norm((b, 1))
                post((b, 0), 0)
                k_evac((b, 1), 0)
                heads((b, 1), 0)
                reciprocals((b, 1), 1)
                for hp in range(HP):
                    if hp + 1 < HP:
                        heads((b, 1), hp + 1, (b, 0))
                    post((b, 0), 2 * hp + 1)
                    if hp + 1 < HP:
                        reciprocals((b, 1), 2 * hp + 3)
                    post((b, 0), 2 * hp + 2)
                post((b, 0), POINTS - 1)
            def gate(i, f):
                dve.wait_ge(ssil_ready, at(i, FC, f + 1))
                dve.wait_ge(sh_psum, at(i, 2 * FC, 2 * f + 2))
                v.tensor_tensor(act_s[:, f], sil[:, f % 2], bank[2 * (f % 2) + 1][:], ALU.mult).then_inc(sact_ready, 1)

            for point in range(POINTS):
                post((None, B - 1), point)
                post((None, B - 1), point + 0.5)
                for i, f in UNITS[point]:
                    if f < FC:
                        gate((None, i), f)

            def rows_in(e):
                dve.wait_ge(xb_psum, at(e, 1, 1))
                v.tensor_copy(xbT.rearrange("p c n -> p (c n)"), bank[6][:, 0:C * CAP]).then_inc(xbT_ready, 1)

            def tags(e, s):
                dve.wait_ge(ebo_free, at(e, 1, 1))
                for dst, src in ((token_e, xb), (token_e2, xb2)):
                    v.tensor_copy(dst[:, s:s + 1], src[:, s, D + NE:ROW]).then_inc(tags_ready, 1)
                for dst, src in ((gate_e, xb), (gate_e2, xb2)):
                    v.tensor_copy(dst[:, s:s + 1], src[:, s, bass.ds(index((e[0], e[1] + D)), 1)]
                                  ).then_inc(tags_ready, 1)

            def expert(e, s, last=False):
                for half in range(2):
                    dve.wait_ge(sil_ready, at(e, 2, half + 1))
                    dve.wait_ge(h_psum, at(e, 4, 2 * half + 2))
                    v.tensor_tensor(act_e[:, 3 * half:3 * half + 3].rearrange("p f n -> p (f n)"),
                                    sil[:, half, 0:3 * CAP], bank[2 * half + 1][:, 0:3 * CAP],
                                    ALU.mult).then_inc(act_ready, 1)
                if not last:
                    rows_in((e[0], e[1] + 1))
                dve.wait_ge(eo_psum, at(e, 1, 1))
                for c in range(C):
                    v.tensor_copy(eo[:, c], bank[(4, 7)[c]][:, 0:CAP]).then_inc(eo_ready, 1)
                if not last:
                    tags((e[0], e[1] + 1), 1 - s)

            rows_in((None, 0))
            tags((None, 0), 0)
            with dve.Fori(0, NE // 2 - 1) as j:
                for s in range(2):
                    expert((2 * j, s), s)
            expert((None, NE - 2), 0)
            expert((None, NE - 1), 1, last=True)

            f_count = [0, 0]

            def finish(i, late, part, s=0):
                def did(ins):
                    f_count[late] += 1
                    return ins.then_inc(f_order[late], 1)

                def in_order():
                    dve.wait_ge(f_order[late], at(i, F_STEPS[late], f_count[late]))

                rows = acc_f[late]

                def tile(t):
                    return rows[:, t]

                if part == 0:
                    f_count[late] = 0
                    dve.wait_ge(sums_loaded[late], at(i, 32, 32))
                    if late:
                        for j in range(2):
                            dve.wait_ge(sout_psum, at((i[0], i[1] + EARLY), 2, j + 1))
                            did(v.tensor_tensor(rows[:, 2 * j:2 * j + 2], rows[:, 2 * j:2 * j + 2],
                                                bank[4 + 2 * s + j][:].rearrange("p (t d) -> p t d", d=D), ALU.add))
                        in_order()
                        dve.sem_inc(sout_free, 1)
                    means(did, in_order, tile, stats_p, mv_p, vare_p)
                else:
                    rsqrt(did, in_order, vare_p, rstd_p, newton_p)
                    for t in range(T):
                        did(v.tensor_scalar(rows[:, t], rows[:, t], mv_p[:, t, 0:1], rstd_p[:, t:t + 1], ALU.subtract,
                                            ALU.mult))
                    in_order()
                    dve.wait_ge(out_free[late], at(i, 1, 1))
                    v.tensor_tensor(out_f[late], x3_f[late], rows, ALU.add).then_inc(f_made[late], 1)
                    assert f_count[late] == F_STEPS[late], f_count

            def gates_and_sums(n, s):
                before = (n[0], n[1] - 1)
                for f in range(FC):
                    gate((n[0], n[1] + EARLY), f)
                    if before != (None, -1) and f in (2, 3):
                        finish(before, 1, f - 2, 1 - s)
                for part in range(2):
                    finish(n, 0, part)

            dve.sem_inc(sout_free, 2)
            gates_and_sums((None, 0), 0)
            with dve.Fori(0, LATE // 2 - 1) as j:
                gates_and_sums((2 * j, 1), 1)
                gates_and_sums((2 * j, 2), 0)
            gates_and_sums((None, LATE - 1), 1)
            for part in range(2):
                finish((None, LATE - 1), 1, part, 1)

        @block.tensor
        def _(pe):
            mm = nc.tensor.matmul

            def enter(i):
                pe.wait_ge(x_normed, at(i, T, T))
                for c in range(C):
                    for t in range(T):
                        ins = nc.tensor.transpose(bank[4 + c][:, t * P:(t + 1) * P], xa[:, t, c * P:(c + 1) * P],
                                                  ident[:])
                    ins.then_inc(x_transposed, 1)
                pe.wait_ge(xT_ready, at(i, C, C))
                queries(i, 0)
                values(i, 0)
                keys(i, 0)
                for u in range(1, V_FIRST):
                    values(i, u)

            def values(i, u):
                if u >= 2:
                    pe.wait_ge(v_ready, at(i, 2 * T, u - 1))
                if u == V_FIRST:
                    pe.wait_ge(biased, at(i, H * T, 2 * T))
                for c in range(C):
                    ins = mm(bank[V_BANKS[u % 2]][:], xT[:, c, (u // 2) * P:(u // 2 + 1) * P],
                             wv_s[:, c, (u % 2) * 512:(u % 2 + 1) * 512], start=(c == 0), stop=(c == C - 1))
                ins.then_inc(v_psum, 1)

            def first_scores(i):
                pair_scores(i, 0)
                for u in range(V_FIRST, 2 * T):
                    values(i, u)

            def queries(i, hp):
                if hp:
                    pe.wait_ge(k_ready, at(i, 2 * HP, 2 * hp))
                for c in range(C):
                    ins = mm(bank[2][:], wq_s[:, c, hp * P:(hp + 1) * P], xT[:, c], start=(c == 0), stop=(c == C - 1))
                ins.then_inc(q_psum, 1)

            def keys(i, hp):
                pe.wait_ge(q_ready, at(i, HP, hp + 1))
                for c in range(C):
                    ins = mm(bank[2][:], wk_s[:, c, hp * P:(hp + 1) * P], xT[:, c], start=(c == 0), stop=(c == C - 1))
                ins.then_inc(k_psum, 1)

            def head_scores(i, n):
                hp, s = n // 2, n % 2
                for u, unit in enumerate(S_UNITS):
                    if n:
                        pe.wait_ge(biased, at(i, H * T, (n - 1) * T + (1, 3, 4)[u]))
                    if S_BANKS[u] == 3 and s == 0:
                        if hp >= 2:
                            pe.wait_ge(oT_ready, at(i, HP, hp - 1))
                        else:
                            pe.wait_ge(v_ready, at(i, 2 * T, 2 * T if hp else V_FIRST))
                    for t, col in unit:
                        ins = mm(bank[S_BANKS[u]][:, col:col + COLS[t]], qT[:, hp % 2, t * P:(t + 1) * P],
                                 kpad[:, hp % 2, s, 0:COLS[t]], start=True, stop=True, skip_group_check=True)
                    ins.then_inc(scores, 1)

            def pair_scores(i, hp):
                pe.wait_ge(k_ready, at(i, 2 * HP, 2 * hp + 2))
                head_scores(i, 2 * hp)
                if hp + 1 < HP:
                    queries(i, hp + 1)
                head_scores(i, 2 * hp + 1)
                if hp + 1 < HP:
                    keys(i, hp + 1)

            def pair_transposes(i, hp):
                if hp == 0:
                    pe.wait_ge(v_ready, at(i, 2 * T, 2 * T))
                for s in range(2):
                    pe.wait_ge(probs, at(i, H, 2 * hp + s + 1))
                    for u, unit in enumerate(T_UNITS):
                        m = (2 * hp + s) * 3 + u
                        if m >= 3:
                            pe.wait_ge(pT_ready, at(i, 3 * H, m - 2))
                        if T_BANKS[u] == 2 and s == 0:
                            pe.wait_ge(k_ready, at(i, 2 * HP, 2 * min(hp + 3, HP)))
                        for j, col in unit:
                            for t in range(j, T):
                                ins = nc.tensor.transpose(
                                    bank[T_BANKS[u]][:, col + (t - j) * P:col + (t - j + 1) * P],
                                    prob[:, (2 * hp + s) % 4, P_AT[t] + j * P:P_AT[t] + (j + 1) * P], ident[:])
                        ins.then_inc(pT_psum, 1)

            def pair_values(i, hp):
                if hp + 1 < HP:
                    pe.wait_ge(biased, at(i, H * T, 2 * (hp + 2) * T))
                if hp:
                    pe.wait_ge(oT_ready, at(i, HP, hp))
                order = [(u, j) for u, unit in enumerate(T_UNITS) for j, _ in unit]
                for u, j in order:
                    pe.wait_ge(pT_ready, at(i, 3 * H, 6 * hp + 4 + u))
                    for s in range(2):
                        ins = mm(bank[3][s * DH:(s + 1) * DH, j * P:N],
                                 v_s[:, j, (2 * hp + s) * DH:(2 * hp + s + 1) * DH],
                                 pT[:, s, T_AT[j]:T_AT[j] + N - j * P], start=(j == 0), stop=(j == order[-1][1]),
                                 skip_group_check=True)
                ins.then_inc(oT_psum, 1)

            def rows_out(lhs, rhs, chunks, signal, tiles=range(T)):
                for t in tiles:
                    for c in range(chunks):
                        ins = mm(bank[PA + t // 2][:, (t % 2) * D:(t % 2 + 1) * D], lhs[:, c, t * P:(t + 1) * P],
                                 rhs(c), start=(c == 0), stop=(c == chunks - 1), skip_group_check=True)
                    if t % 2:
                        ins.then_inc(signal, 1)

            def leave(tiles):
                rows_out(oT, lambda c: wo_s[:, c], HP, wo_psum, tiles)

            def transposes(p, r, src):
                pe.wait_ge(normed, at(p, ROUNDS * T, (r + 1) * T))
                for c in range(C):
                    for t in range(T):
                        ins = nc.tensor.transpose(bank[PA + c][:, t * P:(t + 1) * P], src[:, t, c * P:(c + 1) * P],
                                                  ident[:])
                    ins.then_inc(transposed, 1)

            def xT_wait(p, r):
                pe.wait_ge(xTp_ready, at(p, C * ROUNDS, (r + 1) * C))

            def post(p, point):
                if point == 0:
                    transposes(p, R_FFN, xn)
                elif point == 1:
                    xT_wait(p, R_FFN)
                    rows_out(xTp, lambda c: weff[:, c], C, rows_psum)
                elif point == 3:
                    transposes(p, R_L1, xn)
                elif point == 4:
                    xT_wait(p, R_L1)
                    for c in range(C):
                        for t in range(T):
                            ins = mm(bank[PA + c][:, 0:D + 2], xn[:, t, c * P:(c + 1) * P], xn[:, t, 0:D + 2],
                                     start=(t == 0), stop=(t == T - 1))
                        ins.then_inc(gram_psum, 1)
                elif point in (5, 6):
                    k = point - 5
                    if k == 0:
                        pe.wait_ge(ssum_ready, at(p, C, C))
                    else:
                        pe.wait_ge(t1_ready, at(p, 3 * KS, 3))
                    for m in range(C):
                        for c in range(C):
                            mm(bank[PA][:, m * D:(m + 1) * D], gram[:, c, m * P:(m + 1) * P], a_v[:, k, c],
                               start=(c == 0), stop=(c == C - 1), skip_group_check=True)
                    for c in range(C):
                        ins = mm(bank[PB][:, 0:D], ssum_b[:, c], a_v[:, k, c], start=(c == 0), stop=(c == C - 1))
                    ins.then_inc(t1_psum, 1)
                elif point == 7:
                    pe.wait_ge(t1_ready, at(p, 3 * KS, 3 * KS))
                    for k in range(KS):
                        for h in range(C):
                            for m in range(C):
                                ins = mm(bank[PA][:, (k * C + h) * P:(k * C + h + 1) * P],
                                         a_k[:, k, m, h * P:(h + 1) * P], t1[:, k, m, h * P:(h + 1) * P],
                                         start=(m == 0), stop=(m == C - 1), skip_group_check=True)
                        ins.then_inc(state_psum, 1)
                elif point == 8:
                    pe.wait_ge(sbd_ready, at(p, 1, 1))
                    for h in range(C):
                        for c in range(C):
                            mm(bank[PA][:, c * D + h * P:c * D + (h + 1) * P], a_qT[:, h, c * P:(c + 1) * P], sbd[:, h],
                               start=True, stop=True, skip_group_check=True)
                        ins = mm(bank[PB][:, h * P:(h + 1) * P], bq_b[:, h], sbd[:, h], start=True, stop=True,
                                 skip_group_check=True)
                    ins.then_inc(mix_psum, 1)
                elif point == 9:
                    pe.wait_ge(mix_ready, at(p, 1, 1))
                    pe.wait_ge(bqs_ready, at(p, 1, 1))
                    rows_out(xTp, lambda c: mix[:, c], C, rows_psum)
                elif point == 10:
                    transposes(p, R_L1O, xn)
                elif point == 11:
                    xT_wait(p, R_L1O)
                    rows_out(xTp, lambda c: l1wo_s[:, c], C, rows_psum)
                elif point == 15:
                    transposes(p, R_MOE, hn)
                elif point == 16:
                    xT_wait(p, R_MOE)
                    for t in range(T):
                        for c in range(C):
                            ins = mm(bank[PB][:, t * NE:(t + 1) * NE], hT[:, c, t * P:(t + 1) * P], wg_s[:, c],
                                     start=(c == 0), stop=(c == C - 1), skip_group_check=True)
                    ins.then_inc(logits_psum, 1)
                elif point == 17:
                    pe.wait_ge(sel_ready, at(p, 1, 1))
                    for t in range(T):
                        dst = bank[PB][:, (T + t) * NE:(T + t + 1) * NE]
                        mm(dst, ones_b[:], cum[:], start=True, stop=False, skip_group_check=True)
                        for s in range(t):
                            mm(dst, ones_b[:], sel_b[:, s], start=False, stop=False, skip_group_check=True)
                        ins = mm(dst, tri[:], sel_b[:, t], start=False, stop=True, skip_group_check=True)
                    ins.then_inc(rank_psum, 1)

            pe.wait_ge(ident_made, 2)
            pe.wait_ge(att_loaded, 16 * 3)
            enter((None, 0))
            first_scores((None, 0))
            for hp in range(HP):
                if hp + 1 < HP:
                    pair_scores((None, 0), hp + 1)
                pair_transposes((None, 0), hp)
                pair_values((None, 0), hp)
            pe.wait_ge(post_loaded, 16 * N_POST)
            pe.wait_ge(oT_ready, HP)
            pe.wait_ge(setup_pe, 2 * C)
            for c in range(C):
                ins = mm(bank[3][:, 0:D], lnb_b[:, c], l1wo_raw[:, c], start=(c == 0), stop=(c == C - 1))
            ins.then_inc(setup_pe, 1)
            leave(range(T))
            pe.wait_ge(ready, 1)
            with pe.Fori(0, B - 1) as b:
                enter((b, 1))
                first_scores((b, 1))
                post((b, 0), 0)
                for hp in range(HP):
                    if hp + 1 < HP:
                        pair_scores((b, 1), hp + 1)
                    if 2 * hp + 1 not in BEHIND:
                        post((b, 0), 2 * hp + 1)
                    pair_transposes((b, 1), hp)
                    if 2 * hp + 1 in BEHIND:
                        post((b, 0), 2 * hp + 1)
                    pair_values((b, 1), hp)
                    post((b, 0), 2 * hp + 2)
                pe.wait_ge(oT_ready, at((b, 1), HP, HP))
                leave(range(T // 2))
                post((b, 0), POINTS - 1)
                pe.wait_ge(ranks_read, b * 2 + 2)
                leave(range(T // 2, T))
            sw1 = sw_s[:, 0:W1C].rearrange("p (c f) -> p c f", c=C)
            sw2 = sw_s[:, W1C:EWC].rearrange("p (f d) -> p f d", f=FC)

            def shared_hidden(i, f, rows):
                if f >= 2:
                    pe.wait_ge(sact_ready, at(i, FC, f - 1))
                for part in (1, 0):
                    for c in range(C):
                        ins = mm(bank[2 * (f % 2) + 1 - part][:],
                                 sw1[:, c, (part * FC + f) * P:(part * FC + f + 1) * P], rows[:, c],
                                 start=(c == 0), stop=(c == C - 1))
                    ins.then_inc(sh_psum, 1)

            def shared_out(i, first_bank):
                pe.wait_ge(sact_ready, at(i, FC, FC))
                for t in range(T):
                    for f in range(FC):
                        ins = mm(bank[first_bank + t // 2][:, (t % 2) * D:(t % 2 + 1) * D],
                                 act_s[:, f, t * P:(t + 1) * P], sw2[:, f], start=(f == 0), stop=(f == FC - 1),
                                 skip_group_check=True)
                    if t % 2:
                        ins.then_inc(sout_psum, 1)

            pe.wait_ge(sw_loaded, 16)
            for point in range(POINTS):
                if point:
                    post((None, B - 1), point)
                for i, f in UNITS[point]:
                    if f == 0:
                        pe.wait_ge(early_loaded[i], 16)
                    if f < FC:
                        shared_hidden((None, i), f, hT_early[i])
                    else:
                        if i:
                            pe.wait_ge(early_ready, 2 * i)
                        shared_out((None, i), 4)
                if point == 0:
                    post((None, B - 1), point)

            def rows_in(e, s, j):
                pe.wait_ge(xb_loaded[s], j * 32 + 32)
                for c in range(C):
                    nc.tensor.transpose(bank[6][:, c * CAP:c * CAP + P], xb[:, s, c * P:(c + 1) * P], ident[:])
                    i = nc.tensor.transpose(bank[6][:, c * CAP + P:(c + 1) * CAP], xb2[:, s, c * P:(c + 1) * P],
                                            ident[0:CAPR, 0:CAPR])
                i.then_inc(xb_psum, 1)

            def rows_back(e):
                pe.wait_ge(eo_ready, at(e, 2, 2))
                for c in range(C):
                    nc.tensor.transpose(bank[5][:, c * P:(c + 1) * P], eo[:, c, 0:P], ident[:])
                    i = nc.tensor.transpose(bank[5][0:CAPR, D + c * P:D + (c + 1) * P], eo[:, c, P:CAP], ident[:])
                i.then_inc(ebo_psum, 1)

            def expert(e, s, j, first=False, last=False):
                w1 = ew_s[:, s, 0:W1C].rearrange("p (c f) -> p c f", c=C)
                w2 = ew_s[:, s, W1C:EWC].rearrange("p (f d) -> p f d", f=FC)
                pe.wait_ge(w1_loaded[s], j * 16 + 16)
                pe.wait_ge(xbT_ready, at(e, 1, 1))
                for half in range(2):
                    for part in (1, 0):
                        for q in range(3):
                            f = part * FC + 3 * half + q
                            for c in range(C):
                                i = mm(bank[2 * half + 1 - part][:, q * CAP:(q + 1) * CAP], w1[:, c, f * P:(f + 1) * P],
                                       xbT[:, c], start=(c == 0), stop=(c == C - 1), skip_group_check=True)
                        i.then_inc(h_psum, 1)
                    if half == 0 and not first:
                        rows_back((e[0], e[1] - 1))
                if not last:
                    rows_in((e[0], e[1] + 1), 1 - s, j + s)
                pe.wait_ge(w2_loaded[s], j * 16 + 16)
                for half in range(2):
                    pe.wait_ge(act_ready, at(e, 2, half + 1))
                    for c in range(C):
                        for f in range(3 * half, 3 * half + 3):
                            i = mm(bank[(4, 7)[c]][:, 0:CAP],
                                   w2[:, f, c * P:(c + 1) * P], act_e[:, f], start=(f == 0), stop=(f == FC - 1),
                                   skip_group_check=True)
                i.then_inc(eo_psum, 1)

            rows_in((None, 0), 0, 0)
            expert((None, 0), 0, 0, first=True)
            with pe.Fori(0, NE // 2 - 1) as j:
                expert((2 * j, 1), 1, j)
                expert((2 * j, 2), 0, j + 1)
            expert((None, NE - 1), 1, NE // 2 - 1, last=True)
            rows_back((None, NE - 1))

            with pe.Fori(0, LATE // 2) as j:
                for s in range(2):
                    i = (2 * j, s + EARLY)
                    pe.wait_ge(late_loaded[s], j * 16 + 16)
                    for f in range(FC):
                        shared_hidden(i, f, hT_late[s])
                    pe.wait_ge(sout_free, at((2 * j, s), 1, 1))
                    shared_out(i, 4 + 2 * s)


_NAMES = ["x", "wq", "wk", "wv", "wo", "bo", "ffn_w", "ffn_d", "l1_wq", "l1_wqT", "l1_bq", "l1_wk", "l1_bk", "l1_wv",
          "l1_bv", "l1_wo", "l1_bo", "ln_g", "ln_b", "wgT", "sw", "ew"]


def _gated_weights(np, w1, w2):
    lead = w1.shape[:-2]
    a = np.swapaxes(w1, -1, -2).reshape(*lead, C, P, 2 * FFN)
    b = np.swapaxes(w2, -1, -2).reshape(*lead, FC, P, D)
    a = np.swapaxes(a, -3, -2).reshape(*lead, P, W1C)
    b = np.swapaxes(b, -3, -2).reshape(*lead, P, FC * D)
    return np.concatenate([a, b], axis=-1)


def kernel(**inputs):
    import numpy as np
    import concourse.bacc as bacc
    from concourse.bass_utils import run_bass_kernel_spmd

    i = {k: np.asarray(v) for k, v in inputs.items()}
    laid = [i["L0_attn_x"], i["L0_attn_Wq"], i["L0_attn_Wk"], i["L0_attn_Wv"], i["L0_attn_Wo"], i["L0_attn_bo"],
            i["L0_ffn_weight"].T, i["L0_ffn_disha"], i["L1_attn_Wq"], i["L1_attn_Wq"].T, i["L1_attn_bq"],
            i["L1_attn_Wk"], i["L1_attn_bk"], i["L1_attn_Wv"], i["L1_attn_bv"], i["L1_attn_Wo"], i["L1_attn_bo"],
            i["L1_attn_ln_g"], i["L1_attn_ln_b"], i["L1_ffn_wg"].T,
            _gated_weights(np, i["L1_ffn_shared_w1"], i["L1_ffn_shared_w2"]),
            _gated_weights(np, i["L1_ffn_expert_w1"], i["L1_ffn_expert_w2"])]
    nc = bacc.Bacc("TRN2", target_bir_lowering=False, num_devices=1)
    arrays, args = {}, []
    for name, a in zip(_NAMES, laid):
        arrays[name] = np.ascontiguousarray(a)
        args.append(nc.dram_tensor(name, a.shape, mybir.dt.from_np(a.dtype), kind="ExternalInput").ap())
    out = nc.dram_tensor("out", [B, N, D], F32, kind="ExternalOutput").ap()
    bass_sandwich(nc, *args, out)
    r = run_bass_kernel_spmd(nc, [arrays], core_ids=[0])
    return r.results[0]["out"]
```
